# Optimizing a Trainium2 kernel written in Bass

```python
import numpy as np
import jax
import jax.numpy as jnp

def _softmax(x, axis=-1):
    return jax.nn.softmax(x, axis=axis)

def _gelu(x):
    return jax.nn.gelu(x, approximate=True)

def _silu(x):
    return jax.nn.silu(x)

def _sigmoid(x):
    return jax.nn.sigmoid(x)

def _layernorm(x, axis=-1, eps=1e-05):
    m = jnp.mean(x, axis=axis, keepdims=True)
    v = jnp.var(x, axis=axis, keepdims=True)
    return (x - m) / jnp.sqrt(v + eps)

def _scatter_add(tgt, idx, src, axis=0):
    return tgt.at[idx].add(src)

def _segment_sum(src, seg, n):
    return jax.ops.segment_sum(src, seg, n)
kernel_name = 'mk_flamingo_gated_d1_seqx_r8_65349a'

def setup_inputs(seed: int=0):
    np.random.seed(seed)
    _w = jnp.asarray

    def _rec_inputs():
        import jax
        import jax.numpy as jnp
        _rk = jax.random.key(seed)
        x = 7.22e-05 + 1 * jax.random.normal(jax.random.fold_in(_rk, 1), (32, 128, 128), jnp.float32)
        _lenS = 128 - jax.random.randint(jax.random.fold_in(_rk, 7), (32,), 0, max(1, 128 // 4) + 1, jnp.int32)
        _lenS2 = 128 - jax.random.randint(jax.random.fold_in(_rk, 8), (32,), 0, max(1, 128 // 4) + 1, jnp.int32)
        _ctx_1024P = jax.random.normal(jax.random.fold_in(_rk, 11), (32, 16, 128), jnp.float32)
        _ctx_1024c = jax.random.dirichlet(jax.random.fold_in(_rk, 511), 0.3 * jnp.ones((16,), jnp.float32), (32, 128))
        _ctx_1024t = jnp.einsum('bsk,bkd->bsd', _ctx_1024c, _ctx_1024P)
        _ctx_1024t = _ctx_1024t * jax.lax.rsqrt(jnp.mean(jnp.square(_ctx_1024t)) + 1e-12) * 0.953939
        ctx_1024 = 4.13588e-05 + 0.999923 * (_ctx_1024t + 0.3 * jax.random.normal(jax.random.fold_in(_rk, 611), (32, 128, 128), jnp.float32))
        _validS = jnp.arange(128)[None, :] < _lenS[:, None]
        _validS2 = jnp.arange(128)[None, :] < _lenS2[:, None]
        _causal = jnp.tril(jnp.ones((128, 128), dtype=bool))
        mask_BxS2_ff0 = jnp.where(jnp.ones((32, 128), dtype=bool), 0.0, -1000000000.0).astype(jnp.float32)
        _g = jax.random.normal(jax.random.fold_in(_rk, 9001), (2, 1), jnp.float32)
        _g = jnp.sign(_g) * jnp.maximum(jnp.abs(_g), 1.0) + (_g == 0) * 1.0
        g_xattn = _g[0]
        g_ffn = _g[1]
        return (x, ctx_1024, mask_BxS2_ff0, g_xattn, g_ffn)
    x, ctx_1024, mask_BxS2_ff0, g_xattn, g_ffn = _rec_inputs()

    def _L0_xattn_setup():
        import jax, jax.numpy as jnp
        import numpy as np
        B, S, D, H = (4, 256, 128, 16)
        DK = D // H
        WINDOW = 32
        GLOBAL = 16
        NEG_INF = float(np.finfo(np.float32).min)

        def local_window_mask(seq_len, window, global_tokens):
            i = jnp.arange(seq_len)[:, None]
            j = jnp.arange(seq_len)[None, :]
            is_global = (i < global_tokens) | (j < global_tokens)
            out_of_window = jnp.abs(i - j) > window
            return jnp.where(out_of_window & ~is_global, NEG_INF, 0.0).astype(jnp.float32)
        key = jax.random.key(seed)
        ks = jax.random.split(key, 8)
        std = 1.0 / np.sqrt(D)
        return {'q': jax.random.normal(ks[0], (B, S, D), jnp.float32), 'k': jax.random.normal(ks[1], (B, S, D), jnp.float32), 'v': jax.random.normal(ks[2], (B, S, D), jnp.float32), 'attn_mask': jnp.zeros((B, S), jnp.float32), 'wq': jax.random.normal(ks[3], (D, D), jnp.float32) * std, 'bq': jnp.zeros((D,), jnp.float32), 'wk': jax.random.normal(ks[4], (D, D), jnp.float32) * std, 'bk': jnp.zeros((D,), jnp.float32), 'wv': jax.random.normal(ks[5], (D, D), jnp.float32) * std, 'bv': jnp.zeros((D,), jnp.float32), 'wo': jax.random.normal(ks[6], (D, D), jnp.float32) * std, 'bo': jnp.zeros((D,), jnp.float32)}
    _L0_xattn_all = _L0_xattn_setup()
    _L0_xattn_in = {k: v for k, v in _L0_xattn_all.items() if k in ('wq', 'bq', 'wk', 'bk', 'wv', 'bv', 'wo', 'bo')}
    del _L0_xattn_all

    def _L0_ffn_setup():
        import jax, jax.numpy as jnp
        import numpy as np
        TOP_K = 2
        key = jax.random.key(seed)
        ks = jax.random.split(key, 5)
        B, T, D, F, E = (4, 256, 128, 512, 8)
        s = 0.02
        return {'x': jax.random.normal(ks[0], (B, T, D), jnp.float32), 'gate_w': jax.random.normal(ks[1], (D, E), jnp.float32) * s, 'w1': jax.random.normal(ks[2], (E, D, F), jnp.float32) * s, 'w3': jax.random.normal(ks[3], (E, D, F), jnp.float32) * s, 'w2': jax.random.normal(ks[4], (E, F, D), jnp.float32) * s}
    _L0_ffn_all = _L0_ffn_setup()
    _L0_ffn_in = {k: v for k, v in _L0_ffn_all.items() if k in ('gate_w', 'w1', 'w3', 'w2')}
    del _L0_ffn_all
    return {'x': x, 'ctx_1024': ctx_1024, 'mask_BxS2_ff0': mask_BxS2_ff0, 'g_xattn': g_xattn, 'g_ffn': g_ffn, 'L0_xattn_wq': _L0_xattn_in['wq'], 'L0_xattn_bq': _L0_xattn_in['bq'], 'L0_xattn_wk': _L0_xattn_in['wk'], 'L0_xattn_bk': _L0_xattn_in['bk'], 'L0_xattn_wv': _L0_xattn_in['wv'], 'L0_xattn_bv': _L0_xattn_in['bv'], 'L0_xattn_wo': _L0_xattn_in['wo'], 'L0_xattn_bo': _L0_xattn_in['bo'], 'L0_ffn_gate_w': _L0_ffn_in['gate_w'], 'L0_ffn_w1': _L0_ffn_in['w1'], 'L0_ffn_w3': _L0_ffn_in['w3'], 'L0_ffn_w2': _L0_ffn_in['w2']}

def reference(x, ctx_1024, mask_BxS2_ff0, g_xattn, g_ffn, L0_xattn_wq, L0_xattn_bq, L0_xattn_wk, L0_xattn_bk, L0_xattn_wv, L0_xattn_bv, L0_xattn_wo, L0_xattn_bo, L0_ffn_gate_w, L0_ffn_w1, L0_ffn_w3, L0_ffn_w2):
    import jax
    import jax.numpy as jnp

    def _L0_xattn_ref(q, k, v, attn_mask, wq, bq, wk, bk, wv, bv, wo, bo):
        import jax, jax.numpy as jnp
        import numpy as np
        B, S, D, H = (4, 256, 128, 16)
        DK = D // H
        WINDOW = 32
        GLOBAL = 16
        NEG_INF = float(np.finfo(np.float32).min)

        def local_window_mask(seq_len, window, global_tokens):
            i = jnp.arange(seq_len)[:, None]
            j = jnp.arange(seq_len)[None, :]
            is_global = (i < global_tokens) | (j < global_tokens)
            out_of_window = jnp.abs(i - j) > window
            return jnp.where(out_of_window & ~is_global, NEG_INF, 0.0).astype(jnp.float32)
        b, s, d = q.shape
        Q = (q @ wq + bq).reshape(b, s, H, DK).transpose(0, 2, 1, 3)
        K = (k @ wk + bk).reshape(b, s, H, DK).transpose(0, 2, 1, 3)
        V = (v @ wv + bv).reshape(b, s, H, DK).transpose(0, 2, 1, 3)
        scale = 1.0 / np.sqrt(DK)
        scores = jnp.einsum('bhqd,bhkd->bhqk', Q, K) * scale
        scores = scores + attn_mask[:, None, None, :]
        scores = scores + local_window_mask(s, WINDOW, GLOBAL)[None, None, :, :]
        probs = jax.nn.softmax(scores, axis=-1)
        out = jnp.einsum('bhqk,bhkd->bhqd', probs, V)
        out = out.transpose(0, 2, 1, 3).reshape(b, s, d)
        return out @ wo + bo

    def _L0_ffn_ref(x, gate_w, w1, w3, w2):
        import jax, jax.numpy as jnp
        import numpy as np
        TOP_K = 2
        logits = jnp.einsum('btd,de->bte', x, gate_w)
        probs = jax.nn.softmax(logits, axis=-1)
        expert_weights, expert_indices = jax.lax.top_k(probs, TOP_K)
        expert_weights = expert_weights / expert_weights.sum(-1, keepdims=True)
        E = w1.shape[0]
        out = jnp.zeros_like(x)
        for i in range(E):
            wi = jnp.where(expert_indices == i, expert_weights, 0.0).sum(-1)
            h = jax.nn.silu(jnp.einsum('btd,df->btf', x, w1[i])) * jnp.einsum('btd,df->btf', x, w3[i])
            out = out + jnp.einsum('btf,fd->btd', h, w2[i]) * wi[..., None]
        return out
    x = x + jnp.tanh(g_xattn[0]) * _L0_xattn_ref(_layernorm(x, axis=-1), ctx_1024, ctx_1024, mask_BxS2_ff0, L0_xattn_wq, L0_xattn_bq, L0_xattn_wk, L0_xattn_bk, L0_xattn_wv, L0_xattn_bv, L0_xattn_wo, L0_xattn_bo)
    x = x + jnp.tanh(g_ffn[0]) * _L0_ffn_ref(_layernorm(x, axis=-1), L0_ffn_gate_w, L0_ffn_w1, L0_ffn_w3, L0_ffn_w2)
    return x

_drawn_inputs = setup_inputs


def setup_inputs(seed=0):
    import zlib

    import numpy as np

    out = dict(_drawn_inputs(seed))
    spreads = {'L0_xattn_bq': (0.0, 0.42),
     'L0_xattn_bk': (0.0, 0.8),
     'L0_xattn_bv': (0.0, 0.1),
     'L0_xattn_bo': (0.0, 0.1)}
    factors = {'L0_ffn_gate_w': 8.0, 'L0_ffn_w1': 7.887, 'L0_ffn_w3': 7.858, 'L0_ffn_w2': 7.857}
    for name, (base, spread) in spreads.items():
        noise = np.random.default_rng([zlib.crc32(name.encode()), seed]).standard_normal(out[name].shape)
        drawn = base * np.exp(spread * noise) if base else spread * noise
        out[name] = jnp.asarray(drawn.astype(out[name].dtype))
    for name, factor in factors.items():
        out[name] = (out[name] * factor).astype(out[name].dtype)
    return out
```

```python
from contextlib import ExitStack

import numpy as np

import concourse.bass as bass
from concourse import mybir

P = 128
F32 = mybir.dt.float32
BF16 = mybir.dt.bfloat16
I32 = mybir.dt.int32
U32 = mybir.dt.uint32
ALU = mybir.AluOpType
ACT = mybir.ActivationFunctionType
AX = mybir.AxisListType

H = 16
WINDOW, GLOBAL = 32, 16
MASKED = -1e38
EPS = 1e-5
PARTS = 3
Q_PART = [0, 0, 0, 1, 1, 2]
K_PART = [0, 1, 2, 0, 1, 0]


def build(nc, x, ctx_in, mask_in, g_xattn, g_ffn, wq, bq, wk, bk, wv, bv, wo, bo, gate_w, w1, w3, w2, out):
    B, S, D = x.shape
    E, _, F = w1.shape
    assert S == P and D == P
    DK = D // H
    T = B * S
    GB = 4
    NG = B // GB
    GT = GB * S
    FC = F // P
    SCALE = float(1.0 / np.sqrt(DK))
    ROWS_P = len(Q_PART) * DK
    ROWS_M = ROWS_P + PARTS
    ROWS_X = ROWS_M + PARTS
    HB = GB
    NB = H // HB
    VW = DK + 1
    NT = 2 * T // P + E
    CAP = T + P
    XW = D + 2
    X_IDX, X_GATE = D, D + 1
    RING = 6

    qk_d = nc.dram_tensor("qk_parts_scratch", (PARTS, 2, D, T), BF16, kind="Internal").ap()
    mask_d = nc.dram_tensor("mask_parts_scratch", (PARTS, T), BF16, kind="Internal").ap()
    rows_d = nc.dram_tensor("expert_rows_scratch", (E * CAP + E * P, XW), F32, kind="Internal").ap()
    acc_d = nc.dram_tensor("result_scratch", (T + P, D), F32, kind="Internal").ap()

    with ExitStack() as stack:
        def sb(name, shape, dt=F32):
            return stack.enter_context(nc.sbuf_tensor(name, shape, dt))

        def sem(name):
            return stack.enter_context(nc.semaphore(name))

        ps1 = stack.enter_context(nc.psum_tensor("ps_max_scores", [P, 2, 512], F32))
        ps2 = stack.enter_context(nc.psum_tensor("ps_scores", [P, NB, 512], F32))
        psm = stack.enter_context(nc.psum_tensor("ps_values", [P, 512], F32))
        psy = stack.enter_context(nc.psum_tensor("ps_out", [P, 512], F32))

        ident = sb("ident", [P, P])
        ident_b = sb("ident_b", [P, P], BF16)
        wmask = sb("wmask", [P, HB, P], BF16)
        tri = sb("tri", [P, P], BF16)
        ones_b = sb("ones_b", [P, P], BF16)
        iota_e = sb("iota_e", [P, E])
        cap_e = sb("cap_e", [P, E])
        iota_t = sb("iota_t", [P, NT])
        ones_s = sb("ones_s", [P, E])
        minus_half = sb("minus_half", [P, GB])
        fill = sb("fill", [P, XW])
        xs = sb("xs", [P, B, D])
        w_sb = {n: sb(f"w_{n}", [P, D]) for n in ("q", "k", "v", "o")}
        gate_sb = sb("gate_sb", [P, E])
        bq_col = sb("bq_col", [P, 1])
        bqs_col = sb("bqs_col", [P, 1])
        bk_col = sb("bk_col", [P, 1])
        bv_row = sb("bv_row", [P, D])
        bo_row = sb("bo_row", [P, D])
        gates = sb("gates", [P, 2])
        tg = sb("tg", [P, 2])
        mrow = sb("mrow", [B, S])
        mres = sb("mres", [B, S])
        mpart = sb("mpart", [B, PARTS, S], BF16)
        w1_sb = sb("w1_sb", [P, E, F])
        w3_sb = sb("w3_sb", [P, E, F])
        w2_sb = sb("w2_sb", [P, E, FC, D])
        va = sb("va", [P, B, H, VW])
        qs = [sb(f"qs{u}", [P, H, GT], BF16) for u in range(2)]
        ks = [sb(f"ks{u}", [P, H, GT], BF16) for u in range(2)]
        pT = sb("pT", [P, H, S])
        npart = sb("npart", [P, P // H, H], BF16)
        oh_sum = sb("oh_sum", [P, E], BF16)
        idx_f = sb("idx_f", [P, GB])

        early = ExitStack()

        def sb_early(name, shape, dt=F32):
            return early.enter_context(nc.sbuf_tensor(name, shape, dt))

        stats = sb_early("stats", [P, B, 6])
        mv = sb_early("mv", [P, B, 2])
        rstd = sb_early("rstd", [P, B])
        cg = sb_early("cg", [P, 2, GB, D])
        xn = sb_early("xn", [P, 2, GB, D])
        xnT = sb_early("xnT", [P, 2, GT])
        ctxT = sb_early("ctxT", [P, 2, GT])
        qkf = sb_early("qkf", [P, 2, 2, GT])
        parts = sb_early("parts", [P, 2, PARTS, 2, GT], BF16)

        XCH = 4
        x_loaded = [sem(f"x_loaded{i}") for i in range(XCH)]
        small_loaded = sem("small_loaded")
        w_loaded = sem("w_loaded")
        ctx_loaded = [sem(f"ctx_loaded{u}") for u in range(2)]
        ident_ready = sem("ident_ready")
        pool_step = sem("pool_step")
        ones_ready = sem("ones_ready")
        dve_step = sem("dve_step")
        var_ready = sem("var_ready")
        std_ready = sem("std_ready")
        gates_ready = sem("gates_ready")
        xn_written = sem("xn_written")
        xn_turned = sem("xn_turned")
        ctx_turned = sem("ctx_turned")
        turned_copied = sem("turned_copied")
        qk_done = sem("qk_done")
        qk_copied = sem("qk_copied")
        v_done = sem("v_done")
        v_copied = sem("v_copied")
        split1 = sem("split1")
        parts_ready = sem("parts_ready")
        parts_stored = [sem(f"parts_stored{u}") for u in range(2)]
        mpart_ready = sem("mpart_ready")
        mpart_stored = sem("mpart_stored")
        fill_ready = sem("fill_ready")
        fill_stored = sem("fill_stored")
        res_ready = sem("res_ready")
        var_stats = sem("var_stats")
        SMALL = 4 + 8
        STEADY = (NG - 2) // 2

        with nc.Block() as block:
            @block.sync
            def _(sp):
                x_v = x.rearrange("b s d -> s b d")
                for i in range(XCH):
                    n = B // XCH
                    sp.dma_start(xs[:, i * n:(i + 1) * n], x_v[:, i * n:(i + 1) * n]).then_inc(x_loaded[i], 16)
                ctx_v = ctx_in.rearrange("b s d -> s b d")
                for u in range(2):
                    sp.dma_start(cg[:, u], ctx_v[:, u * GB:(u + 1) * GB]).then_inc(ctx_loaded[u], 16)

                def store_parts(g, u):
                    sp.wait_ge(parts_ready, g + 1)
                    sp.dma_start(qk_d.rearrange("a s p t -> p (a s) t")[:, :, bass.ds(g * GT, GT)],
                                 parts[:, u].rearrange("p a s t -> p (a s) t")).then_inc(parts_stored[u], 16)

                with sp.Fori(0, STEADY) as it:
                    for u in range(2):
                        g = it * 2 + u
                        sp.wait_ge(ctx_turned, g + 1)
                        sp.dma_start(cg[:, u], ctx_v[:, bass.ds((g + 2) * GB, GB)]).then_inc(ctx_loaded[u], 16)
                        store_parts(g, u)
                for u in range(2):
                    store_parts(NG - 2 + u, u)
                sp.wait_ge(fill_ready, 1)
                for e in range(E):
                    sp.dma_start(rows_d[E * CAP + e * P:E * CAP + (e + 1) * P], fill[:]).then_inc(fill_stored, 16)
                sp.dma_start(acc_d[T:T + P], fill[:, 0:D]).then_inc(fill_stored, 16)
                sp.dma_start(w1_sb[:], w1.rearrange("e d f -> d e f")).then_inc(w_loaded, 16)
                sp.dma_start(w3_sb[:], w3.rearrange("e d f -> d e f")).then_inc(w_loaded, 16)
                sp.dma_start(w2_sb[:], w2.rearrange("e (c f) d -> f e c d", f=P)).then_inc(w_loaded, 16)
                sp.wait_ge(fill_stored, 16 * (E + 1))
                for u in range(2):
                    sp.wait_ge(parts_stored[u], 16 * (NG // 2))

            @block.gpsimd
            def _(pool):
                pool.memset(ident[:], 0.0).then_inc(pool_step, 1)
                pool.memset(ident_b[:], 0.0).then_inc(pool_step, 1)
                pool.wait_ge(pool_step, 2)
                for m in (ident, ident_b):
                    pool.affine_select(out=m[:], in_=m[:], compare_op=ALU.not_equal, fill=1.0, base=0,
                                       pattern=[[-1, P]], channel_multiplier=1).then_inc(ident_ready, 1)
                pool.memset(va[:], 1.0).then_inc(ones_ready, 1)
                pool.memset(wmask[:], 0.0).then_inc(pool_step, 1)
                pool.memset(tri[:], 1.0).then_inc(pool_step, 1)
                pool.memset(ones_b[:], 1.0)
                pool.memset(ones_s[:], 1.0)
                pool.memset(minus_half[:], -0.5)
                pool.memset(npart[:], 0.0)
                pool.memset(oh_sum[:], 0.0)
                pool.memset(fill[:], 0.0).then_inc(pool_step, 1)
                pool.wait_ge(pool_step, 5)
                pool.iota(fill[:].bitcast(U32)[:, X_IDX:X_IDX + 1], [[0, 1]], base=T, channel_multiplier=1)\
                    .then_inc(fill_ready, 1)
                pool.affine_select(out=tri[:], in_=tri[:], compare_op=ALU.is_gt, fill=0.0, base=0,
                                   pattern=[[1, P]], channel_multiplier=-1)
                pool.affine_select(out=wmask[:], in_=wmask[:], compare_op=ALU.is_ge, fill=MASKED, base=WINDOW,
                                   pattern=[[0, HB], [1, P]], channel_multiplier=-1).then_inc(pool_step, 1)
                pool.wait_ge(pool_step, 6)
                pool.affine_select(out=wmask[:], in_=wmask[:], compare_op=ALU.is_ge, fill=MASKED, base=WINDOW,
                                   pattern=[[0, HB], [-1, P]], channel_multiplier=1).then_inc(pool_step, 1)
                pool.wait_ge(pool_step, 7)
                pool.affine_select(out=wmask[:], in_=wmask[:], compare_op=ALU.is_ge, fill=0.0, base=-GLOBAL,
                                   pattern=[[0, HB], [0, P]], channel_multiplier=1).then_inc(pool_step, 1)
                pool.wait_ge(pool_step, 8)
                pool.affine_select(out=wmask[:], in_=wmask[:], compare_op=ALU.is_ge, fill=0.0, base=-GLOBAL,
                                   pattern=[[0, HB], [1, P]], channel_multiplier=0)
                for t, pattern, base, mult in ((iota_e, [[1, E]], -E, 0), (cap_e, [[CAP, E]], 0, 0),
                                               (iota_t, [[1, NT]], 0, 0), (idx_f, [[S, GB]], 0, 1)):
                    pool.iota(t[:], pattern, base=base, channel_multiplier=mult, allow_small_or_imprecise_dtypes=True)
                pool.wait_ge(ones_ready, 1)
                pool.wait_ge(fill_ready, 1)
                pool.drain()
                for t in (*qs, *ks):
                    pool.memset(t[32:64], 1.0).then_inc(ones_ready, 1)
                pool.wait_ge(ones_ready, 5)
                pool.wait_ge(gates_ready, 1)
                pool.wait_ge(small_loaded, 16 * SMALL)
                pool.tensor_scalar(bo_row[:], bo_row[:], tg[:, 0:1], 0.0, ALU.mult, ALU.add).then_inc(pool_step, 1)
                pool.wait_ge(pool_step, 9)
                pool.wait_ge(xn_written, NG * GB)
                pool.tensor_tensor(xs[:], xs[:], bo_row[:].unsqueeze(1).to_broadcast([P, B, D]),
                                   ALU.add).then_inc(res_ready, 1)
                pool.wait_ge(res_ready, 1)

            @block.scalar
            def _(act):
                act.dma_start(gates[:, 0:1], g_xattn.partition_broadcast(P)).then_inc(small_loaded, 16)
                act.dma_start(gates[:, 1:2], g_ffn.partition_broadcast(P)).then_inc(small_loaded, 16)
                act.dma_start(mrow[:], mask_in).then_inc(small_loaded, 16)
                act.dma_start(bq_col[:], bq.rearrange("(p a) -> p a", a=1)).then_inc(small_loaded, 16)
                act.dma_start(bk_col[:], bk.rearrange("(p a) -> p a", a=1)).then_inc(small_loaded, 16)
                act.dma_start(bv_row[:], bv.partition_broadcast(P)).then_inc(small_loaded, 16)
                act.dma_start(bo_row[:], bo.partition_broadcast(P)).then_inc(small_loaded, 16)
                act.dma_start(gate_sb[:], gate_w).then_inc(small_loaded, 16)
                for n, src in (("q", wq), ("k", wk), ("v", wv), ("o", wo)):
                    act.dma_start(w_sb[n][:], src).then_inc(small_loaded, 16)
                act.wait_ge(small_loaded, 16 * SMALL)
                nc.scalar.activation(tg[:], gates[:], ACT.Tanh).then_inc(gates_ready, 1)
                nc.scalar.mul(bqs_col[:], bq_col[:], SCALE).then_inc(gates_ready, 1)
                act.wait_ge(mpart_ready, 1)
                act.dma_start(mask_d.rearrange("a (b s) -> b a s", s=S), mpart[:]).then_inc(mpart_stored, 16)
                act.wait_ge(var_ready, 1)
                nc.scalar.activation(rstd[:], mv[:, :, 1], ACT.Sqrt).then_inc(std_ready, 1)

                def copy_turned(g, u):
                    act.wait_ge(xn_turned, g + 1)
                    nc.scalar.copy(xnT[:, u], ps2[:, 0]).then_inc(turned_copied, 1)
                    act.wait_ge(ctx_turned, g + 1)
                    nc.scalar.copy(ctxT[:, u], ps2[:, 1]).then_inc(turned_copied, 1)

                def bias(g, u, half):
                    act.wait_ge(qk_done, g + 1)
                    if not (isinstance(half, int) and half == 0):
                        act.wait_ge(parts_stored[u], half * 16)
                    for s, (b, scale) in enumerate(((bqs_col, SCALE), (bk_col, 1.0))):
                        nc.scalar.activation(qkf[:, u, s], ps2[:, 2 + s], ACT.Identity, bias=b[:, 0:1], scale=scale)
                        ins = nc.scalar.activation(parts[:, u, 0, s], ps2[:, 2 + s], ACT.Identity,
                                                   bias=b[:, 0:1], scale=scale)
                    ins.then_inc(qk_copied, 1)

                act.wait_ge(gates_ready, 2)
                copy_turned(0, 0)
                copy_turned(1, 1)
                bias(0, 0, 0)
                copy_turned(2, 0)
                bias(1, 1, 0)
                with act.Fori(1, STEADY) as it:
                    for u in range(2):
                        g = it * 2 + u
                        copy_turned(g + 1, 1 - u)
                        bias(g, u, it)
                copy_turned(NG - 1, 1)
                bias(NG - 2, 0, NG // 2 - 1)
                bias(NG - 1, 1, NG // 2 - 1)
                act.wait_ge(mpart_stored, 16)

            @block.vector
            def _(dve):
                steps = [0]

                def then_wait(ins):
                    steps[0] += 1
                    ins.then_inc(dve_step, 1)
                    dve.wait_ge(dve_step, steps[0])

                for i in range(XCH):
                    dve.wait_ge(x_loaded[i], 16)
                    with dve.Fori(i * (B // XCH), (i + 1) * (B // XCH)) as b:
                        nc.vector.bn_stats(stats[:, b], xs[:, b]).then_inc(var_stats, 1)
                dve.wait_ge(var_stats, B)
                for b in range(B):
                    nc.vector.bn_aggr(mv[:, b], stats[:, b]).then_inc(var_stats, 1)
                dve.wait_ge(var_stats, 2 * B)
                nc.vector.tensor_scalar(mv[:, :, 1], mv[:, :, 1], EPS, None, ALU.add).then_inc(var_ready, 1)
                dve.wait_ge(small_loaded, 16 * SMALL)
                then_wait(nc.vector.tensor_copy(mpart[:, 0], mrow[:]))
                then_wait(nc.vector.tensor_tensor(mres[:], mrow[:], mpart[:, 0], ALU.subtract))
                then_wait(nc.vector.tensor_copy(mpart[:, 1], mres[:]))
                nc.vector.tensor_tensor(mpart[:, 2], mres[:], mpart[:, 1], ALU.subtract).then_inc(mpart_ready, 1)
                dve.wait_ge(std_ready, 1)
                then_wait(nc.vector.reciprocal(rstd[:], rstd[:]))

                def normalise(g, u):
                    if not (isinstance(g, int) and g < 2):
                        dve.wait_ge(xn_turned, g - 1)
                    for j in range(GB):
                        b = g * GB + j
                        nc.vector.tensor_scalar(xn[:, u, j], xs[:, b], mv[:, b, 0:1], rstd[:, bass.ds(b, 1)],
                                                ALU.subtract, ALU.mult).then_inc(xn_written, 1)

                def bias_v(g):
                    dve.wait_ge(v_done, g + 1)
                    nc.vector.tensor_tensor(
                        va[:, bass.ds(g * GB, GB), :, 0:DK].rearrange("p b h d -> p (b h) d"),
                        ps1[:, 0].rearrange("p (c d) -> p c d", d=DK),
                        bv_row[:].unsqueeze(1).to_broadcast([P, GB, D]).rearrange("p b (h d) -> p b h d", h=H),
                        ALU.add).then_inc(v_copied, 1)

                def split(g, u):
                    dve.wait_ge(qk_copied, g + 1)
                    nc.vector.tensor_tensor(qkf[:, u], qkf[:, u], parts[:, u, 0], ALU.subtract).then_inc(split1, 1)
                    dve.wait_ge(split1, g * 2 + 1)
                    nc.vector.tensor_copy(parts[:, u, 1], qkf[:, u]).then_inc(split1, 1)
                    dve.wait_ge(split1, g * 2 + 2)
                    nc.vector.tensor_tensor(parts[:, u, 2], qkf[:, u], parts[:, u, 1], ALU.subtract)\
                        .then_inc(parts_ready, 1)

                normalise(0, 0)
                normalise(1, 1)
                dve.wait_ge(ones_ready, 1)
                with dve.Fori(0, STEADY) as it:
                    for u in range(2):
                        g = it * 2 + u
                        normalise(g + 2, u)
                        bias_v(g)
                        split(g, u)
                for g in range(NG - 2, NG):
                    bias_v(g)
                    split(g, g % 2)

            @block.tensor
            def _(pe):
                def turn(g, u, half):
                    pe.wait_ge(xn_written, (g + 1) * GB)
                    if not (isinstance(g, int) and g == 0):
                        pe.wait_ge(turned_copied, g * 2)
                    for j in range(GB):
                        ins = nc.tensor.transpose(ps2[:, 0, j * P:(j + 1) * P], xn[:, u, j], ident[:])
                    ins.then_inc(xn_turned, 1)
                    pe.wait_ge(ctx_loaded[u], half * 16 + 16)
                    for j in range(GB):
                        ins = nc.tensor.transpose(ps2[:, 1, j * P:(j + 1) * P], cg[:, u, j], ident[:])
                    ins.then_inc(ctx_turned, 1)

                def project(g, u):
                    pe.wait_ge(turned_copied, g * 2 + 2)
                    if not (isinstance(g, int) and g == 0):
                        pe.wait_ge(qk_copied, g)
                    nc.tensor.matmul(ps2[:, 2], w_sb["q"][:], xnT[:, u], start=True, stop=True)
                    nc.tensor.matmul(ps2[:, 3], w_sb["k"][:], ctxT[:, u], start=True, stop=True).then_inc(qk_done, 1)
                    if not (isinstance(g, int) and g == 0):
                        pe.wait_ge(v_copied, g)
                    for j in range(GB):
                        ins = nc.tensor.matmul(ps1[:, 0, j * P:(j + 1) * P], ctxT[:, u, j * P:(j + 1) * P],
                                               w_sb["v"][:], start=True, stop=True)
                    ins.then_inc(v_done, 1)

                pe.wait_ge(ident_ready, 2)
                pe.wait_ge(small_loaded, 16 * SMALL)
                turn(0, 0, 0)
                turn(1, 1, 0)
                project(0, 0)
                turn(2, 0, 1)
                project(1, 1)
                with pe.Fori(1, STEADY) as it:
                    for u in range(2):
                        g = it * 2 + u
                        turn(g + 1, 1 - u, it + u)
                        project(g, u)
                turn(NG - 1, 1, NG // 2 - 1)
                project(NG - 2, 0)
                project(NG - 1, 1)
        early.close()

        rmax = sb("rmax", [P, H])
        nmax = sb("nmax", [P, 2, H])
        npT = sb("npT", [PARTS * H, 2, S], BF16)
        vst = sb("vst", [P, 2, H, VW])
        oT = sb("oT", [P, HB * P])
        rden = sb("rden", [P, H])
        attn = sb("attn", [P, H, DK])
        attnT = sb("attnT", [P, S])
        st2 = sb("st2", [P, GB, 6])
        mv2 = sb("mv2", [P, GB, 2])
        rstd2 = sb("rstd2", [P, GB])
        xr = sb("xr", [P, 2, 2, GB, XW])
        xr_u = xr[:].bitcast(U32)
        xrT = sb("xrT", [P, GT])
        lg = sb("lg", [P, GB, E])
        tmp = sb("tmp", [P, GB, E])
        oh = [sb(f"oh{k}", [P, GB, E]) for k in range(2)]
        ohb = sb("ohb", [P, GB, E], BF16)
        rank = sb("rank", [P, GB, E])
        lk = [sb(f"lk{k}", [P, GB]) for k in range(2)]
        first = sb("first", [P, GB])
        ed = sb("ed", [P, GB])
        ed1 = sb("ed1", [P, GB])
        wt = sb("wt", [P, GB])
        new_oh = sb("new_oh", [P, E])
        posf = sb("posf", [P, 2, GB])
        pos = sb("pos", [P, 2, 2, GB], U32)

        qk_loaded = sem("qk_loaded")
        max_scored = sem("max_scored")
        max_taken = sem("max_taken")
        npart_ready = sem("npart_ready")
        npart_turned = sem("npart_turned")
        npT_ready = sem("npT_ready")
        nmax_loaded = [sem(f"nmax_loaded{u}") for u in range(2)]
        pool_b = sem("pool_b")
        scored = sem("scored")
        exp_done = sem("exp_done")
        vst_ready = sem("vst_ready")
        pv_done = sem("pv_done")
        oT_ready = sem("oT_ready")
        o_turned = sem("o_turned")
        rden_ready = sem("rden_ready")
        attn_ready = sem("attn_ready")
        attn_turned = sem("attn_turned")
        attnT_ready = sem("attnT_ready")
        out_done = sem("out_done")
        res_done = sem("res_done")
        res_stored = sem("res_stored")
        zeroed = sem("zeroed")
        wait_passed = [sem(f"wait_passed{e}") for e in range(2)]
        r_stats = sem("r_stats")
        r_std = sem("r_std")
        r_pool = sem("r_pool")
        xr_ready = sem("xr_ready")
        xr_turned = sem("xr_turned")
        xrT_ready = sem("xrT_ready")
        logits_done = sem("logits_done")
        logits_taken = sem("logits_taken")
        r_mean = sem("r_mean")
        choice_step = sem("choice_step")
        gate_step = sem("gate_step")
        place_step = sem("place_step")
        gap_ready = sem("gap_ready")
        odds_ready = sem("odds_ready")
        oh_ready = sem("oh_ready")
        ranked = sem("ranked")
        rank_taken = sem("rank_taken")
        oh_summed = sem("oh_summed")
        gates_written = sem("gates_written")
        pos_ready = sem("pos_ready")
        rows_ready = sem("rows_ready")
        scattered = [sem(f"scattered{u}") for u in range(2)]

        LOADS = len(Q_PART) * 2 + 1
        AHEAD = 2
        UNROLL = 2 * GB
        LOOPS = B // UNROLL - 2
        ps_np = ps1[:, 0, 0:S // 2].bitcast(BF16)
        ps_l = ps1[:, 1, 0:GB * E]
        ps_aT = psy[:, 0:P]
        ps_y = psy[:, P:2 * P]
        QW = P // HB
        ps_on = psm[:].rearrange("p (h v) -> p h v", v=QW)

        class At:
            def __init__(self, it, c):
                self.it, self.c = it, c
                self.b = it * UNROLL + c
                self.g = it * (UNROLL // GB) + c // GB
                self.j = c % GB
                self.u = (c // GB) % 2
                self.half = it * (UNROLL // 2) + c // 2
                self.known = isinstance(it, int)

            def plus(self, n):
                return At(self.it, self.c + n)

            def exists(self):
                return not self.known or 0 <= self.b < B

            def is_past(self, n):
                return not self.known or self.b >= n

        def batches(eng, step):
            for c in range(UNROLL):
                step(At(0, c))
            with eng.Fori(1, 1 + LOOPS) as it:
                for c in range(UNROLL):
                    step(At(it, c))
            for c in range(UNROLL):
                step(At(B // UNROLL - 1, c))

        class Group:
            def __init__(self, at, less):
                self.g = at.g - less
                self.u = (at.c // GB - less) % 2
                self.half = at.it * (UNROLL // GB // 2) + (at.c // GB - less) // 2
                self.known = at.known

            def exists(self):
                return not self.known or 0 <= self.g < NG

            def is_past(self, n):
                return not self.known or self.g >= n

        def route(at, phase):
            g = Group(at, 2 if phase == 4 else 1)
            return g if at.j == phase % GB and g.exists() else None

        def stand_alone(eng):
            eng.sem_inc(wait_passed[eng is nc.gpsimd], 1)

        def last_steps(step):
            for c in range(UNROLL, UNROLL + GB + 2):
                step(At(B // UNROLL - 1, c))

        with nc.Block() as block:
            @block.sync
            def _(sp):
                def load_group(g, u):
                    for tile, s, slots in ((qs, 0, Q_PART), (ks, 1, K_PART)):
                        for n, a in enumerate(slots):
                            sp.dma_start(tile[u][n * DK:(n + 1) * DK],
                                         qk_d[a, s].rearrange("(h d) t -> d h t", d=DK)[:, :, bass.ds(g * GT, GT)])\
                                .then_inc(qk_loaded, 16)
                    sp.dma_start(ks[u][ROWS_P:ROWS_M],
                                 mask_d[:, bass.ds(g * GT, GT)].unsqueeze(1).to_broadcast([PARTS, H, GT]))\
                        .then_inc(qk_loaded, 16)

                def load_max(at):
                    sp.wait_ge(npT_ready, at.b + 1)
                    for a in range(PARTS):
                        sp.dma_start(qs[at.u][ROWS_M + a:ROWS_M + a + 1, :, at.j * S:(at.j + 1) * S],
                                     npT[a * H:(a + 1) * H, at.c % 2]).then_inc(nmax_loaded[at.c % 2], 16)

                def store_res(g):
                    sp.wait_ge(res_done, (g + 1) * GB)
                    sp.dma_start(acc_d[0:T].rearrange("(b s) d -> s b d", s=S)[:, bass.ds(g * GB, GB)],
                                 xs[:, bass.ds(g * GB, GB)]).then_inc(res_stored, 16)

                def step(at):
                    if at.j == 0 and (not at.known or at.g + 1 < NG):
                        if at.is_past(1):
                            sp.wait_ge(scored, at.b * NB)
                        load_group(at.g + 1, 1 - at.u)
                    if at.plus(AHEAD).exists():
                        load_max(at.plus(AHEAD))
                    if at.j == 2 and at.is_past(GB):
                        store_res(at.g - 1)

                load_group(0, 0)
                for c in range(AHEAD):
                    load_max(At(0, c))
                batches(sp, step)
                store_res(NG - 1)
                sp.wait_ge(res_stored, 16 * NG)

            @block.tensor
            def _(pe):
                window = wmask[:].rearrange("p h s -> p (h s)")

                def score_max(at):
                    col = at.j * S
                    if at.j == 0:
                        pe.wait_ge(qk_loaded, (at.g + 1) * (16 * LOADS))
                    if at.is_past(1):
                        pe.wait_ge(npT_ready, at.b)
                    for n in range(NB):
                        if n == 1 and at.is_past(AHEAD):
                            routed(at.plus(-AHEAD))
                        if at.is_past(1) or n >= 2:
                            pe.wait_ge(max_taken, at.b * NB + (n - 1))
                        bank = ps1[:, n % 2]
                        nc.tensor.matmul(bank, ident_b[:], window, start=True, stop=False)
                        for j in range(HB):
                            h = n * HB + j
                            ins = nc.tensor.matmul(bank[:, j * S:(j + 1) * S], qs[at.u][0:ROWS_M, h, col:col + S],
                                                   ks[at.u][0:ROWS_M, h, col:col + S], start=False, stop=(j == HB - 1))
                        ins.then_inc(max_scored, 1)

                def routed(at):
                    if (r := route(at.plus(-1), 2)):
                        pe.wait_ge(logits_taken, r.g + 1)
                    if (r := route(at.plus(-1), 4)):
                        pe.wait_ge(rank_taken, r.g + 1)

                def turn_max(at):
                    pe.wait_ge(npart_ready, at.b + 1)
                    nc.tensor.transpose(ps_np, npart[:].rearrange("p a h -> p (a h)"), ident_b[:]).then_inc(npart_turned, 1)

                def score(at):
                    col = at.j * S
                    pe.wait_ge(nmax_loaded[at.c % 2], at.half * (16 * PARTS) + 16 * PARTS)
                    if at.is_past(1):
                        pe.wait_ge(exp_done, at.b * 2)
                    for n in range(NB):
                        bank = ps2[:, n]
                        nc.tensor.matmul(bank, ident_b[:], window, start=True, stop=False)
                        for j in range(HB):
                            h = n * HB + j
                            ins = nc.tensor.matmul(bank[:, j * S:(j + 1) * S], ks[at.u][0:ROWS_X, h, col:col + S],
                                                   qs[at.u][0:ROWS_X, h, col:col + S], start=False, stop=(j == HB - 1))
                        ins.then_inc(scored, 1)

                def values(at):
                    pe.wait_ge(vst_ready, at.b + 1)
                    if at.is_past(1):
                        pe.wait_ge(attn_ready, at.b)
                    for n in range(NB):
                        if n % 2 == 0:
                            pe.wait_ge(exp_done, at.b * 2 + (n // 2 + 1))
                        for j in range(HB):
                            h = n * HB + j
                            ins = nc.tensor.matmul(psm[j * QW:j * QW + VW, n * P:(n + 1) * P], vst[:, at.c % 2, h],
                                                   pT[:, h], start=True, stop=True)
                    ins.then_inc(pv_done, 1)

                def turn_values(at):
                    pe.wait_ge(oT_ready, at.b + 1)
                    for n in range(NB):
                        ins = nc.tensor.transpose(psm[:, n * P:(n + 1) * P], oT[:, n * P:(n + 1) * P], ident[:])
                    ins.then_inc(o_turned, 1)

                def turn_attn(at):
                    pe.wait_ge(attn_ready, at.b + 1)
                    if at.is_past(1):
                        pe.wait_ge(res_done, at.b)
                    nc.tensor.transpose(ps_aT, attn[:].rearrange("p h d -> p (h d)"), ident[:]).then_inc(attn_turned, 1)

                def project(at):
                    pe.wait_ge(attnT_ready, at.b + 1)
                    nc.tensor.matmul(ps_y, attnT[:], w_sb["o"][:], start=True, stop=True).then_inc(out_done, 1)

                def turn_rows(r):
                    pe.wait_ge(xr_ready, (r.g + 1) * GB)
                    for j in range(GB):
                        ins = nc.tensor.transpose(psy[:, j * P:(j + 1) * P], xr[:, r.u, 0, j, 0:D], ident[:])
                    ins.then_inc(xr_turned, 1)

                def logits(r):
                    pe.wait_ge(xrT_ready, r.g + 1)
                    for j in range(GB):
                        ins = nc.tensor.matmul(ps_l[:, j * E:(j + 1) * E], xrT[:, j * P:(j + 1) * P], gate_sb[:],
                                               start=True, stop=True)
                    ins.then_inc(logits_done, 1)

                def ranks(r):
                    pe.wait_ge(oh_ready, r.g + 1)
                    pe.wait_ge(oh_summed, r.g + 1)
                    nc.tensor.matmul(ps_l, tri[:], ohb[:].rearrange("p b e -> p (b e)"), start=True, stop=False)
                    for j in range(GB - 1):
                        n = GB - 1 - j
                        nc.tensor.matmul(ps_l[:, (j + 1) * E:].rearrange("p (b e) -> p b e", e=E), ones_b[:],
                                         ohb[:, j].unsqueeze(1).to_broadcast([P, n, E]), start=False, stop=False)
                    nc.tensor.matmul(ps_l.rearrange("p (b e) -> p b e", e=E), ones_b[:],
                                     oh_sum[:].unsqueeze(1).to_broadcast([P, GB, E]), start=False, stop=True)\
                        .then_inc(ranked, 1)

                def step(at):
                    last, ahead = at.plus(-1), at.plus(AHEAD)
                    if at.exists():
                        score(at)
                    if at.is_past(1) and last.exists():
                        turn_values(last)
                    if (r := route(at, 2)):
                        if at.plus(-2).exists():
                            pe.wait_ge(res_done, at.b - 1)
                        turn_rows(r)
                    if ahead.exists():
                        score_max(ahead)
                    if at.is_past(1) and last.exists():
                        if (r := route(at, 2)):
                            pe.wait_ge(xrT_ready, r.g + 1)
                        turn_attn(last)
                    if at.exists():
                        values(at)
                    if at.is_past(1) and last.exists():
                        project(last)
                    if ahead.exists():
                        turn_max(ahead)
                    if (r := route(at, 2)):
                        logits(r)
                    if (r := route(at, 4)):
                        ranks(r)

                pe.wait_ge(zeroed, 1)
                for c in range(AHEAD):
                    score_max(At(0, c))
                    turn_max(At(0, c))
                batches(pe, step)
                last_steps(step)

            @block.scalar
            def _(act):
                def copy_max(at):
                    act.wait_ge(npart_turned, at.b + 1)
                    if at.is_past(2):
                        act.wait_ge(nmax_loaded[at.c % 2], at.half * (16 * PARTS))
                    nc.scalar.copy(npT[:, at.c % 2], ps_np[0:PARTS * H]).then_inc(npT_ready, 1)

                def exps(at, n):
                    act.wait_ge(scored, at.b * NB + (n + 1) * (NB // 2))
                    if at.is_past(1):
                        act.wait_ge(pv_done, at.b)
                    lo, hi = n * (NB // 2), (n + 1) * (NB // 2)
                    nc.scalar.activation(pT[:, lo * HB:hi * HB].rearrange("p h s -> p (h s)"),
                                         ps2[:, lo:hi].rearrange("p n s -> p (n s)"), ACT.Exp).then_inc(exp_done, 1)

                def copy_values(at):
                    act.wait_ge(pv_done, at.b + 1)
                    nc.scalar.copy(oT[:], psm[:]).then_inc(oT_ready, 1)

                def copy_attn(at):
                    act.wait_ge(attn_turned, at.b + 1)
                    nc.scalar.copy(attnT[:], ps_aT).then_inc(attnT_ready, 1)

                def copy_rows(r):
                    act.wait_ge(xr_turned, r.g + 1)
                    if r.is_past(1):
                        act.wait_ge(logits_done, r.g)
                    nc.scalar.copy(xrT[:], psy[:]).then_inc(xrT_ready, 1)

                def odds(r):
                    act.wait_ge(gap_ready, r.g + 1)
                    nc.scalar.activation(ed[:], ed[:], ACT.Exp).then_inc(odds_ready, 1)

                def step(at):
                    last, ahead = at.plus(-1), at.plus(AHEAD)
                    if at.is_past(1) and last.exists():
                        copy_values(last)
                        if last.plus(AHEAD).exists():
                            copy_max(last.plus(AHEAD))
                    if at.exists():
                        exps(at, 0)
                    if (r := route(at, 2)):
                        copy_rows(r)
                    if (r := route(at, 4)):
                        odds(r)
                    if at.exists():
                        exps(at, 1)
                    if at.is_past(1) and last.exists():
                        copy_attn(last)

                for c in range(AHEAD):
                    copy_max(At(0, c))
                batches(act, step)
                last_steps(step)

            @block.vector
            def _(dve):
                def take_max(at):
                    for n in range(NB):
                        dve.wait_ge(max_scored, at.b * NB + (n + 1))
                        if n == 0 and at.is_past(1):
                            dve.wait_ge(npart_ready, at.b)
                        nc.vector.tensor_reduce(rmax[:, n * HB:(n + 1) * HB],
                                                ps1[:, n % 2].rearrange("p (h s) -> p h s", h=HB),
                                                AX.X, ALU.max).then_inc(max_taken, 1)

                def residual(at):
                    dve.wait_ge(out_done, at.b + 1)
                    nc.vector.scalar_tensor_tensor(out=xs[:, at.b], in0=ps_y, scalar=tg[:, 0:1], in1=xs[:, at.b],
                                                   op0=ALU.mult, op1=ALU.add).then_inc(res_done, 1)
                    dve.wait_ge(res_done, at.b + 1)
                    stand_alone(dve)
                    nc.vector.bn_stats(st2[:, at.j], xs[:, at.b]).then_inc(r_stats, 1)

                def normalise(at):
                    dve.wait_ge(o_turned, at.b + 1)
                    nc.vector.reciprocal(rden[:], ps_on[:, :, DK]).then_inc(rden_ready, 1)
                    dve.wait_ge(rden_ready, at.b + 1)
                    nc.vector.tensor_tensor(attn[:], ps_on[:, :, 0:DK], rden[:].unsqueeze(2).to_broadcast([P, H, DK]),
                                            ALU.mult).then_inc(attn_ready, 1)

                gbe = [P, GB, E]
                iota_g = iota_e[:].unsqueeze(1).to_broadcast(gbe)

                class InARow:
                    def __init__(self, done, r, count):
                        self.done, self.before, self.count, self.n = done, r.g * count, count, 0

                    def __call__(self, ins):
                        self.n += 1
                        assert self.n <= self.count
                        ins.then_inc(self.done, 1)
                        dve.wait_ge(self.done, self.before + self.n)

                def route_norm(r):
                    dve.wait_ge(r_stats, (r.g + 1) * GB)
                    stand_alone(dve)
                    for j in range(GB):
                        nc.vector.bn_aggr(mv2[:, j], st2[:, j]).then_inc(r_mean, 1)
                    dve.wait_ge(r_mean, (r.g + 1) * GB)
                    dve.sem_inc(r_std, 1)
                    dve.wait_ge(r_pool, r.g * 2 + 2)
                    for j in range(GB):
                        b = r.g * GB + j
                        nc.vector.tensor_scalar(xr[:, r.u, 0, j, 0:D], xs[:, b], mv2[:, j, 0:1], rstd2[:, j:j + 1],
                                                ALU.subtract, ALU.mult).then_inc(xr_ready, 1)

                def take_logits(r):
                    dve.wait_ge(logits_done, r.g + 1)
                    nc.vector.tensor_copy(lg[:].rearrange("p b e -> p (b e)"), ps_l).then_inc(logits_taken, 1)
                    dve.wait_ge(logits_taken, r.g + 1)

                def choose(r):
                    then_wait = InARow(choice_step, r, 11)
                    for k in range(2):
                        then_wait(nc.vector.tensor_reduce(lk[k][:], lg[:], AX.X, ALU.max))
                        then_wait(nc.vector.tensor_tensor(tmp[:], lg[:], lk[k][:].unsqueeze(2).to_broadcast(gbe), ALU.is_equal))
                        then_wait(nc.vector.tensor_tensor(tmp[:], tmp[:], iota_g, ALU.mult))
                        then_wait(nc.vector.tensor_reduce(first[:], tmp[:], AX.X, ALU.min))
                        then_wait(nc.vector.tensor_tensor(oh[k][:], iota_g, first[:].unsqueeze(2).to_broadcast(gbe), ALU.is_equal))
                        if k == 0:
                            then_wait(nc.vector.scalar_tensor_tensor(
                                out=lg[:].rearrange("p b e -> p (b e)"), in0=oh[0][:].rearrange("p b e -> p (b e)"),
                                scalar=-3e38, in1=lg[:].rearrange("p b e -> p (b e)"), op0=ALU.mult, op1=ALU.add))
                    nc.vector.tensor_tensor(ed[:], lk[1][:], lk[0][:], ALU.subtract).then_inc(gap_ready, 1)
                    nc.vector.tensor_tensor(ohb[:], oh[0][:], oh[1][:], ALU.add).then_inc(oh_ready, 1)

                def gate(r):
                    then_wait = InARow(gate_step, r, 3)
                    dve.wait_ge(odds_ready, r.g + 1)
                    then_wait(nc.vector.tensor_scalar(ed1[:], ed[:], 1.0, None, ALU.add))
                    then_wait(nc.vector.reciprocal(ed1[:], ed1[:]))
                    then_wait(nc.vector.tensor_scalar(wt[:], ed1[:], tg[:, 1:2], None, ALU.mult))
                    nc.vector.tensor_copy(xr[:, r.u, 0, :, X_GATE], wt[:])
                    nc.vector.tensor_tensor(xr[:, r.u, 1, :, X_GATE], wt[:], ed[:], ALU.mult).then_inc(gates_written, 1)

                def take_ranks(r):
                    dve.wait_ge(ranked, r.g + 1)
                    nc.vector.tensor_tensor(rank[:], ps_l.rearrange("p (b e) -> p b e", e=E),
                                            cap_e[:].unsqueeze(1).to_broadcast(gbe), ALU.add).then_inc(rank_taken, 1)
                    dve.wait_ge(rank_taken, r.g + 1)

                def places(r):
                    then_wait = InARow(place_step, r, 5)
                    for k in range(2):
                        then_wait(nc.vector.tensor_tensor(tmp[:], oh[k][:], rank[:], ALU.mult))
                        then_wait(nc.vector.tensor_reduce(posf[:, k], tmp[:], AX.X, ALU.add))
                    nc.vector.tensor_copy(pos[:, r.u], posf[:]).then_inc(pos_ready, 1)
                    then_wait(nc.vector.tensor_reduce(new_oh[:], ohb[:].rearrange("p b e -> p e b"), AX.X, ALU.add))
                    nc.vector.tensor_tensor(oh_sum[:], oh_sum[:], new_oh[:], ALU.add).then_inc(oh_summed, 1)
                    dve.wait_ge(oh_summed, r.g + 2)

                def step(at):
                    last, ahead = at.plus(-1), at.plus(AHEAD)
                    if at.is_past(2) and at.plus(-2).exists():
                        residual(at.plus(-2))
                    if (r := route(last, 2)):
                        take_logits(r)
                    if (r := route(last, 4)):
                        take_ranks(r)
                    if at.is_past(1) and last.exists():
                        normalise(last)
                    if ahead.exists():
                        take_max(ahead)
                    if (r := route(at, 1)):
                        route_norm(r)
                    if (r := route(last, 2)):
                        choose(r)
                    if (r := route(at, 4)):
                        gate(r)
                    if (r := route(last, 4)):
                        places(r)

                nc.vector.memset(psm[:], 0.0).then_inc(zeroed, 1)
                dve.sem_inc(oh_summed, 1)
                for c in range(AHEAD):
                    take_max(At(0, c))
                batches(dve, step)
                last_steps(step)

            @block.gpsimd
            def _(pool):
                POOL_B = 4

                def split_max(at):
                    def then_wait(ins, n):
                        ins.then_inc(pool_b, 1)
                        pool.wait_ge(pool_b, at.b * POOL_B + n)
                        stand_alone(pool)

                    pool.wait_ge(max_taken, at.b * NB + NB)
                    if at.is_past(1):
                        pool.wait_ge(npart_turned, at.b)
                    stand_alone(pool)
                    then_wait(pool.tensor_scalar(nmax[:, 0], rmax[:], -1.0, 0.0, ALU.mult, ALU.add), 1)
                    then_wait(pool.tensor_copy(npart[:, 0], nmax[:, 0]), 2)
                    then_wait(pool.tensor_tensor(nmax[:, 1], nmax[:, 0], npart[:, 0], ALU.subtract), 3)
                    then_wait(pool.tensor_copy(npart[:, 1], nmax[:, 1]), 4)
                    pool.tensor_tensor(npart[:, 2], nmax[:, 1], npart[:, 1], ALU.subtract).then_inc(npart_ready, 1)

                def copy_v(at):
                    if at.is_past(2):
                        pool.wait_ge(pv_done, at.b - 1)
                    stand_alone(pool)
                    pool.tensor_copy(vst[:, at.c % 2], va[:, at.b]).then_inc(vst_ready, 1)

                def route_std(r):
                    pool.wait_ge(r_std, r.g + 1)
                    stand_alone(pool)
                    pool.tensor_scalar(rstd2[:], mv2[:, :, 1], EPS, 0.0, ALU.add, ALU.add).then_inc(r_pool, 1)
                    pool.wait_ge(r_pool, r.g * 2 + 1)
                    pool.tensor_tensor(rstd2[:], rstd2[:], minus_half[:], ALU.pow).then_inc(r_pool, 1)

                def route_rows(r):
                    pool.wait_ge(xr_ready, (r.g + 1) * GB)
                    stand_alone(pool)
                    pool.tensor_copy(xr[:, r.u, 1, :, 0:D], xr[:, r.u, 0, :, 0:D]).then_inc(rows_ready, 1)
                    for k in range(2):
                        pool.tensor_copy(xr_u[:, r.u, k, :, X_IDX], idx_f[:]).then_inc(rows_ready, 1)
                    pool.wait_ge(rows_ready, r.g * 4 + 3)
                    stand_alone(pool)
                    pool.tensor_scalar(idx_f[:], idx_f[:], float(GT), 0.0, ALU.add, ALU.add).then_inc(rows_ready, 1)
                    pool.wait_ge(rows_ready, r.g * 4 + 4)
                    stand_alone(pool)

                def scatter(r, j):
                    if j == 0:
                        pool.wait_ge(pos_ready, r.g + 1)
                        pool.wait_ge(gates_written, r.g + 1)
                        stand_alone(pool)
                    for k in range(2):
                        pool.indirect_dma_start(
                            out=rows_d, out_offset=bass.IndirectOffsetOnAxis(ap=pos[:, r.u, k, j:j + 1], axis=0),
                            in_=xr[:, r.u, k, j], in_offset=None).then_inc(scattered[r.u], 16)

                def step(at):
                    ahead = at.plus(AHEAD)
                    if ahead.exists():
                        split_max(ahead)
                    if (r := route(at, 1)):
                        route_std(r)
                    if (r := route(at, 2)):
                        route_rows(r)
                    if at.plus(1).exists():
                        copy_v(at.plus(1))
                    r = Group(at, 2)
                    if at.j == 1 and r.exists():
                        scatter(r, 0)
                        scatter(r, 1)
                    if at.j in (2, 3) and r.exists():
                        scatter(r, at.j)
                    if at.j == 3 and r.exists():
                        pool.wait_ge(scattered[r.u], r.half * (2 * GB * 16) + 2 * GB * 16)
                        stand_alone(pool)

                for c in range(AHEAD):
                    split_max(At(0, c))
                copy_v(At(0, 0))
                batches(pool, step)
                for c in range(UNROLL, UNROLL + 2 * GB):
                    step(At(B // UNROLL - 1, c))
                for u in range(2):
                    pool.wait_ge(scattered[u], NG // 2 * (2 * GB * 16))

        cnt = sb("cnt", [P, E])
        nt_f = sb("nt_f", [P, E])
        nt_i = sb("nt_i", [P, E], I32)
        nt_s = sb("nt_s", [P, E], I32)
        cum = sb("cum", [P, E])
        skip = sb("skip", [P, E])
        end_f = sb("end_f", [P, E])
        end_i = sb("end_i", [P, E], I32)
        past = sb("past", [P, NT, E])
        tile_f = sb("tile_f", [P, NT])
        tile_e = sb("tile_e", [P, NT], I32)
        tile_r = sb("tile_r", [P, NT], I32)
        plan_step = sem("plan_step")
        counted = sem("counted")
        end_ready = sem("end_ready")
        tail_stored = sem("tail_stored")

        with nc.Block() as block:
            @block.tensor
            def _(pe):
                nc.tensor.matmul(psy[:, 0:E], ones_b[:], oh_sum[:], start=True, stop=True).then_inc(counted, 1)

            @block.vector
            def _(dve):
                steps = [0]

                def then_wait(ins):
                    steps[0] += 1
                    ins.then_inc(plan_step, 1)
                    dve.wait_ge(plan_step, steps[0])

                dve.wait_ge(counted, 1)
                then_wait(nc.vector.tensor_copy(cnt[:], psy[:, 0:E]))
                then_wait(nc.vector.tensor_tensor(end_f[:], cnt[:], cap_e[:], ALU.add))
                nc.vector.tensor_copy(end_i[:], end_f[:]).then_inc(end_ready, 1)
                then_wait(nc.vector.tensor_scalar(nt_f[:], cnt[:], float(P - 1), None, ALU.add))
                then_wait(nc.vector.tensor_copy(nt_i[:], nt_f[:]))
                then_wait(nc.vector.tensor_scalar(nt_s[:], nt_i[:], P.bit_length() - 1, None, ALU.arith_shift_right))
                then_wait(nc.vector.tensor_copy(nt_f[:], nt_s[:]))
                then_wait(nc.vector.tensor_tensor_scan(cum[:], ones_s[:], nt_f[:], 0.0, ALU.mult, ALU.add))
                then_wait(nc.vector.tensor_scalar(skip[:], nt_f[:], -float(P), float(CAP), ALU.mult, ALU.add))
                te = [P, NT, E]
                then_wait(nc.vector.tensor_tensor(past[:], iota_t[:].unsqueeze(2).to_broadcast(te),
                                                  cum[:].unsqueeze(1).to_broadcast(te), ALU.is_ge))
                then_wait(nc.vector.tensor_reduce(tile_f[:], past[:], AX.X, ALU.add))
                then_wait(nc.vector.tensor_scalar(tile_f[:], tile_f[:], float(E - 1), float(F), ALU.min, ALU.mult))
                then_wait(nc.vector.tensor_copy(tile_e[:], tile_f[:]))
                then_wait(nc.vector.tensor_tensor(past[:], past[:], skip[:].unsqueeze(1).to_broadcast(te), ALU.mult))
                then_wait(nc.vector.tensor_reduce(tile_f[:], past[:], AX.X, ALU.add))
                then_wait(nc.vector.scalar_tensor_tensor(out=tile_f[:], in0=iota_t[:], scalar=float(P), in1=tile_f[:],
                                                         op0=ALU.mult, op1=ALU.add))
                then_wait(nc.vector.tensor_copy(tile_r[:], tile_f[:]))

            @block.sync
            def _(sp):
                sp.wait_ge(end_ready, 1)
                for e in range(E):
                    row = sp.value_load(end_i[0:1, e:e + 1], min_val=e * CAP, max_val=e * CAP + T)
                    sp.dma_start(rows_d[bass.ds(row, P)], fill[:]).then_inc(tail_stored, 16)
                sp.wait_ge(tail_stored, 16 * E)

        xg = sb("xg", [P, RING, XW])
        xg_u = xg[:].bitcast(U32)
        xgT = sb("xgT", [P, P])
        act_s = sb("act_s", [P, F])
        hid = sb("hid", [P, F])
        hidT = sb("hidT", [P, FC, P])
        yt = sb("yt", [P, 2, D])
        xg_loaded = [sem(f"xg_loaded{u}") for u in range(RING)]
        xg_free = sem("xg_free")
        xg_turned = sem("xg_turned")
        xgT_ready = sem("xgT_ready")
        gate_done = sem("gate_done")
        up_done = sem("up_done")
        silu_done = sem("silu_done")
        hid_ready = sem("hid_ready")
        hid_turned = sem("hid_turned")
        hidT_ready = sem("hidT_ready")
        down_done = sem("down_done")
        yt_ready = sem("yt_ready")
        added = sem("added")
        out_stored = sem("out_stored")

        ps_a, ps_b = ps2[:, 0], ps2[:, 1]
        ps_h = ps2[:, 2]
        ps_x = psm[:, 0:P]
        ps_d = psy[:, 0:D]
        assert NT % RING == 0 and RING % 2 == 0

        def tiles(eng, step, lo, hi):
            turns = (hi - lo) // RING
            with eng.Fori(0, turns) as it:
                for c in range(lo, lo + RING):
                    step(it * RING + c, c % RING, it + c // RING)
            for t in range(lo + turns * RING, hi):
                step(t, t % RING, t // RING)

        with nc.Block() as block:
            @block.sync
            def _(sp):
                def load(t, u, turn):
                    row = sp.value_load(tile_r[0:1, bass.ds(t, 1)], min_val=0, max_val=E * CAP + (E - 1) * P)
                    sp.wait_ge(xg_free, t + 1)
                    sp.dma_start(xg[:, u], rows_d[bass.ds(row, P)]).then_inc(xg_loaded[u], 16)

                tiles(sp, load, 0, NT)
                sp.wait_ge(added, 16 * NT)
                for i in range(XCH):
                    n = B // XCH
                    sp.dma_start(out[i * n:(i + 1) * n].rearrange("b s d -> (b s) d"),
                                 acc_d[i * n * S:(i + 1) * n * S]).then_inc(out_stored, 16)
                sp.wait_ge(out_stored, 16 * XCH)

            @block.tensor
            def _(pe):
                def expert(t):
                    return pe.value_load(tile_e[0:1, t:t + 1] if isinstance(t, int) else tile_e[0:1, bass.ds(t, 1)],
                                         min_val=0, max_val=(E - 1) * F)

                def turn_rows(t, u, turn):
                    pe.wait_ge(xg_loaded[u], turn * 16 + 16)
                    nc.tensor.transpose(ps_x, xg[:, u, 0:D], ident[:]).then_inc(xg_turned, 1)

                def up(t, at):
                    pe.wait_ge(xgT_ready, t + 1)
                    nc.tensor.matmul(ps_a, xgT[:], w1_sb[:].rearrange("p e f -> p (e f)")[:, bass.ds(at, F)],
                                     start=True, stop=True).then_inc(gate_done, 1)
                    nc.tensor.matmul(ps_b, xgT[:], w3_sb[:].rearrange("p e f -> p (e f)")[:, bass.ds(at, F)],
                                     start=True, stop=True).then_inc(up_done, 1)

                def turn_hidden(t):
                    pe.wait_ge(hid_ready, t + 1)
                    for c in range(FC):
                        ins = nc.tensor.transpose(ps_h[:, c * P:(c + 1) * P], hid[:, c * P:(c + 1) * P], ident[:])
                    ins.then_inc(hid_turned, 1)

                def down(t, at):
                    pe.wait_ge(hidT_ready, t + 1)
                    pe.wait_ge(yt_ready, t + 1)
                    for c in range(FC):
                        ins = nc.tensor.matmul(ps_d, hidT[:, c],
                                               w2_sb[:].rearrange("p e c d -> p (e c d)")[:, bass.ds(at + c * D, D)],
                                               start=(c == 0), stop=(c == FC - 1))
                    ins.then_inc(down_done, 1)

                def step(t, u, turn):
                    before, own = expert(t - 1), expert(t)
                    turn_hidden(t - 1)
                    up(t, own)
                    down(t - 1, before)
                    c = u + 1
                    turn_rows(t + 1, c % RING, turn + c // RING)

                pe.wait_ge(w_loaded, 48)
                own = expert(0)
                turn_rows(0, 0, 0)
                up(0, own)
                turn_rows(1, 1, 0)
                tiles(pe, step, 1, NT - 1)
                before, own = expert(NT - 2), expert(NT - 1)
                turn_hidden(NT - 2)
                up(NT - 1, own)
                down(NT - 2, before)
                turn_hidden(NT - 1)
                down(NT - 1, own)

            @block.scalar
            def _(act):
                def copy_rows(t):
                    act.wait_ge(xg_turned, t + 1)
                    nc.scalar.copy(xgT[:], ps_x).then_inc(xgT_ready, 1)

                def gate(t):
                    act.wait_ge(gate_done, t + 1)
                    nc.scalar.activation(act_s[:], ps_a, ACT.Silu).then_inc(silu_done, 1)

                def scale_out(t, u):
                    act.wait_ge(down_done, t + 1)
                    if not (isinstance(t, int) and t < 2):
                        act.wait_ge(added, (t - 1) * 16)
                    nc.scalar.activation(yt[:, u % 2], ps_d, ACT.Copy, scale=xg[:, u, X_GATE:X_GATE + 1])\
                        .then_inc(yt_ready, 1)

                def step(t, u, turn):
                    gate(t)
                    if not (isinstance(t, int) and t == 0):
                        scale_out(t - 1, (u - 1) % RING)
                    if not (isinstance(t, int) and t == NT - 1):
                        copy_rows(t + 1)

                act.sem_inc(yt_ready, 1)
                copy_rows(0)
                for t in range(RING):
                    step(t, t, 0)
                with act.Fori(1, NT // RING - 1) as it:
                    for u in range(RING):
                        step(it * RING + u, u, it)
                for u in range(RING):
                    step(NT - RING + u, u, NT // RING - 1)
                scale_out(NT - 1, RING - 1)

            @block.vector
            def _(dve):
                def gated(t):
                    dve.wait_ge(silu_done, t + 1)
                    dve.wait_ge(up_done, t + 1)
                    nc.vector.tensor_tensor(hid[:], act_s[:], ps_b, ALU.mult).then_inc(hid_ready, 1)

                def copy_hidden(t):
                    dve.wait_ge(hid_turned, t + 1)
                    nc.vector.tensor_copy(hidT[:].rearrange("p c s -> p (c s)"), ps_h).then_inc(hidT_ready, 1)

                gated(0)
                with dve.Fori(0, NT - 1) as t:
                    copy_hidden(t)
                    gated(t + 1)
                copy_hidden(NT - 1)

            @block.gpsimd
            def _(pool):
                def add(t, u, turn):
                    pool.wait_ge(yt_ready, t + 2)
                    if not (isinstance(t, int) and t == 0):
                        pool.wait_ge(added, t * 16)
                        pool.sem_inc(xg_free, 1)
                    stand_alone(pool)
                    pool.indirect_dma_start(
                        out=acc_d, out_offset=bass.IndirectOffsetOnAxis(ap=xg_u[:, u, X_IDX:X_IDX + 1], axis=0),
                        in_=yt[:, u % 2], in_offset=None, compute_op=ALU.add).then_inc(added, 16)

                pool.sem_inc(xg_free, RING)
                add(0, 0, 0)
                tiles(pool, add, 1, NT)


_INS = ["x", "ctx_1024", "mask_BxS2_ff0", "g_xattn", "g_ffn", "L0_xattn_wq", "L0_xattn_bq", "L0_xattn_wk",
        "L0_xattn_bk", "L0_xattn_wv", "L0_xattn_bv", "L0_xattn_wo", "L0_xattn_bo", "L0_ffn_gate_w",
        "L0_ffn_w1", "L0_ffn_w3", "L0_ffn_w2"]


def kernel(**inputs):
    import concourse.bacc as bacc
    from concourse.bass_utils import run_bass_kernel_spmd

    nc = bacc.Bacc("TRN2", target_bir_lowering=False, num_devices=1)
    arrays, args = {}, []
    for name in _INS:
        a = np.ascontiguousarray(inputs[name])
        arrays[f"in_{name}_dram"] = a
        args.append(nc.dram_tensor(f"in_{name}_dram", a.shape, mybir.dt.from_np(a.dtype), kind="ExternalInput").ap())
    shape = inputs["x"].shape
    args.append(nc.dram_tensor("out_0_dram", shape, F32, kind="ExternalOutput").ap())
    build(nc, *args)
    r = run_bass_kernel_spmd(nc, [arrays], core_ids=[0])
    return r.results[0]["out_0_dram"]
```

```python
from contextlib import ExitStack

import numpy as np

import concourse.bass as bass
from concourse import mybir

P = 128
F32 = mybir.dt.float32
BF16 = mybir.dt.bfloat16
I32 = mybir.dt.int32
U32 = mybir.dt.uint32
ALU = mybir.AluOpType
ACT = mybir.ActivationFunctionType
AX = mybir.AxisListType

H = 16
WINDOW, GLOBAL = 32, 16
MASKED = -1e38
EPS = 1e-5
PARTS = 3


def build(nc, x, ctx_in, mask_in, g_xattn, g_ffn, wq, bq, wk, bk, wv, bv, wo, bo, gate_w, w1, w3, w2, out):
    B, S, D = x.shape
    E, _, F = w1.shape
    assert S == P and D == P
    DK = D // H
    T = B * S
    GB = 4
    NG = B // GB
    GT = GB * S
    FC = F // P
    SCALE = float(1.0 / np.sqrt(DK))
    ROWS_P = PARTS * (PARTS + 1) // 2 * DK
    ROWS_M = ROWS_P + PARTS
    ROWS_X = ROWS_M + PARTS
    HB = GB
    NB = H // HB
    VW = DK + 1
    NT = 2 * T // P + E
    CAP = T + P
    XW = D + 2
    X_IDX, X_GATE = D, D + 1
    RING = 6

    qk_d = nc.dram_tensor("qk_parts_scratch", (B // 2, 2 * PARTS, D, 2 * S), BF16, kind="Internal").ap()
    mask_d = nc.dram_tensor("mask_parts_scratch", (PARTS, T), BF16, kind="Internal").ap()
    rows_d = nc.dram_tensor("expert_rows_scratch", (E * CAP + E * P, XW), F32, kind="Internal").ap()
    acc_d = nc.dram_tensor("result_scratch", (T + P, D), F32, kind="Internal").ap()

    with ExitStack() as stack:
        def sb(name, shape, dt=F32):
            return stack.enter_context(nc.sbuf_tensor(name, shape, dt))

        def sem(name):
            return stack.enter_context(nc.semaphore(name))

        ps1 = stack.enter_context(nc.psum_tensor("ps_max_scores", [P, 2, 512], F32))
        ps2 = stack.enter_context(nc.psum_tensor("ps_scores", [P, NB, 512], F32))
        psm = stack.enter_context(nc.psum_tensor("ps_values", [P, 512], F32))
        psy = stack.enter_context(nc.psum_tensor("ps_out", [P, 512], F32))

        early = ExitStack()

        def sb_early(name, shape, dt=F32):
            return early.enter_context(nc.sbuf_tensor(name, shape, dt))

        stats = sb_early("stats", [P, B, 6])
        mv = sb_early("mv", [P, B, 2])
        rstd = sb_early("rstd", [P, B])
        cg = sb_early("cg", [P, 2, GB, D])
        xn = sb_early("xn", [P, 2, GB, D])
        xnT = sb_early("xnT", [P, 2, GT])
        ctxT = sb_early("ctxT", [P, 2, GT])
        qkf = sb_early("qkf", [P, 2, 2, GT])
        parts = sb_early("parts", [P, 2, 2 * PARTS, GT], BF16)
        early.close()
        w1_sb = sb("w1_sb", [P, E, F])
        w3_sb = sb("w3_sb", [P, E, F])
        w2_sb = sb("w2_sb", [P, E, FC, D])
        ident = sb("ident", [P, P])
        ident_b = sb("ident_b", [P, P], BF16)
        wmask = sb("wmask", [P, HB, P], BF16)
        tri = sb("tri", [P, P], BF16)
        ones_b = sb("ones_b", [P, P], BF16)
        iota_e = sb("iota_e", [P, E])
        cap_e = sb("cap_e", [P, E])
        iota_t = sb("iota_t", [P, NT])
        ones_s = sb("ones_s", [P, E])
        minus_half = sb("minus_half", [P, GB])
        fill = sb("fill", [P, XW])
        xs = sb("xs", [P, B, D])
        w_sb = {n: sb(f"w_{n}", [P, D]) for n in ("q", "k", "v", "o")}
        w_by_dim = {n: sb(f"w_by_dim_{n}", [P, D]) for n in ("q", "k")}
        gate_sb = sb("gate_sb", [P, E])
        bq_col = sb("bq_col", [P, 1])
        bqs_col = sb("bqs_col", [P, 1])
        bk_col = sb("bk_col", [P, 1])
        bv_row = sb("bv_row", [P, D])
        bo_row = sb("bo_row", [P, D])
        gates = sb("gates", [P, 2])
        tg = sb("tg", [P, 2])
        mrow = sb("mrow", [B, S])
        mres = sb("mres", [B, S])
        mpart = sb("mpart", [B, PARTS, S], BF16)
        va = sb("va", [P, B, H, VW])
        qs = [sb(f"qs{u}", [P, H, GT], BF16) for u in range(2)]
        ks = [sb(f"ks{u}", [P, H, GT], BF16) for u in range(2)]
        pT = sb("pT", [P, H, S])
        npart = sb("npart", [P, P // H, H], BF16)
        oh_sum = sb("oh_sum", [P, E], BF16)
        idx_f = sb("idx_f", [P, GB])

        XCH = 4
        x_loaded = [sem(f"x_loaded{i}") for i in range(XCH)]
        proj_loaded = sem("proj_loaded")
        by_dim_ready = sem("by_dim_ready")
        small_loaded = sem("small_loaded")
        w_loaded = sem("w_loaded")
        ctx_loaded = [sem(f"ctx_loaded{u}") for u in range(2)]
        ident_ready = sem("ident_ready")
        pool_step = sem("pool_step")
        ones_ready = sem("ones_ready")
        dve_step = sem("dve_step")
        var_ready = sem("var_ready")
        std_ready = sem("std_ready")
        gates_ready = sem("gates_ready")
        xn_written = sem("xn_written")
        xn_turned = sem("xn_turned")
        ctx_turned = sem("ctx_turned")
        turned_copied = sem("turned_copied")
        qk_done = sem("qk_done")
        qk_copied = sem("qk_copied")
        v_done = sem("v_done")
        v_copied = sem("v_copied")
        split1 = sem("split1")
        parts_ready = sem("parts_ready")
        parts_stored = [sem(f"parts_stored{u}") for u in range(2)]
        mpart_ready = sem("mpart_ready")
        mpart_stored = sem("mpart_stored")
        fill_ready = sem("fill_ready")
        fill_stored = sem("fill_stored")
        res_ready = sem("res_ready")
        var_stats = sem("var_stats")
        PROJ = 3 + 2
        SMALL = 7
        ctx_v = ctx_in.rearrange("b s d -> s b d")
        STEADY = (NG - 2) // 2
        SLOTS = 2 * GB // 2
        LOADS = PARTS * 2 + 1
        qk_loaded = [sem(f"qk_loaded{n}") for n in range(SLOTS)]

        def load_pair(sp, half, slot):
            u, col = slot // 2, slot % 2 * 2 * S
            tokens = bass.ds(half * (2 * S), 2 * S)
            first = 0
            for n in range(PARTS, 0, -1):
                slots = slice(first * DK, (first + n) * DK)
                for tile, units in ((qs, slice(0, n)), (ks, slice(2 * PARTS - n, 2 * PARTS))):
                    sp.dma_start(tile[u][slots, :, col:col + 2 * S],
                                 qk_d[bass.ds(half, 1), units].rearrange("n u (d h) t -> (n u d) h t", d=DK))\
                        .then_inc(qk_loaded[slot], 16)
                first += n
            sp.dma_start(ks[u][ROWS_P:ROWS_M, :, col:col + 2 * S],
                         mask_d[:, tokens].unsqueeze(1).to_broadcast([PARTS, H, 2 * S])).then_inc(qk_loaded[slot], 16)

        def part(u, n):
            return parts[:, u, n:2 * PARTS - n:2 * PARTS - 1 - 2 * n]

        def project_sync(sp):
            x_v = x.rearrange("b s d -> s b d")
            for i in range(XCH):
                n = B // XCH
                sp.dma_start(xs[:, i * n:(i + 1) * n], x_v[:, i * n:(i + 1) * n]).then_inc(x_loaded[i], 16)
                if i == 0:
                    for u in range(2):
                        sp.dma_start(cg[:, u], ctx_v[:, u * GB:(u + 1) * GB]).then_inc(ctx_loaded[u], 16)

            def store_parts(g, u):
                sp.wait_ge(parts_ready, g + 1)
                for i in range(GB // 2):
                    sp.dma_start(qk_d[bass.ds(g * (GB // 2) + i, 1)].rearrange("n u p t -> p (n u) t"),
                                 parts[:, u, :, i * 2 * S:(i + 1) * 2 * S]).then_inc(parts_stored[u], 16)

            with sp.Fori(0, STEADY) as it:
                for u in range(2):
                    store_parts(it * 2 + u, u)
            sp.wait_ge(ones_ready, 5)
            sp.wait_ge(mpart_stored, 16)
            for u in range(2):
                sp.wait_ge(parts_stored[u], 16 * (GB // 2))
            load_pair(sp, 0, 0)
            load_pair(sp, 1, 1)
            store_parts(NG - 2, 0)
            load_pair(sp, 2, 2)
            store_parts(NG - 1, 1)
            load_pair(sp, 3, 3)

        def project_gpsimd(pool):
            pool.memset(ident[:], 0.0).then_inc(pool_step, 1)
            pool.memset(ident_b[:], 0.0).then_inc(pool_step, 1)
            pool.wait_ge(pool_step, 2)
            for m in (ident, ident_b):
                pool.affine_select(out=m[:], in_=m[:], compare_op=ALU.not_equal, fill=1.0, base=0,
                                   pattern=[[-1, P]], channel_multiplier=1).then_inc(ident_ready, 1)
            pool.wait_ge(proj_loaded, 16 * PROJ)
            for n in ("q", "k"):
                pool.tensor_copy(w_by_dim[n][:], w_sb[n][:].rearrange("p (h d) -> p d h", d=DK))\
                    .then_inc(by_dim_ready, 1)
            pool.memset(va[:, :, :, DK:VW], 1.0).then_inc(ones_ready, 1)
            pool.memset(wmask[:], 0.0).then_inc(pool_step, 1)
            pool.memset(tri[:], 1.0).then_inc(pool_step, 1)
            pool.memset(ones_b[:], 1.0)
            pool.memset(ones_s[:], 1.0)
            pool.memset(minus_half[:], -0.5)
            pool.memset(npart[:], 0.0)
            pool.memset(oh_sum[:], 0.0)
            pool.memset(fill[:], 0.0).then_inc(pool_step, 1)
            pool.wait_ge(pool_step, 5)
            pool.iota(fill[:].bitcast(U32)[:, X_IDX:X_IDX + 1], [[0, 1]], base=T, channel_multiplier=1)\
                .then_inc(fill_ready, 1)
            pool.affine_select(out=tri[:], in_=tri[:], compare_op=ALU.is_gt, fill=0.0, base=0,
                               pattern=[[1, P]], channel_multiplier=-1)
            pool.affine_select(out=wmask[:], in_=wmask[:], compare_op=ALU.is_ge, fill=MASKED, base=WINDOW,
                               pattern=[[0, HB], [1, P]], channel_multiplier=-1).then_inc(pool_step, 1)
            pool.wait_ge(pool_step, 6)
            pool.affine_select(out=wmask[:], in_=wmask[:], compare_op=ALU.is_ge, fill=MASKED, base=WINDOW,
                               pattern=[[0, HB], [-1, P]], channel_multiplier=1).then_inc(pool_step, 1)
            pool.wait_ge(pool_step, 7)
            pool.affine_select(out=wmask[:], in_=wmask[:], compare_op=ALU.is_ge, fill=0.0, base=-GLOBAL,
                               pattern=[[0, HB], [0, P]], channel_multiplier=1).then_inc(pool_step, 1)
            pool.wait_ge(pool_step, 8)
            pool.affine_select(out=wmask[:], in_=wmask[:], compare_op=ALU.is_ge, fill=0.0, base=-GLOBAL,
                               pattern=[[0, HB], [1, P]], channel_multiplier=0)
            for t, pattern, base, mult in ((iota_e, [[1, E]], 0, 0), (cap_e, [[CAP, E]], 0, 0),
                                           (iota_t, [[1, NT]], 0, 0), (idx_f, [[S, GB]], 0, 1)):
                pool.iota(t[:], pattern, base=base, channel_multiplier=mult, allow_small_or_imprecise_dtypes=True)
            pool.wait_ge(ones_ready, 1)
            pool.wait_ge(fill_ready, 1)
            pool.drain()
            for value, tiles in ((1.0, qs), (-1.0, ks)):
                two = int(np.float32(value).view(np.uint32)) >> 16
                two = float(np.uint32(two << 16 | two).view(np.float32))
                for t in tiles:
                    pool.memset(t[32:64].bitcast(F32), two).then_inc(ones_ready, 1)
            pool.wait_ge(ones_ready, 5)
            with pool.Fori(0, NG // 2) as it:
                for u in range(2):
                    pool.wait_ge(split1, (it * 2 + u) * 2 + 2)
                    pool.tensor_tensor(part(u, 2), qkf[:, u], part(u, 1), ALU.subtract)\
                        .then_inc(parts_ready, 1)

        def project_scalar(act):
            for n, src in (("q", wq), ("k", wk), ("v", wv)):
                act.dma_start(w_sb[n][:], src).then_inc(proj_loaded, 16)
            act.dma_start(bq_col[:], bq.rearrange("(h d a) -> d h a", d=DK, a=1), allow_slow_non_contiguous=True)\
                .then_inc(proj_loaded, 16)
            act.dma_start(bk_col[:], bk.rearrange("(h d a) -> d h a", d=DK, a=1), allow_slow_non_contiguous=True)\
                .then_inc(proj_loaded, 16)

            def std(i):
                n = B // XCH
                act.wait_ge(var_ready, i + 1)
                nc.scalar.activation(rstd[:, i * n:(i + 1) * n], mv[:, i * n:(i + 1) * n, 1], ACT.Sqrt)\
                    .then_inc(std_ready, 1)

            std(0)
            act.dma_start(bv_row[:], bv.partition_broadcast(P)).then_inc(small_loaded, 16)
            act.dma_start(w_sb["o"][:], wo).then_inc(small_loaded, 16)
            act.dma_start(bo_row[:], bo.partition_broadcast(P)).then_inc(small_loaded, 16)
            act.dma_start(mrow[:], mask_in).then_inc(small_loaded, 16)
            act.dma_start(gates[:, 0:1], g_xattn.partition_broadcast(P)).then_inc(small_loaded, 16)
            act.dma_start(gates[:, 1:2], g_ffn.partition_broadcast(P)).then_inc(small_loaded, 16)
            act.dma_start(gate_sb[:], gate_w).then_inc(small_loaded, 16)
            act.wait_ge(proj_loaded, 16 * PROJ)
            nc.scalar.mul(bqs_col[:], bq_col[:], SCALE).then_inc(gates_ready, 1)

            def copy_turned(g, u):
                act.wait_ge(xn_turned, g + 1)
                nc.scalar.copy(xnT[:, u], ps2[:, 0]).then_inc(turned_copied, 1)
                act.wait_ge(ctx_turned, g + 1)
                nc.scalar.copy(ctxT[:, u], ps2[:, 1]).then_inc(turned_copied, 1)

            def bias(g, u, half):
                act.wait_ge(qk_done, g + 1)
                if not (isinstance(half, int) and half == 0):
                    act.wait_ge(parts_stored[u], half * (16 * (GB // 2)))
                for s, (b, scale) in enumerate(((bqs_col, SCALE), (bk_col, 1.0))):
                    nc.scalar.activation(qkf[:, u, s], ps2[:, 2 + s], ACT.Identity, bias=b[:, 0:1], scale=scale)
                    ins = nc.scalar.activation(parts[:, u, (0, 2 * PARTS - 1)[s]], ps2[:, 2 + s], ACT.Identity,
                                               bias=b[:, 0:1], scale=scale)
                ins.then_inc(qk_copied, 1)

            act.wait_ge(gates_ready, 1)
            def load_ctx(g, u):
                act.dma_start(cg[:, u], ctx_v[:, bass.ds((g + 2) * GB, GB)]).then_inc(ctx_loaded[u], 16)

            copy_turned(0, 0)
            load_ctx(0, 0)
            std(1)
            copy_turned(1, 1)
            load_ctx(1, 1)
            bias(0, 0, 0)
            std(2)
            copy_turned(2, 0)
            bias(1, 1, 0)
            std(3)
            act.wait_ge(small_loaded, 16 * SMALL)
            nc.scalar.activation(tg[:], gates[:], ACT.Tanh).then_inc(gates_ready, 1)
            act.wait_ge(mpart_ready, 1)
            act.dma_start(mask_d.rearrange("a (b s) -> b a s", s=S), mpart[:]).then_inc(mpart_stored, 16)
            with act.Fori(1, STEADY) as it:
                for u in range(2):
                    g = it * 2 + u
                    load_ctx(g, u)
                    copy_turned(g + 1, 1 - u)
                    bias(g, u, it)
            copy_turned(NG - 1, 1)
            bias(NG - 2, 0, NG // 2 - 1)
            bias(NG - 1, 1, NG // 2 - 1)

        def project_vector(dve):
            steps = [0]

            def then_wait(ins):
                steps[0] += 1
                ins.then_inc(dve_step, 1)
                dve.wait_ge(dve_step, steps[0])

            def statistics(i):
                n = B // XCH
                dve.wait_ge(x_loaded[i], 16)
                for b in range(i * n, (i + 1) * n):
                    nc.vector.bn_stats(stats[:, b], xs[:, b]).then_inc(var_stats, 1)
                dve.wait_ge(var_stats, (2 * i + 1) * n)
                for b in range(i * n, (i + 1) * n):
                    nc.vector.bn_aggr(mv[:, b], stats[:, b]).then_inc(var_stats, 1)
                dve.wait_ge(var_stats, (2 * i + 2) * n)
                nc.vector.tensor_scalar(mv[:, i * n:(i + 1) * n, 1], mv[:, i * n:(i + 1) * n, 1], EPS, None,
                                        ALU.add).then_inc(var_ready, 1)

            def invert(i):
                n = B // XCH
                dve.wait_ge(std_ready, i + 1)
                then_wait(nc.vector.reciprocal(rstd[:, i * n:(i + 1) * n], rstd[:, i * n:(i + 1) * n]))

            def normalise(g, u):
                if not (isinstance(g, int) and g < 2):
                    dve.wait_ge(xn_turned, g - 1)
                for j in range(GB):
                    b = g * GB + j
                    nc.vector.tensor_scalar(xn[:, u, j], xs[:, b], mv[:, b, 0:1], rstd[:, bass.ds(b, 1)],
                                            ALU.subtract, ALU.mult).then_inc(xn_written, 1)

            def bias_v(g):
                dve.wait_ge(v_done, g + 1)
                nc.vector.tensor_tensor(
                    va[:, bass.ds(g * GB, GB), :, 0:DK].rearrange("p b h d -> p (b h) d"),
                    ps1[:, 0].rearrange("p (c d) -> p c d", d=DK),
                    bv_row[:].unsqueeze(1).to_broadcast([P, GB, D]).rearrange("p b (h d) -> p b h d", h=H),
                    ALU.add).then_inc(v_copied, 1)

            def split(g, u):
                dve.wait_ge(qk_copied, g + 1)
                nc.vector.tensor_tensor(qkf[:, u], qkf[:, u], part(u, 0), ALU.subtract).then_inc(split1, 1)
                dve.wait_ge(split1, g * 2 + 1)
                nc.vector.tensor_copy(part(u, 1), qkf[:, u]).then_inc(split1, 1)

            statistics(0)
            statistics(1)
            invert(0)
            assert XCH * 2 == NG
            normalise(0, 0)
            normalise(1, 1)
            invert(1)
            dve.wait_ge(ones_ready, 1)
            dve.wait_ge(small_loaded, 16 * SMALL)
            for g in range(2):
                normalise(g + 2, g)
                bias_v(g)
                split(g, g)
                statistics(g + 2)
            then_wait(nc.vector.tensor_copy(mpart[:, 0], mrow[:]))
            then_wait(nc.vector.tensor_tensor(mres[:], mrow[:], mpart[:, 0], ALU.subtract))
            then_wait(nc.vector.tensor_copy(mpart[:, 1], mres[:]))
            nc.vector.tensor_tensor(mpart[:, 2], mres[:], mpart[:, 1], ALU.subtract).then_inc(mpart_ready, 1)
            for i in range(2, XCH):
                invert(i)
            with dve.Fori(1, STEADY) as it:
                for u in range(2):
                    g = it * 2 + u
                    normalise(g + 2, u)
                    bias_v(g)
                    split(g, u)
            for g in range(NG - 2, NG):
                bias_v(g)
                split(g, g % 2)

        def project_tensor(pe):

            def turn(g, u, half):
                pe.wait_ge(xn_written, (g + 1) * GB)
                if not (isinstance(g, int) and g == 0):
                    pe.wait_ge(turned_copied, g * 2)
                for j in range(GB):
                    ins = nc.tensor.transpose(ps2[:, 0, j * P:(j + 1) * P], xn[:, u, j], ident[:])
                ins.then_inc(xn_turned, 1)
                pe.wait_ge(ctx_loaded[u], half * 16 + 16)
                for j in range(GB):
                    ins = nc.tensor.transpose(ps2[:, 1, j * P:(j + 1) * P], cg[:, u, j], ident[:])
                ins.then_inc(ctx_turned, 1)

            def project(g, u):
                pe.wait_ge(turned_copied, g * 2 + 2)
                if not (isinstance(g, int) and g == 0):
                    pe.wait_ge(qk_copied, g)
                nc.tensor.matmul(ps2[:, 2], w_by_dim["q"][:], xnT[:, u], start=True, stop=True)
                nc.tensor.matmul(ps2[:, 3], w_by_dim["k"][:], ctxT[:, u], start=True, stop=True).then_inc(qk_done, 1)
                if not (isinstance(g, int) and g == 0):
                    pe.wait_ge(v_copied, g)
                for j in range(GB):
                    ins = nc.tensor.matmul(ps1[:, 0, j * P:(j + 1) * P], ctxT[:, u, j * P:(j + 1) * P],
                                           w_sb["v"][:], start=True, stop=True)
                ins.then_inc(v_done, 1)

            pe.wait_ge(ident_ready, 2)
            pe.wait_ge(proj_loaded, 16 * PROJ)
            pe.wait_ge(by_dim_ready, 2)
            turn(0, 0, 0)
            turn(1, 1, 0)
            project(0, 0)
            turn(2, 0, 1)
            project(1, 1)
            with pe.Fori(1, STEADY) as it:
                for u in range(2):
                    g = it * 2 + u
                    turn(g + 1, 1 - u, it + u)
                    project(g, u)
            turn(NG - 1, 1, NG // 2 - 1)
            project(NG - 2, 0)
            project(NG - 1, 1)
        rmax = sb("rmax", [P, H])
        nmax = sb("nmax", [P, H])
        npT = sb("npT", [PARTS * H, 2, S], BF16)
        vst = sb("vst", [P, 2, H, VW])
        oT = sb("oT", [P, HB * P])
        rden = sb("rden", [P, H])
        attn = sb("attn", [P, H, DK])
        attnT = sb("attnT", [P, S])
        st2 = sb("st2", [P, GB, 6])
        mv2 = sb("mv2", [P, GB, 2])
        rstd2 = sb("rstd2", [P, GB])
        shift2 = sb("shift2", [P, GB])
        xr = sb("xr", [P, 2, 2, GB, XW])
        xr_u = xr[:].bitcast(U32)
        xrT = sb("xrT", [P, GT])
        lg = sb("lg", [P, GB, E])
        tmp = sb("tmp", [P, 2, GB, E])
        oh = sb("oh", [P, 2, GB, E])
        ohb = sb("ohb", [P, GB, E], BF16)
        rank = sb("rank", [P, GB, E])
        top = sb("top", [P, GB, 8])
        top_e = sb("top_e", [P, GB, 8], U32)
        ed = sb("ed", [P, GB])
        ed1 = sb("ed1", [P, GB])
        new_oh = sb("new_oh", [P, E])
        posf = sb("posf", [P, 2, GB])
        pos = sb("pos", [P, 2, 2, GB], U32)

        max_scored = sem("max_scored")
        max_taken = sem("max_taken")
        npart_ready = sem("npart_ready")
        npart_turned = sem("npart_turned")
        npT_ready = sem("npT_ready")
        nmax_loaded = [sem(f"nmax_loaded{u}") for u in range(2)]
        pool_b = sem("pool_b")
        scored = sem("scored")
        exp_done = sem("exp_done")
        vst_ready = sem("vst_ready")
        pv_done = sem("pv_done")
        oT_ready = sem("oT_ready")
        o_turned = sem("o_turned")
        rden_ready = sem("rden_ready")
        bias_added = sem("bias_added")
        attn_ready = sem("attn_ready")
        attn_turned = sem("attn_turned")
        attnT_ready = sem("attnT_ready")
        out_done = sem("out_done")
        res_done = sem("res_done")
        res_stored = sem("res_stored")
        zeroed = sem("zeroed")
        wait_passed = [sem(f"wait_passed{e}") for e in range(2)]
        r_stats = sem("r_stats")
        r_std = sem("r_std")
        r_pool = sem("r_pool")
        xr_ready = sem("xr_ready")
        xr_copied = sem("xr_copied")
        xr_turned = sem("xr_turned")
        xrT_ready = sem("xrT_ready")
        logits_done = sem("logits_done")
        logits_taken = sem("logits_taken")
        r_mean = sem("r_mean")
        choice_step = sem("choice_step")
        gate_step = sem("gate_step")
        place_step = sem("place_step")
        gap_ready = sem("gap_ready")
        odds_ready = sem("odds_ready")
        oh_ready = sem("oh_ready")
        ranked = sem("ranked")
        rank_taken = sem("rank_taken")
        oh_summed = sem("oh_summed")
        gates_written = sem("gates_written")
        pos_ready = sem("pos_ready")
        rows_ready = sem("rows_ready")
        scattered = [sem(f"scattered{u}") for u in range(2)]

        AHEAD = 2
        UNROLL = 2 * GB
        LOOPS = B // UNROLL - 2
        ps_np = ps1[:, 0, 0:S // 2].bitcast(BF16)
        ps_l = ps1[:, 1, 0:GB * E]
        ps_aT = psy[:, 0:P]
        ps_y = psy[:, P:2 * P]
        QW = P // HB
        ps_on = psm[:].rearrange("p (h v) -> p h v", v=QW)

        class At:
            def __init__(self, it, c):
                self.it, self.c = it, c
                self.b = it * UNROLL + c
                self.g = it * (UNROLL // GB) + c // GB
                self.j = c % GB
                self.u = (c // GB) % 2
                self.half = it * (UNROLL // 2) + c // 2
                self.slot = c // 2 % SLOTS
                self.turn = it * (UNROLL // 2 // SLOTS) + c // 2 // SLOTS
                self.known = isinstance(it, int)

            def plus(self, n):
                return At(self.it, self.c + n)

            def exists(self):
                return not self.known or 0 <= self.b < B

            def is_past(self, n):
                return not self.known or self.b >= n

        def batches(eng, step):
            for c in range(UNROLL):
                step(At(0, c))
            with eng.Fori(1, 1 + LOOPS) as it:
                for c in range(UNROLL):
                    step(At(it, c))
            for c in range(UNROLL):
                step(At(B // UNROLL - 1, c))

        class Group:
            def __init__(self, at, less):
                self.g = at.g - less
                self.u = (at.c // GB - less) % 2
                self.half = at.it * (UNROLL // GB // 2) + (at.c // GB - less) // 2
                self.known = at.known

            def exists(self):
                return not self.known or 0 <= self.g < NG

            def is_past(self, n):
                return not self.known or self.g >= n

        def route(at, phase):
            g = Group(at, 2 if phase == 4 else 1)
            return g if at.j == phase % GB and g.exists() else None

        def stand_alone(eng):
            eng.sem_inc(wait_passed[eng is nc.gpsimd], 1)

        def last_steps(step):
            for c in range(UNROLL, UNROLL + GB + 1):
                step(At(B // UNROLL - 1, c))

        def attend_sync(sp):
            def load_max(at):
                sp.wait_ge(npT_ready, at.b + 1)
                sp.dma_start(qs[at.u][ROWS_M:ROWS_X, :, at.j * S:(at.j + 1) * S], npT[:, at.c % 2])\
                    .then_inc(nmax_loaded[at.c % 2], 16)

            def store_res(g):
                sp.wait_ge(res_done, (g + 1) * GB)
                sp.dma_start(acc_d[0:T].rearrange("(b s) d -> s b d", s=S)[:, bass.ds(g * GB, GB)],
                             xs[:, bass.ds(g * GB, GB)]).then_inc(res_stored, 16)

            def step(at):
                if at.plus(1).exists():
                    load_max(at.plus(1))
                pair = at.plus(UNROLL - 2)
                if at.c % 2 == 0 and at.is_past(2) and pair.exists():
                    sp.wait_ge(scored, at.b * NB)
                    load_pair(sp, pair.half, pair.slot)
                if at.known and at.b == 2:
                    for u in range(2):
                        sp.wait_ge(parts_stored[u], 16 * (GB // 2) * (NG // 2))
                    sp.wait_ge(v_copied, NG)
                if at.known and 2 <= at.b < 2 + E // 2:
                    for e in range(2 * (at.b - 2), 2 * (at.b - 1)):
                        sp.dma_start(w1_sb[:, e], w1[e]).then_inc(w_loaded, 16)
                        sp.dma_start(w3_sb[:, e], w3[e]).then_inc(w_loaded, 16)
                        sp.dma_start(w2_sb[:, e], w2[e].rearrange("(c f) d -> f c d", f=P)).then_inc(w_loaded, 16)
                if at.known and at.b == UNROLL - 1:
                    for e in range(E):
                        sp.dma_start(rows_d[E * CAP + e * P:E * CAP + (e + 1) * P], fill[:]).then_inc(fill_stored, 16)
                    sp.dma_start(acc_d[T:T + P], fill[:, 0:D]).then_inc(fill_stored, 16)
                if at.j == 2 and at.is_past(GB):
                    store_res(at.g - 1)

            load_max(At(0, 0))
            batches(sp, step)
            store_res(NG - 1)

        def attend_tensor(pe):
            window = wmask[:].rearrange("p h s -> p (h s)")

            def score_max(at, banks=range(NB)):
                col = at.j * S
                if at.c % 2 == 0 and 0 in banks:
                    pe.wait_ge(qk_loaded[at.slot], at.turn * (16 * LOADS) + 16 * LOADS)
                if at.is_past(1) and 0 in banks:
                    pe.wait_ge(npT_ready, at.b)
                for n in banks:
                    if n == 1 and at.is_past(AHEAD):
                        routed(at.plus(-AHEAD))
                    if at.is_past(1) or n >= 2:
                        pe.wait_ge(max_taken, at.b * NB + (n - 1))
                    bank = ps1[:, n % 2]
                    nc.tensor.matmul(bank, ident_b[:], window, start=True, stop=False)
                    for j in range(HB):
                        h = n * HB + j
                        ins = nc.tensor.matmul(bank[:, j * S:(j + 1) * S], qs[at.u][0:ROWS_M, h, col:col + S],
                                               ks[at.u][0:ROWS_M, h, col:col + S], start=False, stop=(j == HB - 1))
                    ins.then_inc(max_scored, 1)

            def routed(at):
                if (r := route(at.plus(-1), 2)):
                    pe.wait_ge(logits_taken, r.g + 1)
                if (r := route(at, 4)):
                    pe.wait_ge(rank_taken, r.g + 1)

            def turn_max(at):
                pe.wait_ge(npart_ready, at.b + 1)
                nc.tensor.transpose(ps_np, npart[:].rearrange("p a h -> p (a h)"), ident_b[:]).then_inc(npart_turned, 1)

            def score(at):
                col = at.j * S
                pe.wait_ge(nmax_loaded[at.c % 2], at.half * 16 + 16)
                if at.is_past(1):
                    pe.wait_ge(exp_done, at.b * 2)
                for n in range(NB):
                    bank = ps2[:, n]
                    nc.tensor.matmul(bank, ident_b[:], window, start=True, stop=False)
                    for j in range(HB):
                        h = n * HB + j
                        ins = nc.tensor.matmul(bank[:, j * S:(j + 1) * S], ks[at.u][0:ROWS_X, h, col:col + S],
                                               qs[at.u][0:ROWS_X, h, col:col + S], start=False, stop=(j == HB - 1))
                    ins.then_inc(scored, 1)

            def values(at, half):
                if half == 0:
                    pe.wait_ge(vst_ready, at.b + 1)
                    if at.is_past(1):
                        pe.wait_ge(attn_ready, at.b)
                pe.wait_ge(exp_done, at.b * 2 + (half + 1))
                for n in range(half * (NB // 2), (half + 1) * (NB // 2)):
                    for j in range(HB):
                        h = n * HB + j
                        ins = nc.tensor.matmul(psm[j * QW:j * QW + VW, n * P:(n + 1) * P], vst[:, at.c % 2, h],
                                               pT[:, h], start=True, stop=True)
                if half == 1:
                    ins.then_inc(pv_done, 1)

            def turn_values(at):
                pe.wait_ge(oT_ready, at.b + 1)
                for n in range(NB):
                    ins = nc.tensor.transpose(psm[:, n * P:(n + 1) * P], oT[:, n * P:(n + 1) * P], ident[:])
                ins.then_inc(o_turned, 1)

            def turn_attn(at):
                pe.wait_ge(attn_ready, at.b + 1)
                if at.is_past(1):
                    pe.wait_ge(res_done, at.b)
                nc.tensor.transpose(ps_aT, attn[:].rearrange("p h d -> p (h d)"), ident[:]).then_inc(attn_turned, 1)

            def project(at):
                pe.wait_ge(attnT_ready, at.b + 1)
                nc.tensor.matmul(ps_y, attnT[:], w_sb["o"][:], start=True, stop=True).then_inc(out_done, 1)

            def turn_rows(r):
                pe.wait_ge(xr_ready, (r.g + 1) * GB)
                for j in range(GB):
                    ins = nc.tensor.transpose(psy[:, j * P:(j + 1) * P], xr[:, r.u, 0, j, 0:D], ident[:])
                ins.then_inc(xr_turned, 1)

            def logits(r):
                pe.wait_ge(xrT_ready, r.g + 1)
                for j in range(GB):
                    ins = nc.tensor.matmul(ps_l[:, j * E:(j + 1) * E], xrT[:, j * P:(j + 1) * P], gate_sb[:],
                                           start=True, stop=True)
                ins.then_inc(logits_done, 1)

            def ranks(r):
                pe.wait_ge(oh_ready, r.g + 1)
                pe.wait_ge(oh_summed, r.g + 1)
                nc.tensor.matmul(ps_l, tri[:], ohb[:].rearrange("p b e -> p (b e)"), start=True, stop=False)
                for j in range(GB - 1):
                    n = GB - 1 - j
                    nc.tensor.matmul(ps_l[:, (j + 1) * E:].rearrange("p (b e) -> p b e", e=E), ones_b[:],
                                     ohb[:, j].unsqueeze(1).to_broadcast([P, n, E]), start=False, stop=False)
                nc.tensor.matmul(ps_l.rearrange("p (b e) -> p b e", e=E), ones_b[:],
                                 oh_sum[:].unsqueeze(1).to_broadcast([P, GB, E]), start=False, stop=True)\
                    .then_inc(ranked, 1)

            def step(at):
                last, ahead = at.plus(-1), at.plus(AHEAD)
                if at.exists():
                    score(at)
                if at.plus(1).exists():
                    turn_max(at.plus(1))
                if (r := route(last, 2)):
                    logits(r)
                if (r := route(at, 4)):
                    ranks(r)
                if at.is_past(1) and last.exists():
                    turn_values(last)
                if (r := route(at, 2)):
                    if at.plus(-2).exists():
                        pe.wait_ge(res_done, at.b - 1)
                    turn_rows(r)
                if ahead.exists():
                    score_max(ahead, range(0, 2))
                if at.exists():
                    values(at, 0)
                if ahead.exists():
                    score_max(ahead, range(2, 3))
                if at.is_past(1) and last.exists():
                    if (r := route(at, 2)):
                        pe.wait_ge(xrT_ready, r.g + 1)
                    turn_attn(last)
                if at.exists():
                    values(at, 1)
                if ahead.exists():
                    score_max(ahead, range(3, 4))
                if at.is_past(1) and last.exists():
                    project(last)

            pe.wait_ge(zeroed, 1)
            score_max(At(0, 0))
            turn_max(At(0, 0))
            score_max(At(0, 1))
            batches(pe, step)
            last_steps(step)

        def attend_scalar(act):
            def copy_max(at):
                act.wait_ge(npart_turned, at.b + 1)
                if at.is_past(2):
                    act.wait_ge(nmax_loaded[at.c % 2], at.half * 16)
                nc.scalar.copy(npT[:, at.c % 2], ps_np[0:PARTS * H]).then_inc(npT_ready, 1)

            def exps(at, n):
                act.wait_ge(scored, at.b * NB + (n + 1) * (NB // 2))
                if at.is_past(1):
                    act.wait_ge(pv_done, at.b)
                lo, hi = n * (NB // 2), (n + 1) * (NB // 2)
                nc.scalar.activation(pT[:, lo * HB:hi * HB].rearrange("p h s -> p (h s)"),
                                     ps2[:, lo:hi].rearrange("p n s -> p (n s)"), ACT.Exp).then_inc(exp_done, 1)

            def copy_values(at):
                act.wait_ge(pv_done, at.b + 1)
                nc.scalar.copy(oT[:], psm[:]).then_inc(oT_ready, 1)

            def copy_attn(at):
                act.wait_ge(attn_turned, at.b + 1)
                nc.scalar.copy(attnT[:], ps_aT).then_inc(attnT_ready, 1)

            def norm_rows(r):
                act.wait_ge(r_pool, r.g * 4 + 4)
                for j in range(GB):
                    nc.scalar.activation(xr[:, r.u, 0, j, 0:D], xs[:, r.g * GB + j], ACT.Identity,
                                         bias=shift2[:, j:j + 1], scale=rstd2[:, j:j + 1]).then_inc(xr_ready, 1)

            def copy_choice(r):
                act.wait_ge(xr_ready, (r.g + 1) * GB)
                nc.scalar.copy(xr[:, r.u, 1, :, 0:D], xr[:, r.u, 0, :, 0:D]).then_inc(xr_copied, 1)

            def copy_rows(r):
                act.wait_ge(xr_turned, r.g + 1)
                if r.is_past(1):
                    act.wait_ge(logits_done, r.g)
                nc.scalar.copy(xrT[:], psy[:]).then_inc(xrT_ready, 1)

            def odds(r):
                act.wait_ge(gap_ready, r.g + 1)
                nc.scalar.activation(ed[:], ed[:], ACT.Exp).then_inc(odds_ready, 1)

            def step(at):
                last, ahead = at.plus(-1), at.plus(AHEAD)
                if at.is_past(1) and last.exists():
                    copy_values(last)
                if at.exists():
                    exps(at, 0)
                if at.plus(1).exists():
                    copy_max(at.plus(1))
                if (r := route(at, 2)):
                    copy_rows(r)
                if (r := route(at, 4)):
                    odds(r)
                if at.exists():
                    exps(at, 1)
                if at.is_past(1) and last.exists():
                    copy_attn(last)
                if (r := route(at, 1)):
                    norm_rows(r)
                if (r := route(at, 2)):
                    copy_choice(r)

            copy_max(At(0, 0))
            batches(act, step)
            last_steps(step)

        def attend_vector(dve):
            def take_max(at):
                for n in range(NB):
                    dve.wait_ge(max_scored, at.b * NB + (n + 1))
                    if n == 0 and at.is_past(1):
                        dve.wait_ge(npart_ready, at.b)
                    nc.vector.tensor_reduce(rmax[:, n * HB:(n + 1) * HB],
                                            ps1[:, n % 2].rearrange("p (h s) -> p h s", h=HB),
                                            AX.X, ALU.max).then_inc(max_taken, 1)

            def residual(at):
                if at.j == 0:
                    dve.wait_ge(bias_added, at.g + 1)
                dve.wait_ge(out_done, at.b + 1)
                nc.vector.scalar_tensor_tensor(out=xs[:, at.b], in0=ps_y, scalar=tg[:, 0:1], in1=xs[:, at.b],
                                               op0=ALU.mult, op1=ALU.add).then_inc(res_done, 1)
                dve.wait_ge(res_done, at.b + 1)
                stand_alone(dve)
                nc.vector.bn_stats(st2[:, at.j], xs[:, at.b]).then_inc(r_stats, 1)

            def normalise(at):
                dve.wait_ge(o_turned, at.b + 1)
                nc.vector.reciprocal(rden[:], ps_on[:, :, DK]).then_inc(rden_ready, 1)
                dve.wait_ge(rden_ready, at.b + 1)
                nc.vector.tensor_tensor(attn[:], ps_on[:, :, 0:DK], rden[:].unsqueeze(2).to_broadcast([P, H, DK]),
                                        ALU.mult).then_inc(attn_ready, 1)

            gbe = [P, GB, E]
            kgbe = [P, 2, GB, E]

            class InARow:
                def __init__(self, done, r, count):
                    self.done, self.before, self.count, self.n = done, r.g * count, count, 0

                def __call__(self, ins):
                    self.n += 1
                    assert self.n <= self.count
                    ins.then_inc(self.done, 1)
                    dve.wait_ge(self.done, self.before + self.n)

            def route_mean(r):
                dve.wait_ge(r_stats, (r.g + 1) * GB)
                stand_alone(dve)
                for j in range(GB):
                    ins = nc.vector.bn_aggr(mv2[:, j], st2[:, j])
                ins.then_inc(r_mean, 1)

            def take_logits(r):
                dve.wait_ge(logits_done, r.g + 1)
                nc.vector.tensor_copy(lg[:].rearrange("p b e -> p (b e)"), ps_l).then_inc(logits_taken, 1)
                dve.wait_ge(logits_taken, r.g + 1)

            def choose(r):
                before = r.g * (2 * GB + 1)
                stand_alone(dve)
                for j in range(GB):
                    nc.vector.max(top[:, j], lg[:, j]).then_inc(choice_step, 1)
                dve.wait_ge(choice_step, before + GB)
                stand_alone(dve)
                for j in range(GB):
                    nc.vector.max_index(top_e[:, j], top[:, j], lg[:, j]).then_inc(choice_step, 1)
                nc.vector.tensor_tensor(ed[:], top[:, :, 1], top[:, :, 0], ALU.subtract).then_inc(gap_ready, 1)
                dve.wait_ge(choice_step, before + 2 * GB)
                nc.vector.tensor_tensor(oh[:], iota_e[:].unsqueeze(1).unsqueeze(1).to_broadcast(kgbe),
                                        top_e[:, :, 0:2].rearrange("p b k -> p k b").unsqueeze(3).to_broadcast(kgbe),
                                        ALU.is_equal).then_inc(choice_step, 1)
                dve.wait_ge(choice_step, before + 2 * GB + 1)
                nc.vector.tensor_tensor(ohb[:], oh[:, 0], oh[:, 1], ALU.add).then_inc(oh_ready, 1)

            def take_ranks(r):
                dve.wait_ge(ranked, r.g + 1)
                nc.vector.tensor_tensor(rank[:], ps_l.rearrange("p (b e) -> p b e", e=E),
                                        cap_e[:].unsqueeze(1).to_broadcast(gbe), ALU.add).then_inc(rank_taken, 1)
                dve.wait_ge(rank_taken, r.g + 1)

            def places(r):
                then_wait = InARow(place_step, r, 2)
                dve.wait_ge(odds_ready, r.g + 1)
                nc.vector.tensor_tensor(tmp[:], oh[:], rank[:].unsqueeze(1).to_broadcast(kgbe), ALU.mult)
                nc.vector.tensor_reduce(new_oh[:], ohb[:].rearrange("p b e -> p e b"), AX.X, ALU.add)
                then_wait(nc.vector.tensor_scalar(ed1[:], ed[:], 1.0, None, ALU.add))
                nc.vector.tensor_reduce(posf[:], tmp[:], AX.X, ALU.add)
                nc.vector.tensor_tensor(oh_sum[:], oh_sum[:], new_oh[:], ALU.add).then_inc(oh_summed, 1)
                then_wait(nc.vector.reciprocal(ed1[:], ed1[:]))
                nc.vector.tensor_copy(pos[:, r.u], posf[:]).then_inc(pos_ready, 1)
                nc.vector.tensor_scalar(xr[:, r.u, 0, :, X_GATE], ed1[:], tg[:, 1:2], None, ALU.mult)
                nc.vector.scalar_tensor_tensor(out=xr[:, r.u, 1, :, X_GATE], in0=ed1[:], scalar=tg[:, 1:2], in1=ed[:],
                                               op0=ALU.mult, op1=ALU.mult).then_inc(gates_written, 1)

            def step(at):
                last, ahead = at.plus(-1), at.plus(AHEAD)
                if at.is_past(2) and at.plus(-2).exists():
                    residual(at.plus(-2))
                if (r := route(at, 1)):
                    route_mean(r)
                if (r := route(last, 2)):
                    take_logits(r)
                if (r := route(at, 4)):
                    take_ranks(r)
                if at.is_past(1) and last.exists():
                    normalise(last)
                if ahead.exists():
                    take_max(ahead)
                if (r := route(last, 2)):
                    choose(r)
                if (r := route(at, 4)):
                    places(r)

            nc.vector.memset(psm[:], 0.0).then_inc(zeroed, 1)
            dve.sem_inc(oh_summed, 1)
            for c in range(AHEAD):
                take_max(At(0, c))
            batches(dve, step)
            last_steps(step)

        def attend_gpsimd(pool):
            POOL_B = 3

            def split_max(at):
                def then_wait(ins, n):
                    ins.then_inc(pool_b, 1)
                    pool.wait_ge(pool_b, at.b * POOL_B + n)
                    stand_alone(pool)

                pool.wait_ge(max_taken, at.b * NB + NB)
                if at.is_past(1):
                    pool.wait_ge(npart_turned, at.b)
                stand_alone(pool)
                then_wait(pool.tensor_copy(npart[:, 0], rmax[:]), 1)
                then_wait(pool.tensor_tensor(nmax[:], rmax[:], npart[:, 0], ALU.subtract), 2)
                then_wait(pool.tensor_copy(npart[:, 1], nmax[:]), 3)
                pool.tensor_tensor(npart[:, 2], nmax[:], npart[:, 1], ALU.subtract).then_inc(npart_ready, 1)

            def add_bias(g):
                rows = xs[:, bass.ds(g * GB, GB)]
                pool.tensor_tensor(rows, rows, bo_row[:].unsqueeze(1).to_broadcast([P, GB, D]), ALU.add)\
                    .then_inc(bias_added, 1)

            def copy_v(at):
                if at.is_past(2):
                    pool.wait_ge(pv_done, at.b - 1)
                stand_alone(pool)
                pool.tensor_copy(vst[:, at.c % 2], va[:, at.b]).then_inc(vst_ready, 1)

            def route_std(r):
                pool.wait_ge(r_mean, r.g + 1)
                stand_alone(pool)
                pool.tensor_scalar(rstd2[:], mv2[:, :, 1], EPS, 0.0, ALU.add, ALU.add).then_inc(r_pool, 1)
                pool.tensor_scalar(shift2[:], mv2[:, :, 0], -1.0, 0.0, ALU.mult, ALU.add).then_inc(r_pool, 1)
                pool.wait_ge(r_pool, r.g * 4 + 2)
                pool.tensor_tensor(rstd2[:], rstd2[:], minus_half[:], ALU.pow).then_inc(r_pool, 1)
                pool.wait_ge(r_pool, r.g * 4 + 3)
                pool.tensor_tensor(shift2[:], shift2[:], rstd2[:], ALU.mult).then_inc(r_pool, 1)

            def route_tokens(r):
                for k in range(2):
                    pool.tensor_copy(xr_u[:, r.u, k, :, X_IDX], idx_f[:]).then_inc(rows_ready, 1)
                pool.wait_ge(rows_ready, r.g * 3 + 2)
                stand_alone(pool)
                pool.tensor_scalar(idx_f[:], idx_f[:], float(GT), 0.0, ALU.add, ALU.add).then_inc(rows_ready, 1)
                pool.wait_ge(rows_ready, r.g * 3 + 3)
                stand_alone(pool)

            def scatter(r, j):
                if j == 0:
                    pool.wait_ge(pos_ready, r.g + 1)
                    pool.wait_ge(gates_written, r.g + 1)
                    pool.wait_ge(xr_copied, r.g + 1)
                    stand_alone(pool)
                for k in range(2):
                    pool.indirect_dma_start(
                        out=rows_d, out_offset=bass.IndirectOffsetOnAxis(ap=pos[:, r.u, k, j:j + 1], axis=0),
                        in_=xr[:, r.u, k, j], in_offset=None).then_inc(scattered[r.u], 16)

            def step(at):
                ahead = at.plus(AHEAD)
                sent = Group(at, 2)
                if (r := route(at, 1)):
                    route_std(r)
                if at.j in (1, 3) and sent.exists():
                    scatter(sent, at.j - 1)
                if ahead.exists():
                    split_max(ahead)
                if at.plus(1).exists():
                    copy_v(at.plus(1))
                if at.j in (1, 3) and sent.exists():
                    scatter(sent, at.j)
                if (r := route(at, 2)):
                    route_tokens(r)
                if at.j == 3 and (not at.known or at.g + 1 < NG):
                    add_bias(at.g + 1)
                if at.j == 3 and sent.exists():
                    pool.wait_ge(scattered[sent.u], sent.half * (2 * GB * 16) + 2 * GB * 16)
                    stand_alone(pool)

            pool.wait_ge(gates_ready, 2)
            pool.wait_ge(small_loaded, 16 * SMALL)
            pool.tensor_scalar(bo_row[:], bo_row[:], tg[:, 0:1], 0.0, ALU.mult, ALU.add).then_inc(pool_step, 1)
            pool.wait_ge(pool_step, 9)
            add_bias(0)
            for c in range(AHEAD):
                split_max(At(0, c))
            copy_v(At(0, 0))
            batches(pool, step)
            for c in range(UNROLL, UNROLL + 2 * GB):
                step(At(B // UNROLL - 1, c))
            for u in range(2):
                pool.wait_ge(scattered[u], NG // 2 * (2 * GB * 16))

        cnt = sb("cnt", [P, E])
        nt_f = sb("nt_f", [P, E])
        nt_i = sb("nt_i", [P, E], I32)
        nt_s = sb("nt_s", [P, E], I32)
        cum = sb("cum", [P, E])
        skip = sb("skip", [P, E])
        end_f = sb("end_f", [P, E])
        end_i = sb("end_i", [P, E], I32)
        past = sb("past", [P, NT, E])
        tile_f = sb("tile_f", [P, NT])
        tile_e = sb("tile_e", [P, NT], I32)
        tile_r = sb("tile_r", [P, NT], I32)
        plan_step = sem("plan_step")
        counted = sem("counted")
        planned = sem("planned")
        end_ready = sem("end_ready")
        tail_stored = sem("tail_stored")

        def plan_tensor(pe):
            pe.wait_ge(oh_summed, NG + 1)
            pe.wait_ge(res_done, B)
            pe.wait_ge(xrT_ready, NG)
            nc.tensor.matmul(psy[:, 0:E], ones_b[:], oh_sum[:], start=True, stop=True).then_inc(counted, 1)

        def plan_vector(dve):
            steps = [0]

            def then_wait(ins):
                steps[0] += 1
                ins.then_inc(plan_step, 1)
                dve.wait_ge(plan_step, steps[0])

            dve.wait_ge(counted, 1)
            then_wait(nc.vector.tensor_copy(cnt[:], psy[:, 0:E]))
            then_wait(nc.vector.tensor_tensor(end_f[:], cnt[:], cap_e[:], ALU.add))
            nc.vector.tensor_copy(end_i[:], end_f[:]).then_inc(end_ready, 1)
            then_wait(nc.vector.tensor_scalar(nt_f[:], cnt[:], float(P - 1), None, ALU.add))
            then_wait(nc.vector.tensor_copy(nt_i[:], nt_f[:]))
            then_wait(nc.vector.tensor_scalar(nt_s[:], nt_i[:], P.bit_length() - 1, None, ALU.arith_shift_right))
            then_wait(nc.vector.tensor_copy(nt_f[:], nt_s[:]))
            then_wait(nc.vector.tensor_tensor_scan(cum[:], ones_s[:], nt_f[:], 0.0, ALU.mult, ALU.add))
            then_wait(nc.vector.tensor_scalar(skip[:], nt_f[:], -float(P), float(CAP), ALU.mult, ALU.add))
            te = [P, NT, E]
            then_wait(nc.vector.tensor_tensor(past[:], iota_t[:].unsqueeze(2).to_broadcast(te),
                                              cum[:].unsqueeze(1).to_broadcast(te), ALU.is_ge))
            then_wait(nc.vector.tensor_reduce(tile_f[:], past[:], AX.X, ALU.add))
            then_wait(nc.vector.tensor_scalar(tile_f[:], tile_f[:], float(E - 1), float(F), ALU.min, ALU.mult))
            nc.vector.tensor_copy(tile_e[:], tile_f[:]).then_inc(planned, 1)
            then_wait(nc.vector.tensor_tensor(past[:], past[:], skip[:].unsqueeze(1).to_broadcast(te), ALU.mult))
            then_wait(nc.vector.tensor_reduce(tile_f[:], past[:], AX.X, ALU.add))
            then_wait(nc.vector.scalar_tensor_tensor(out=tile_f[:], in0=iota_t[:], scalar=float(P), in1=tile_f[:],
                                                     op0=ALU.mult, op1=ALU.add))
            nc.vector.tensor_copy(tile_r[:], tile_f[:]).then_inc(planned, 1)

        def plan_sync(sp):
            sp.wait_ge(end_ready, 1)
            for e in range(E):
                row = sp.value_load(end_i[0:1, e:e + 1], min_val=e * CAP, max_val=e * CAP + T)
                sp.dma_start(rows_d[bass.ds(row, P)], fill[:]).then_inc(tail_stored, 16)
            sp.wait_ge(tail_stored, 16 * E)
            sp.wait_ge(fill_stored, 16 * (E + 1))
            sp.wait_ge(res_stored, 16 * NG)

        xg = sb("xg", [P, RING, XW])
        xg_u = xg[:].bitcast(U32)
        xgT = sb("xgT", [P, P])
        act_s = sb("act_s", [P, F])
        hid = sb("hid", [P, F])
        hidT = sb("hidT", [P, FC, P])
        yt = sb("yt", [P, 2, D])
        xg_loaded = [sem(f"xg_loaded{u}") for u in range(RING)]
        xg_free = sem("xg_free")
        xg_turned = sem("xg_turned")
        xgT_ready = sem("xgT_ready")
        gate_done = sem("gate_done")
        up_done = sem("up_done")
        silu_done = sem("silu_done")
        hid_ready = sem("hid_ready")
        hid_turned = sem("hid_turned")
        hidT_ready = sem("hidT_ready")
        down_done = sem("down_done")
        yt_ready = sem("yt_ready")
        added = sem("added")
        out_stored = sem("out_stored")

        ps_a, ps_b = ps2[:, 0], ps2[:, 1]
        ps_h = ps2[:, 2]
        ps_x = psm[:, 0:P]
        ps_d = psy[:, 0:D]
        assert NT % RING == 0 and RING % 2 == 0

        def tiles(eng, step, lo, hi):
            turns = (hi - lo) // RING
            with eng.Fori(0, turns) as it:
                for c in range(lo, lo + RING):
                    step(it * RING + c, c % RING, it + c // RING)
            for t in range(lo + turns * RING, hi):
                step(t, t % RING, t // RING)

        def experts_sync(sp):
            def load(t, u, turn):
                row = sp.value_load(tile_r[0:1, bass.ds(t, 1)], min_val=0, max_val=E * CAP + (E - 1) * P)
                sp.wait_ge(xg_free, t + 1)
                sp.dma_start(xg[:, u], rows_d[bass.ds(row, P)]).then_inc(xg_loaded[u], 16)

            sp.wait_ge(planned, 2)
            for u in range(2):
                sp.wait_ge(scattered[u], NG // 2 * (2 * GB * 16))
            tiles(sp, load, 0, NT)
            sp.wait_ge(added, 16 * NT)
            for i in range(XCH):
                n = B // XCH
                sp.dma_start(out[i * n:(i + 1) * n].rearrange("b s d -> (b s) d"),
                             acc_d[i * n * S:(i + 1) * n * S]).then_inc(out_stored, 16)
            sp.wait_ge(out_stored, 16 * XCH)

        def experts_tensor(pe):
            def expert(t):
                return pe.value_load(tile_e[0:1, t:t + 1] if isinstance(t, int) else tile_e[0:1, bass.ds(t, 1)],
                                     min_val=0, max_val=(E - 1) * F)

            def turn_rows(t, u, turn):
                pe.wait_ge(xg_loaded[u], turn * 16 + 16)
                nc.tensor.transpose(ps_x, xg[:, u, 0:D], ident[:]).then_inc(xg_turned, 1)

            def up(t, at):
                pe.wait_ge(xgT_ready, t + 1)
                nc.tensor.matmul(ps_a, xgT[:], w1_sb[:].rearrange("p e f -> p (e f)")[:, bass.ds(at, F)],
                                 start=True, stop=True).then_inc(gate_done, 1)
                nc.tensor.matmul(ps_b, xgT[:], w3_sb[:].rearrange("p e f -> p (e f)")[:, bass.ds(at, F)],
                                 start=True, stop=True).then_inc(up_done, 1)

            def turn_hidden(t):
                pe.wait_ge(hid_ready, t + 1)
                for c in range(FC):
                    ins = nc.tensor.transpose(ps_h[:, c * P:(c + 1) * P], hid[:, c * P:(c + 1) * P], ident[:])
                ins.then_inc(hid_turned, 1)

            def down(t, at):
                pe.wait_ge(hidT_ready, t + 1)
                pe.wait_ge(yt_ready, t + 1)
                for c in range(FC):
                    ins = nc.tensor.matmul(ps_d, hidT[:, c],
                                           w2_sb[:].rearrange("p e c d -> p (e c d)")[:, bass.ds(at + c * D, D)],
                                           start=(c == 0), stop=(c == FC - 1))
                ins.then_inc(down_done, 1)

            def step(t, u, turn):
                before, own = expert(t - 1), expert(t)
                turn_hidden(t - 1)
                up(t, own)
                down(t - 1, before)
                c = u + 1
                turn_rows(t + 1, c % RING, turn + c // RING)

            pe.wait_ge(w_loaded, 48 * E)
            pe.wait_ge(planned, 2)
            pe.wait_ge(exp_done, 2 * B)
            pe.wait_ge(attn_ready, B)
            own = expert(0)
            turn_rows(0, 0, 0)
            up(0, own)
            turn_rows(1, 1, 0)
            tiles(pe, step, 1, NT - 1)
            before, own = expert(NT - 2), expert(NT - 1)
            turn_hidden(NT - 2)
            up(NT - 1, own)
            down(NT - 2, before)
            turn_hidden(NT - 1)
            down(NT - 1, own)

        def experts_scalar(act):
            def copy_rows(t):
                act.wait_ge(xg_turned, t + 1)
                nc.scalar.copy(xgT[:], ps_x).then_inc(xgT_ready, 1)

            def gate(t):
                act.wait_ge(gate_done, t + 1)
                nc.scalar.activation(act_s[:], ps_a, ACT.Silu).then_inc(silu_done, 1)

            def scale_out(t, u):
                act.wait_ge(down_done, t + 1)
                if not (isinstance(t, int) and t < 2):
                    act.wait_ge(added, (t - 1) * 16)
                nc.scalar.activation(yt[:, u % 2], ps_d, ACT.Copy, scale=xg[:, u, X_GATE:X_GATE + 1])\
                    .then_inc(yt_ready, 1)

            def step(t, u, turn):
                gate(t)
                if not (isinstance(t, int) and t == 0):
                    scale_out(t - 1, (u - 1) % RING)
                if not (isinstance(t, int) and t == NT - 1):
                    copy_rows(t + 1)

            act.sem_inc(yt_ready, 1)
            copy_rows(0)
            for t in range(RING):
                step(t, t, 0)
            with act.Fori(1, NT // RING - 1) as it:
                for u in range(RING):
                    step(it * RING + u, u, it)
            for u in range(RING):
                step(NT - RING + u, u, NT // RING - 1)
            scale_out(NT - 1, RING - 1)

        def experts_vector(dve):
            def gated(t):
                dve.wait_ge(silu_done, t + 1)
                dve.wait_ge(up_done, t + 1)
                nc.vector.tensor_tensor(hid[:], act_s[:], ps_b, ALU.mult).then_inc(hid_ready, 1)

            def copy_hidden(t):
                dve.wait_ge(hid_turned, t + 1)
                nc.vector.tensor_copy(hidT[:].rearrange("p c s -> p (c s)"), ps_h).then_inc(hidT_ready, 1)

            gated(0)
            with dve.Fori(0, NT - 1) as t:
                copy_hidden(t)
                gated(t + 1)
            copy_hidden(NT - 1)

        def experts_gpsimd(pool):
            def add(t, u, turn):
                pool.wait_ge(yt_ready, t + 2)
                if not (isinstance(t, int) and t == 0):
                    pool.wait_ge(added, t * 16)
                    pool.sem_inc(xg_free, 1)
                stand_alone(pool)
                pool.indirect_dma_start(
                    out=acc_d, out_offset=bass.IndirectOffsetOnAxis(ap=xg_u[:, u, X_IDX:X_IDX + 1], axis=0),
                    in_=yt[:, u % 2], in_offset=None, compute_op=ALU.add).then_inc(added, 16)

            pool.sem_inc(xg_free, RING)
            add(0, 0, 0)
            tiles(pool, add, 1, NT)

        with nc.Block() as block:
            @block.sync
            def _(sp):
                project_sync(sp)
                attend_sync(sp)
                plan_sync(sp)
                experts_sync(sp)

            @block.tensor
            def _(pe):
                project_tensor(pe)
                attend_tensor(pe)
                plan_tensor(pe)
                experts_tensor(pe)

            @block.scalar
            def _(act):
                project_scalar(act)
                attend_scalar(act)
                experts_scalar(act)

            @block.vector
            def _(dve):
                project_vector(dve)
                attend_vector(dve)
                plan_vector(dve)
                experts_vector(dve)

            @block.gpsimd
            def _(pool):
                project_gpsimd(pool)
                attend_gpsimd(pool)
                experts_gpsimd(pool)


_INS = ["x", "ctx_1024", "mask_BxS2_ff0", "g_xattn", "g_ffn", "L0_xattn_wq", "L0_xattn_bq", "L0_xattn_wk",
        "L0_xattn_bk", "L0_xattn_wv", "L0_xattn_bv", "L0_xattn_wo", "L0_xattn_bo", "L0_ffn_gate_w",
        "L0_ffn_w1", "L0_ffn_w3", "L0_ffn_w2"]


def kernel(**inputs):
    import concourse.bacc as bacc
    from concourse.bass_utils import run_bass_kernel_spmd

    nc = bacc.Bacc("TRN2", target_bir_lowering=False, num_devices=1)
    arrays, args = {}, []
    for name in _INS:
        a = np.ascontiguousarray(inputs[name])
        arrays[f"in_{name}_dram"] = a
        args.append(nc.dram_tensor(f"in_{name}_dram", a.shape, mybir.dt.from_np(a.dtype), kind="ExternalInput").ap())
    shape = inputs["x"].shape
    args.append(nc.dram_tensor("out_0_dram", shape, F32, kind="ExternalOutput").ap())
    build(nc, *args)
    r = run_bass_kernel_spmd(nc, [arrays], core_ids=[0])
    return r.results[0]["out_0_dram"]
```

```python
from contextlib import ExitStack

import numpy as np

import concourse.bass as bass
from concourse import mybir

P = 128
F32 = mybir.dt.float32
BF16 = mybir.dt.bfloat16
I32 = mybir.dt.int32
U32 = mybir.dt.uint32
ALU = mybir.AluOpType
ACT = mybir.ActivationFunctionType
AX = mybir.AxisListType

H = 16
WINDOW, GLOBAL = 32, 16
MASKED = -1e36
EPS = 1e-5
PARTS = 3
PBUF = 3


def build(nc, x, ctx_in, mask_in, g_xattn, g_ffn, wq, bq, wk, bk, wv, bv, wo, bo, gate_w, w1, w3, w2, out):
    B, S, D = x.shape
    E, _, F = w1.shape
    assert S == P and D == P
    DK = D // H
    T = B * S
    GB = 4
    NG = B // GB
    GT = GB * S
    FC = F // P
    SCALE = float(1.0 / np.sqrt(DK))
    QUART = S // 4
    ROWS_W = QUART + 1
    ROW_0 = 2 * ROWS_W
    ROWS_P = ROW_0 + PARTS * (PARTS + 1) // 2 * DK
    assert WINDOW == QUART and 2 * GLOBAL == QUART and 3 * QUART <= ROWS_P
    ROWS_M = ROWS_P + PARTS
    ROWS_X = ROWS_M + PARTS
    HB = GB
    NB = H // HB
    VW = DK + 1
    NT = 2 * T // P + E - 1
    CAP = T + P
    XW = D + 2
    X_IDX, X_GATE = D, D + 1
    EARLY = NG - 3
    SURE = -((E * (P - 1) - 2 * EARLY * GT) // P)
    RING = 12
    YRING = 4

    qk_d = nc.dram_tensor("qk_parts_scratch", (B // 2, 2 * PARTS, D, 2 * S), BF16, kind="Internal").ap()
    mask_d = nc.dram_tensor("mask_parts_scratch", (PARTS, T), BF16, kind="Internal").ap()
    rows_d = nc.dram_tensor("expert_rows_scratch", (E * CAP + E * P, XW), F32, kind="Internal").ap()
    y_d = nc.dram_tensor("choices_scratch", (2 * T + 2 * E * P, D), F32, kind="Internal").ap()

    with ExitStack() as stack:
        def sb(name, shape, dt=F32):
            return stack.enter_context(nc.sbuf_tensor(name, shape, dt))

        def sem(name):
            return stack.enter_context(nc.semaphore(name))

        ps1 = stack.enter_context(nc.psum_tensor("ps_max_scores", [P, 2, 512], F32))
        ps2 = stack.enter_context(nc.psum_tensor("ps_scores", [P, NB, 512], F32))
        psm = stack.enter_context(nc.psum_tensor("ps_values", [P, 512], F32))
        psy = stack.enter_context(nc.psum_tensor("ps_out", [P, 512], F32))

        early = ExitStack()

        def sb_early(name, shape, dt=F32):
            return early.enter_context(nc.sbuf_tensor(name, shape, dt))

        stats = sb_early("stats", [P, B, 6])
        mv = sb_early("mv", [P, B, 2])
        rstd = sb_early("rstd", [P, B])
        cg = sb_early("cg", [P, 2, GB, D])
        xn = sb_early("xn", [P, 2, GB, D])
        xnT = sb_early("xnT", [P, 2, GT])
        ctxT = sb_early("ctxT", [P, 2, GT])
        qkf = sb_early("qkf", [P, 2, 2, GT])
        parts = sb_early("parts", [P, PBUF, 2 * PARTS, GT], BF16)
        early.close()
        w13_sb = sb("w13_sb", [P, E, 2, F])
        w2_sb = sb("w2_sb", [P, E, FC, D])
        ident = sb("ident", [P, P])
        ident_b = sb("ident_b", [P, P], BF16)
        wmask = sb("wmask", [P, HB, 2 * QUART], BF16)
        signs = sb("signs", [PARTS, 2, GT], BF16)
        win = sb("win", [ROWS_W, 2, 2, GB, S], BF16)
        tri = sb("tri", [P, P], BF16)
        ones_b = sb("ones_b", [P, P], BF16)
        iota_e = sb("iota_e", [P, E])
        cap_e = sb("cap_e", [P, E])
        iota_t = sb("iota_t", [P, NT])
        ones_s = sb("ones_s", [P, 2 * E])
        to_next = sb("to_next", [P, 2 * E])
        starts = sb("starts", [P, 2 * E + 1])
        minus_half = sb("minus_half", [P, GB])
        fill = sb("fill", [P, 2 * E, XW])
        xs = sb("xs", [P, B, D])
        w_sb = {n: sb(f"w_{n}", [P, D]) for n in ("q", "k", "v", "o")}
        w_by_dim = {n: sb(f"w_by_dim_{n}", [P, D]) for n in ("q", "k")}
        gate_sb = sb("gate_sb", [P, E])
        bq_col = sb("bq_col", [P, 1])
        bqs_col = sb("bqs_col", [P, 1])
        bk_col = sb("bk_col", [P, 1])
        bv_row = sb("bv_row", [P, D])
        bo_row = sb("bo_row", [P, D])
        gates = sb("gates", [P, 2])
        tg = sb("tg", [P, 2])
        mrow = sb("mrow", [B, S])
        mres = sb("mres", [B, S])
        mpart = sb("mpart", [B, PARTS, S], BF16)
        va = sb("va", [P, B, H, VW])
        qs = [sb(f"qs{u}", [P, H, GT], BF16) for u in range(2)]
        ks = [sb(f"ks{u}", [P, H, GT], BF16) for u in range(2)]
        pT = sb("pT", [P, H, S])
        npart = sb("npart", [P, P // H, H], BF16)
        oh_sum = sb("oh_sum", [P, E], BF16)
        idx_f = sb("idx_f", [P, 2, GB])

        XCH = 4
        x_loaded = [sem(f"x_loaded{i}") for i in range(XCH)]
        proj_loaded = sem("proj_loaded")
        by_dim_ready = sem("by_dim_ready")
        small_loaded = sem("small_loaded")
        w_loaded = sem("w_loaded")
        ctx_loaded = [sem(f"ctx_loaded{u}") for u in range(2)]
        ident_ready = sem("ident_ready")
        pool_step = sem("pool_step")
        ones_ready = sem("ones_ready")
        dve_step = sem("dve_step")
        var_ready = sem("var_ready")
        std_ready = sem("std_ready")
        gates_ready = sem("gates_ready")
        xn_written = sem("xn_written")
        xn_turned = sem("xn_turned")
        ctx_turned = sem("ctx_turned")
        turned_copied = sem("turned_copied")
        qk_done = sem("qk_done")
        qk_copied = sem("qk_copied")
        v_done = sem("v_done")
        v_copied = sem("v_copied")
        split1 = sem("split1")
        parts_ready = sem("parts_ready")
        parts_stored = [sem(f"parts_stored{u}") for u in range(PBUF)]
        mpart_ready = sem("mpart_ready")
        mpart_stored = sem("mpart_stored")
        fill_ready = sem("fill_ready")
        fill_stored = sem("fill_stored")
        win_step = sem("win_step")
        win_ready = sem("win_ready")
        win_loaded = [sem(f"win_loaded{u}") for u in range(2)]
        WIN_SPANS = 10
        var_stats = sem("var_stats")
        PROJ = 3 + 2
        SMALL = 7
        ctx_v = ctx_in.rearrange("b s d -> s b d")
        STEADY = (NG - 2) // 2
        SLOTS = 2 * GB // 2
        LOADS = PARTS * 2 + 1
        qk_loaded = [sem(f"qk_loaded{n}") for n in range(SLOTS)]

        def load_pair(sp, half, slot, stacks=range(PARTS, 0, -1)):
            u, col = slot // 2, slot % 2 * 2 * S
            tokens = bass.ds(half * (2 * S), 2 * S)
            for n in stacks:
                first = sum(range(n + 1, PARTS + 1))
                slots = slice(ROW_0 + first * DK, ROW_0 + (first + n) * DK)
                for tile, units in ((qs, slice(0, n)), (ks, slice(2 * PARTS - n, 2 * PARTS))):
                    sp.dma_start(tile[u][slots, :, col:col + 2 * S],
                                 qk_d[bass.ds(half, 1), units].rearrange("n u (d h) t -> (n u d) h t", d=DK))\
                        .then_inc(qk_loaded[slot], 16)
            if PARTS in stacks:
                sp.dma_start(ks[u][ROWS_P:ROWS_M, :, col:col + 2 * S],
                             mask_d[:, tokens].unsqueeze(1).to_broadcast([PARTS, H, 2 * S]))\
                    .then_inc(qk_loaded[slot], 16)

        def ps_qk(g, u):
            return ps2[:, 2:4] if u == 0 or isinstance(g, int) and g == NG - 1 else ps1

        def part(g, n):
            return parts[:, g % PBUF, n:2 * PARTS - n:2 * PARTS - 1 - 2 * n]

        def project_sync(sp):
            x_v = x.rearrange("b s d -> s b d")
            for i in range(XCH):
                n = B // XCH
                sp.dma_start(xs[:, i * n:(i + 1) * n], x_v[:, i * n:(i + 1) * n]).then_inc(x_loaded[i], 16)
                if i == 0:
                    for u in range(2):
                        sp.dma_start(cg[:, u], ctx_v[:, u * GB:(u + 1) * GB]).then_inc(ctx_loaded[u], 16)

            def store_parts(g):
                sp.wait_ge(parts_ready, g + 1)
                for i in range(GB // 2):
                    sp.dma_start(qk_d[g * (GB // 2) + i:g * (GB // 2) + i + 1].rearrange("n u p t -> p (n u) t"),
                                 parts[:, g % PBUF, :, i * 2 * S:(i + 1) * 2 * S]).then_inc(parts_stored[g % PBUF], 16)

            sp.wait_ge(win_ready, WIN_SPANS + 2)
            for side in range(2):
                load_window(sp, 0, side)
            store_parts(0)
            store_parts(1)
            load_window(sp, 1, 0)
            store_parts(2)
            sp.wait_ge(parts_stored[0], 16 * (GB // 2))
            sp.wait_ge(mpart_stored, 16)
            load_pair(sp, 0, 0)
            store_parts(3)
            store_parts(4)
            load_pair(sp, 1, 1)
            store_parts(5)
            return store_parts

        def window_rows(pool):
            half = QUART - GLOBAL
            spans = ((0, 0, GLOBAL, half, True), (0, 0, 3 * QUART, QUART, False),
                     (1, 0, QUART, QUART, False), (1, 0, 2 * QUART, QUART, True),
                     (0, 1, 2 * QUART, QUART, True), (0, 1, QUART, QUART, False),
                     (1, 1, 3 * QUART, QUART, False), (1, 1, GLOBAL, half, True))
            pool.wait_ge(ones_ready, 1)
            pool.drain()
            pool.memset(win[:], 0.0).then_inc(win_step, 1)
            pool.wait_ge(win_step, 1)
            for x, n, col, count, below in spans:
                pool.memset(win[:, x, n, :, col:col + count], (1.0, MASKED)[x]).then_inc(win_step, 1)
            for col, count in ((GLOBAL, half), (3 * QUART, QUART)):
                pool.memset(win[:, 1, 0, :, col:col + count], MASKED).then_inc(win_step, 1)
            pool.wait_ge(win_step, 1 + len(spans) + 2)
            for x, n, col, count, below in spans:
                span, place = win[:, x, n, :, col:col + count], col % QUART
                if below:
                    pool.affine_select(out=span, in_=span, compare_op=ALU.is_ge, fill=0.0, base=-1 - place,
                                       pattern=[[0, GB], [-1, count]], channel_multiplier=1).then_inc(win_ready, 1)
                else:
                    pool.affine_select(out=span, in_=span, compare_op=ALU.is_ge, fill=0.0, base=place,
                                       pattern=[[0, GB], [1, count]], channel_multiplier=-1).then_inc(win_ready, 1)
            span = win[:, 1, 0, :, GLOBAL:QUART]
            pool.affine_select(out=span, in_=span, compare_op=ALU.is_ge, fill=0.0, base=0,
                               pattern=[[0, GB], [0, half]], channel_multiplier=-1).then_inc(win_ready, 1)
            span = win[:, 1, 0, :, 3 * QUART:]
            pool.affine_select(out=span, in_=span, compare_op=ALU.is_ge, fill=0.0, base=-QUART,
                               pattern=[[0, GB], [0, QUART]], channel_multiplier=1).then_inc(win_ready, 1)
            pool.wait_ge(win_ready, WIN_SPANS)
            pool.drain()
            for n, value in enumerate((1.0, -1.0)):
                pool.memset(signs[:, n], value).then_inc(win_ready, 1)
            pool.wait_ge(win_ready, WIN_SPANS + 2)
            pool.drain()

        def load_window(sp, u, side):
            for n in range(2):
                sp.dma_start((qs, ks)[side][u][n * ROWS_W:(n + 1) * ROWS_W],
                             win[:, side, n].rearrange("r b s -> r (b s)").unsqueeze(1).to_broadcast([ROWS_W, H, GT]))\
                    .then_inc(win_loaded[u], 16)
            sp.dma_start((qs[u][ROWS_P:ROWS_M], ks[u][ROWS_M:ROWS_X])[side],
                         signs[:, side].unsqueeze(1).to_broadcast([PARTS, H, GT])).then_inc(win_loaded[u], 16)

        def project_gpsimd(pool):
            pool.memset(ident[:], 0.0).then_inc(pool_step, 1)
            pool.memset(ident_b[:], 0.0).then_inc(pool_step, 1)
            pool.wait_ge(pool_step, 2)
            for m in (ident, ident_b):
                pool.affine_select(out=m[:], in_=m[:], compare_op=ALU.not_equal, fill=1.0, base=0,
                                   pattern=[[-1, P]], channel_multiplier=1).then_inc(ident_ready, 1)
            pool.wait_ge(proj_loaded, 16 * PROJ)
            for n in ("q", "k"):
                pool.tensor_copy(w_by_dim[n][:], w_sb[n][:].rearrange("p (h d) -> p d h", d=DK))\
                    .then_inc(by_dim_ready, 1)
            pool.memset(va[:, :, :, DK:VW], 1.0).then_inc(ones_ready, 1)
            window_rows(pool)

            def last_part(g):
                pool.wait_ge(split1, g * 2 + 2)
                pool.tensor_tensor(part(g, 2), qkf[:, g % 2], part(g, 1), ALU.subtract).then_inc(parts_ready, 1)

            for g in range(2):
                last_part(g)
            pool.memset(wmask[:], 0.0).then_inc(pool_step, 1)
            pool.memset(tri[:], 1.0).then_inc(pool_step, 1)
            pool.memset(ones_b[:], 1.0)
            pool.memset(ones_s[:], 1.0)
            pool.memset(minus_half[:], -0.5)
            pool.memset(to_next[:], float(F)).then_inc(pool_step, 1)
            pool.memset(npart[:], 0.0)
            pool.memset(oh_sum[:], 0.0)
            pool.memset(fill[:], 0.0).then_inc(pool_step, 1)
            pool.wait_ge(pool_step, 6)
            pool.memset(to_next[:, E - 1:E], -float((E - 1) * F))
            pool.memset(to_next[:, 2 * E - 1:2 * E], 0.0)
            pool.memset(starts[:, 2 * E:2 * E + 1], float(E * CAP))
            pool.iota(fill[:].bitcast(U32)[:, :, X_IDX], [[P, 2 * E]], base=2 * T, channel_multiplier=1)\
                .then_inc(fill_ready, 1)
            pool.affine_select(out=tri[:], in_=tri[:], compare_op=ALU.is_gt, fill=0.0, base=0,
                               pattern=[[1, P]], channel_multiplier=-1)
            pool.affine_select(out=wmask[:], in_=wmask[:], compare_op=ALU.is_ge, fill=MASKED, base=WINDOW + QUART,
                               pattern=[[0, HB], [1, 2 * QUART]], channel_multiplier=-1).then_inc(pool_step, 1)
            pool.wait_ge(pool_step, 7)
            pool.affine_select(out=wmask[:], in_=wmask[:], compare_op=ALU.is_ge, fill=MASKED, base=WINDOW - QUART,
                               pattern=[[0, HB], [-1, 2 * QUART]], channel_multiplier=1).then_inc(pool_step, 1)
            pool.wait_ge(pool_step, 8)
            pool.affine_select(out=wmask[:], in_=wmask[:], compare_op=ALU.is_ge, fill=0.0, base=-GLOBAL,
                               pattern=[[0, HB], [0, 2 * QUART]], channel_multiplier=1).then_inc(pool_step, 1)
            for t, pattern, base, mult in ((iota_e, [[1, E]], 0, 0), (cap_e, [[CAP, E]], 0, 0),
                                           (iota_t, [[1, NT]], 0, 0), (idx_f, [[T, 2], [S, GB]], 0, 1)):
                pool.iota(t[:], pattern, base=base, channel_multiplier=mult, allow_small_or_imprecise_dtypes=True)
            for g in range(2, NG - 2):
                last_part(g)
            return last_part

        def project_scalar(act):
            for n, src in (("q", wq), ("k", wk), ("v", wv)):
                act.dma_start(w_sb[n][:], src).then_inc(proj_loaded, 16)
            act.dma_start(bq_col[:], bq.rearrange("(h d a) -> d h a", d=DK, a=1), allow_slow_non_contiguous=True)\
                .then_inc(proj_loaded, 16)
            act.dma_start(bk_col[:], bk.rearrange("(h d a) -> d h a", d=DK, a=1), allow_slow_non_contiguous=True)\
                .then_inc(proj_loaded, 16)

            def std(i):
                n = B // XCH
                act.wait_ge(var_ready, i + 1)
                nc.scalar.activation(rstd[:, i * n:(i + 1) * n], mv[:, i * n:(i + 1) * n, 1], ACT.Sqrt)\
                    .then_inc(std_ready, 1)

            std(0)
            act.dma_start(bv_row[:], bv.partition_broadcast(P)).then_inc(small_loaded, 16)
            act.dma_start(w_sb["o"][:], wo).then_inc(small_loaded, 16)
            act.dma_start(bo_row[:], bo.partition_broadcast(P)).then_inc(small_loaded, 16)
            act.dma_start(mrow[:], mask_in).then_inc(small_loaded, 16)
            act.dma_start(gates[:, 0:1], g_xattn.partition_broadcast(P)).then_inc(small_loaded, 16)
            act.dma_start(gates[:, 1:2], g_ffn.partition_broadcast(P)).then_inc(small_loaded, 16)
            act.dma_start(gate_sb[:], gate_w).then_inc(small_loaded, 16)
            act.wait_ge(proj_loaded, 16 * PROJ)
            nc.scalar.mul(bqs_col[:], bq_col[:], SCALE).then_inc(gates_ready, 1)

            def copy_turned(g, u):
                act.wait_ge(xn_turned, g + 1)
                nc.scalar.copy(xnT[:, u], ps2[:, 0]).then_inc(turned_copied, 1)
                act.wait_ge(ctx_turned, g + 1)
                nc.scalar.copy(ctxT[:, u], ps2[:, 1]).then_inc(turned_copied, 1)

            def bias(g, u):
                act.wait_ge(qk_done, g + 1)
                if g >= PBUF:
                    act.wait_ge(parts_stored[g % PBUF], g // PBUF * (16 * (GB // 2)))
                if g >= 2:
                    act.wait_ge(parts_ready, g - 1)
                for s, (b, scale) in enumerate(((bqs_col, SCALE), (bk_col, 1.0))):
                    nc.scalar.activation(qkf[:, u, s], ps_qk(g, u)[:, s], ACT.Identity, bias=b[:, 0:1], scale=scale)
                    ins = nc.scalar.activation(parts[:, g % PBUF, (0, 2 * PARTS - 1)[s]], ps_qk(g, u)[:, s], ACT.Identity,
                                               bias=b[:, 0:1], scale=scale)
                ins.then_inc(qk_copied, 1)

            act.wait_ge(gates_ready, 1)
            def load_ctx(g, u):
                act.dma_start(cg[:, u], ctx_v[:, (g + 2) * GB:(g + 3) * GB]).then_inc(ctx_loaded[u], 16)

            copy_turned(0, 0)
            load_ctx(0, 0)
            std(1)
            copy_turned(1, 1)
            load_ctx(1, 1)
            bias(0, 0)
            for i in range(2, XCH):
                std(i)
            copy_turned(2, 0)
            bias(1, 1)
            act.wait_ge(small_loaded, 16 * SMALL)
            nc.scalar.activation(tg[:], gates[:], ACT.Tanh).then_inc(gates_ready, 1)
            act.wait_ge(mpart_ready, 1)
            act.dma_start(mask_d.rearrange("a (b s) -> b a s", s=S), mpart[:]).then_inc(mpart_stored, 16)
            for g in range(2, NG - 2):
                load_ctx(g, g % 2)
                copy_turned(g + 1, (g + 1) % 2)
                bias(g, g % 2)
            copy_turned(NG - 1, 1)
            return bias

        def project_vector(dve):
            steps = [0]

            def then_wait(ins):
                steps[0] += 1
                ins.then_inc(dve_step, 1)
                dve.wait_ge(dve_step, steps[0])

            def statistics(i):
                n = B // XCH
                dve.wait_ge(x_loaded[i], 16)
                for b in range(i * n, (i + 1) * n):
                    nc.vector.bn_stats(stats[:, b], xs[:, b]).then_inc(var_stats, 1)
                dve.wait_ge(var_stats, (2 * i + 1) * n)
                for b in range(i * n, (i + 1) * n):
                    nc.vector.bn_aggr(mv[:, b], stats[:, b]).then_inc(var_stats, 1)
                dve.wait_ge(var_stats, (2 * i + 2) * n)
                nc.vector.tensor_scalar(mv[:, i * n:(i + 1) * n, 1], mv[:, i * n:(i + 1) * n, 1], EPS, None,
                                        ALU.add).then_inc(var_ready, 1)

            def invert(i):
                n = B // XCH
                dve.wait_ge(std_ready, i + 1)
                then_wait(nc.vector.reciprocal(rstd[:, i * n:(i + 1) * n], rstd[:, i * n:(i + 1) * n]))

            def normalise(g, u):
                if g >= 2:
                    dve.wait_ge(xn_turned, g - 1)
                for j in range(GB):
                    b = g * GB + j
                    nc.vector.tensor_scalar(xn[:, u, j], xs[:, b], mv[:, b, 0:1], rstd[:, bass.ds(b, 1)],
                                            ALU.subtract, ALU.mult).then_inc(xn_written, 1)

            def bias_v(g):
                dve.wait_ge(v_done, g + 1)
                nc.vector.tensor_tensor(
                    va[:, bass.ds(g * GB, GB), :, 0:DK].rearrange("p b h d -> p (b h) d"),
                    psm[:].rearrange("p (c d) -> p c d", d=DK),
                    bv_row[:].unsqueeze(1).to_broadcast([P, GB, D]).rearrange("p b (h d) -> p b h d", h=H),
                    ALU.add).then_inc(v_copied, 1)

            def split(g, u):
                dve.wait_ge(qk_copied, g + 1)
                nc.vector.tensor_tensor(qkf[:, u], qkf[:, u], part(g, 0), ALU.subtract).then_inc(split1, 1)
                dve.wait_ge(split1, g * 2 + 1)
                nc.vector.tensor_copy(part(g, 1), qkf[:, u]).then_inc(split1, 1)

            assert XCH * 2 == NG
            statistics(0)
            invert(0)
            normalise(0, 0)
            normalise(1, 1)
            statistics(1)
            invert(1)
            normalise(2, 0)
            for i in range(2, XCH):
                statistics(i)
            dve.wait_ge(small_loaded, 16 * SMALL)
            then_wait(nc.vector.tensor_copy(mpart[:, 0], mrow[:]))
            then_wait(nc.vector.tensor_tensor(mres[:], mrow[:], mpart[:, 0], ALU.subtract))
            then_wait(nc.vector.tensor_copy(mpart[:, 1], mres[:]))
            nc.vector.tensor_tensor(mpart[:, 2], mres[:], mpart[:, 1], ALU.subtract).then_inc(mpart_ready, 1)
            dve.wait_ge(ones_ready, 1)
            for g in range(NG - 2):
                if g in (1, 3):
                    invert(g // 2 + 2)
                bias_v(g)
                if g + 3 < NG:
                    normalise(g + 3, (g + 1) % 2)
                split(g, g % 2)
            return bias_v, split

        def project_tensor(pe):

            def turn(g, u, half):
                pe.wait_ge(xn_written, (g + 1) * GB)
                if not (isinstance(g, int) and g == 0):
                    pe.wait_ge(turned_copied, g * 2)
                for j in range(GB):
                    ins = nc.tensor.transpose(ps2[:, 0, j * P:(j + 1) * P], xn[:, u, j], ident[:])
                ins.then_inc(xn_turned, 1)
                pe.wait_ge(ctx_loaded[u], half * 16 + 16)
                for j in range(GB):
                    ins = nc.tensor.transpose(ps2[:, 1, j * P:(j + 1) * P], cg[:, u, j], ident[:])
                ins.then_inc(ctx_turned, 1)

            def project(g, u):
                pe.wait_ge(turned_copied, g * 2 + 2)
                if not (isinstance(g, int) and g < 2):
                    pe.wait_ge(qk_copied, g if isinstance(g, int) and g == NG - 1 else g - 1)
                bank = ps_qk(g, u)
                nc.tensor.matmul(bank[:, 0], w_by_dim["q"][:], xnT[:, u], start=True, stop=True)
                nc.tensor.matmul(bank[:, 1], w_by_dim["k"][:], ctxT[:, u], start=True, stop=True).then_inc(qk_done, 1)
                if not (isinstance(g, int) and g == 0):
                    pe.wait_ge(v_copied, g)
                for j in range(GB):
                    ins = nc.tensor.matmul(psm[:, j * P:(j + 1) * P], ctxT[:, u, j * P:(j + 1) * P],
                                           w_sb["v"][:], start=True, stop=True)
                ins.then_inc(v_done, 1)

            pe.wait_ge(ident_ready, 2)
            turn(0, 0, 0)
            turn(1, 1, 0)
            pe.wait_ge(proj_loaded, 16 * PROJ)
            pe.wait_ge(by_dim_ready, 2)
            project(0, 0)
            turn(2, 0, 1)
            project(1, 1)
            with pe.Fori(1, STEADY) as it:
                for u in range(2):
                    g = it * 2 + u
                    turn(g + 1, 1 - u, it + u)
                    project(g, u)
            return turn, project

        rmax = sb("rmax", [P, H])
        nmax = sb("nmax", [P, H])
        npT = sb("npT", [PARTS * H, 2, S], BF16)
        vst = sb("vst", [P, 2, H, VW])
        oT = sb("oT", [P, HB * P])
        rden = sb("rden", [P, H])
        attn = sb("attn", [P, H, DK])
        attnT = sb("attnT", [P, S])
        st2 = sb("st2", [P, GB, 6])
        mv2 = sb("mv2", [P, GB, 2])
        rstd2 = sb("rstd2", [P, GB])
        shift2 = sb("shift2", [P, GB])
        xr = sb("xr", [P, 2, 2, GB, XW])
        xr_u = xr[:].bitcast(U32)
        xrT = sb("xrT", [P, GT])
        lg = sb("lg", [P, GB, E])
        tmp = sb("tmp", [P, 2, GB, E])
        oh = sb("oh", [P, 2, GB, E])
        ohb = sb("ohb", [P, GB, E], BF16)
        rank = sb("rank", [P, GB, E])
        top = sb("top", [P, GB, 8])
        top_e = sb("top_e", [P, GB, 8], U32)
        ed = sb("ed", [P, GB])
        ed1 = sb("ed1", [P, GB])
        new_oh = sb("new_oh", [P, E])
        posf = sb("posf", [P, 2, GB])
        pos = sb("pos", [P, 2, 2, GB], U32)

        max_scored = sem("max_scored")
        max_taken = sem("max_taken")
        npart_ready = sem("npart_ready")
        npart_turned = sem("npart_turned")
        npT_ready = sem("npT_ready")
        nmax_loaded = [sem(f"nmax_loaded{u}") for u in range(2)]
        max_split = sem("max_split")
        scored = sem("scored")
        exp_done = sem("exp_done")
        vst_ready = sem("vst_ready")
        pv_done = sem("pv_done")
        oT_ready = sem("oT_ready")
        o_turned = sem("o_turned")
        rden_ready = sem("rden_ready")
        bias_added = sem("bias_added")
        attn_ready = sem("attn_ready")
        attn_turned = sem("attn_turned")
        attnT_ready = sem("attnT_ready")
        out_done = sem("out_done")
        res_done = sem("res_done")
        zeroed = sem("zeroed")
        wait_passed = [sem(f"wait_passed{e}") for e in range(2)]
        r_stats = sem("r_stats")
        r_pool = sem("r_pool")
        xr_ready = sem("xr_ready")
        xr_copied = sem("xr_copied")
        xr_turned = sem("xr_turned")
        xrT_ready = sem("xrT_ready")
        logits_done = sem("logits_done")
        logits_taken = sem("logits_taken")
        r_mean = sem("r_mean")
        choice_step = sem("choice_step")
        place_step = sem("place_step")
        gap_ready = sem("gap_ready")
        odds_ready = sem("odds_ready")
        oh_ready = sem("oh_ready")
        ranked = sem("ranked")
        rank_taken = sem("rank_taken")
        oh_summed = sem("oh_summed")
        gates_written = sem("gates_written")
        pos_ready = sem("pos_ready")
        rows_ready = sem("rows_ready")
        scattered = [sem(f"scattered{u}") for u in range(2)]

        AHEAD = 2
        UNROLL = 2 * GB
        LOOPS = B // UNROLL - 2
        ps_np = psy[:, 2 * P:2 * P + S // 2].bitcast(BF16)
        ps_l = ps1[:, 1, 0:GB * E]
        ps_aT = psy[:, 0:P]
        ps_y = psy[:, P:2 * P]
        QW = P // HB
        ps_on = psm[:].rearrange("p (h v) -> p h v", v=QW)

        class At:
            def __init__(self, it, c):
                self.it, self.c = it, c
                self.b = it * UNROLL + c
                self.g = it * (UNROLL // GB) + c // GB
                self.j = c % GB
                self.u = (c // GB) % 2
                self.half = it * (UNROLL // 2) + c // 2
                self.slot = c // 2 % SLOTS
                self.turn = it * (UNROLL // 2 // SLOTS) + c // 2 // SLOTS
                self.known = isinstance(it, int)

            def plus(self, n):
                return At(self.it, self.c + n)

            def exists(self):
                return not self.known or 0 <= self.b < B

            def is_past(self, n):
                return not self.known or self.b >= n

        def batches(eng, step):
            for c in range(UNROLL):
                step(At(0, c))
            with eng.Fori(1, 1 + LOOPS) as it:
                for c in range(UNROLL):
                    step(At(it, c))
            for c in range(UNROLL):
                step(At(B // UNROLL - 1, c))

        class Group:
            def __init__(self, at, less):
                self.g = at.g - less
                self.u = (at.c // GB - less) % 2
                self.half = at.it * (UNROLL // GB // 2) + (at.c // GB - less) // 2
                self.known = at.known

            def exists(self):
                return not self.known or 0 <= self.g < NG

            def is_past(self, n):
                return not self.known or self.g >= n

        def route(at, phase):
            g = Group(at, 2 if phase == 4 else 1)
            return g if at.j == phase % GB and g.exists() else None

        def stand_alone(eng):
            eng.sem_inc(wait_passed[eng is nc.gpsimd], 1)

        AFTER = At(B // UNROLL - 1, UNROLL)
        LAST = Group(AFTER, 1)
        LATE = 20
        COUNTED = B - 2 * GB + 1
        PLANNING = (COUNTED + 1, COUNTED + 2, COUNTED + 4, COUNTED + 5)

        def attend_sync(sp, store_parts):
            def load_max(at):
                sp.wait_ge(npT_ready, at.b + 1)
                sp.dma_start(qs[at.u][ROWS_M:ROWS_X, :, at.j * S:(at.j + 1) * S], npT[:, at.c % 2])\
                    .then_inc(nmax_loaded[at.c % 2], 16)

            weights = [load for e in range(E) for load in (
                (w13_sb[:, e, 0], w1[e]), (w13_sb[:, e, 1], w3[e]),
                (w2_sb[:, e], w2[e].rearrange("(c f) d -> f c d", f=P)))]
            assert len(weights) == 2 * 2 * (UNROLL - 2)

            def load_weights(n):
                for to, src in weights[2 * n:2 * n + 2]:
                    sp.dma_start(to, src).then_inc(w_loaded, 16)

            def step(at):
                if at.plus(1).exists():
                    load_max(at.plus(1))
                if at.known and at.b == 0:
                    store_parts(NG - 1)
                if at.known and at.b == 1:
                    load_pair(sp, SLOTS - 1, SLOTS - 1)
                odd = at.c % 2
                pair = at.plus(UNROLL - 2 - odd)
                if at.is_past(2) and pair.exists():
                    if not odd:
                        sp.wait_ge(scored, at.b * NB)
                    load_pair(sp, pair.half, pair.slot, range(PARTS - 1, 0, -1) if odd else (PARTS,))
                if at.known and at.b == 2:
                    for u in range(PBUF):
                        sp.wait_ge(parts_stored[u], 16 * (GB // 2) * len(range(u, NG, PBUF)))
                    sp.wait_ge(v_copied, NG)
                if at.known and 2 <= at.b < UNROLL:
                    load_weights(at.b - 2)
                if at.known and B - UNROLL <= at.b < B - 2:
                    load_weights(UNROLL - 2 + at.b - (B - UNROLL))
                if at.known and at.b == UNROLL - 1:
                    sp.wait_ge(fill_ready, 1)
                    for e in range(E):
                        sp.dma_start(rows_d[E * CAP + e * P:E * CAP + (e + 1) * P], fill[:, E + e])\
                            .then_inc(fill_stored, 16)

            load_max(At(0, 0))
            load_window(sp, 1, 1)
            sp.wait_ge(parts_stored[1], 16 * (GB // 2))
            load_pair(sp, 2, 2)
            store_parts(NG - 2)
            batches(sp, step)

        def attend_tensor(pe, turn_group, project_group):
            def middle(bank):
                return nc.tensor.matmul(bank.rearrange("p (h s) -> p h s", s=S)[:, :, QUART:3 * QUART],
                                        ident_b[:], wmask[:],
                                        start=False, stop=True)


            def score_max(at, banks=range(NB)):
                col = at.j * S
                if at.known and at.b in (0, GB) and 0 in banks:
                    pe.wait_ge(win_loaded[at.u], 16 * 6)
                if at.c % 2 == 0 and 0 in banks:
                    pe.wait_ge(qk_loaded[at.slot], at.turn * (16 * LOADS) + 16 * LOADS)
                for n in banks:
                    if n == 1 and at.is_past(AHEAD):
                        routed(at.plus(-AHEAD))
                    if at.is_past(1) or n >= 2:
                        pe.wait_ge(max_taken, at.b * NB + (n - 1))
                    bank = ps1[:, n % 2]
                    for j in range(HB):
                        h = n * HB + j
                        nc.tensor.matmul(bank[:, j * S:(j + 1) * S], qs[at.u][0:ROWS_M, h, col:col + S],
                                               ks[at.u][0:ROWS_M, h, col:col + S], start=(j == 0), stop=False)
                    middle(bank).then_inc(max_scored, 1)

            def routed(at):
                if (r := route(at.plus(-1), 2)):
                    pe.wait_ge(logits_taken, r.g + 1)
                if (r := route(at, 4)):
                    pe.wait_ge(rank_taken, r.g + 1)
                if at.known and at.b == COUNTED:
                    pe.wait_ge(count_taken, 1)

            def turn_max(at):
                pe.wait_ge(npart_ready, at.b + 1)
                if at.is_past(3):
                    pe.wait_ge(res_done, at.b - 2)
                nc.tensor.transpose(ps_np, npart[:].rearrange("p a h -> p (a h)"), ident_b[:]).then_inc(npart_turned, 1)

            def score(at):
                col = at.j * S
                pe.wait_ge(nmax_loaded[at.c % 2], at.half * 16 + 16)
                if at.is_past(1):
                    pe.wait_ge(exp_done, at.b * 2)
                for n in range(NB):
                    bank = ps2[:, n]
                    for j in range(HB):
                        h = n * HB + j
                        nc.tensor.matmul(bank[:, j * S:(j + 1) * S], ks[at.u][0:ROWS_X, h, col:col + S],
                                               qs[at.u][0:ROWS_X, h, col:col + S], start=(j == 0), stop=False)
                    middle(bank).then_inc(scored, 1)

            def values(at, half):
                if half == 0:
                    pe.wait_ge(vst_ready, at.b + 1)
                    if at.is_past(1):
                        pe.wait_ge(attn_ready, at.b)
                    else:
                        pe.wait_ge(zeroed, 1)
                pe.wait_ge(exp_done, at.b * 2 + (half + 1))
                for n in range(half * (NB // 2), (half + 1) * (NB // 2)):
                    for j in range(HB):
                        h = n * HB + j
                        ins = nc.tensor.matmul(psm[j * QW:j * QW + VW, n * P:(n + 1) * P], vst[:, at.c % 2, h],
                                               pT[:, h], start=True, stop=True)
                if half == 1:
                    ins.then_inc(pv_done, 1)

            def turn_values(at):
                pe.wait_ge(oT_ready, at.b + 1)
                for n in range(NB):
                    ins = nc.tensor.transpose(psm[:, n * P:(n + 1) * P], oT[:, n * P:(n + 1) * P], ident[:])
                ins.then_inc(o_turned, 1)

            def turn_attn(at):
                pe.wait_ge(attn_ready, at.b + 1)
                if at.is_past(1):
                    pe.wait_ge(res_done, at.b)
                if at.plus(2).exists():
                    pe.wait_ge(npT_ready, at.b + 3)
                nc.tensor.transpose(ps_aT, attn[:].rearrange("p h d -> p (h d)"), ident[:]).then_inc(attn_turned, 1)

            def project(at):
                pe.wait_ge(attnT_ready, at.b + 1)
                nc.tensor.matmul(ps_y, attnT[:], w_sb["o"][:], start=True, stop=True).then_inc(out_done, 1)

            def turn_rows(r):
                pe.wait_ge(xr_ready, (r.g + 1) * GB)
                for j in range(GB):
                    ins = nc.tensor.transpose(psy[:, j * P:(j + 1) * P], xr[:, r.u, 0, j, 0:D], ident[:])
                ins.then_inc(xr_turned, 1)

            def logits(r):
                pe.wait_ge(xrT_ready, r.g + 1)
                for j in range(GB):
                    ins = nc.tensor.matmul(ps_l[:, j * E:(j + 1) * E], xrT[:, j * P:(j + 1) * P], gate_sb[:],
                                           start=True, stop=True)
                ins.then_inc(logits_done, 1)

            def ranks(r):
                pe.wait_ge(oh_ready, r.g + 1)
                pe.wait_ge(oh_summed, r.g + 1)
                nc.tensor.matmul(ps_l, tri[:], ohb[:].rearrange("p b e -> p (b e)"), start=True, stop=False)
                for j in range(GB - 1):
                    n = GB - 1 - j
                    nc.tensor.matmul(ps_l[:, (j + 1) * E:].rearrange("p (b e) -> p b e", e=E), ones_b[:],
                                     ohb[:, j].unsqueeze(1).to_broadcast([P, n, E]), start=False, stop=False)
                nc.tensor.matmul(ps_l.rearrange("p (b e) -> p b e", e=E), ones_b[:],
                                 oh_sum[:].unsqueeze(1).to_broadcast([P, GB, E]), start=False, stop=True)\
                    .then_inc(ranked, 1)

            def count(bank, groups):
                pe.wait_ge(oh_summed, groups + 1)
                nc.tensor.matmul(bank[:, 0:E], ones_b[:], oh_sum[:], start=True, stop=True).then_inc(counted, 1)

            def after(part):
                if part == 0:
                    turn_values(AFTER.plus(-1))
                elif part == 1:
                    ranks(Group(AFTER, 2))
                elif part == 2:
                    turn_attn(AFTER.plus(-1))
                else:
                    project(AFTER.plus(-1))

            def late(t):
                if t == 4:
                    pe.wait_ge(res_done, B)
                    turn_rows(LAST)
                elif t == 5:
                    logits(LAST)
                elif t == 9:
                    ranks(LAST)
                elif t == 11:
                    count(psy, NG)

            def step(at):
                last, ahead = at.plus(-1), at.plus(AHEAD)
                if at.exists():
                    score(at)
                if at.is_past(1) and last.exists():
                    turn_values(last)
                if at.plus(1).exists():
                    turn_max(at.plus(1))
                if (r := route(last, 2)):
                    logits(r)
                if (r := route(at, 4)):
                    ranks(r)
                if at.known and at.b == COUNTED:
                    count(ps_l, EARLY)
                if ahead.exists():
                    score_max(ahead, range(0, 2))
                if (r := route(at, 2)):
                    if at.plus(-2).exists():
                        pe.wait_ge(res_done, at.b - 1)
                    if at.plus(1).exists():
                        pe.wait_ge(npT_ready, at.b + 2)
                    turn_rows(r)
                if at.exists():
                    values(at, 0)
                if ahead.exists():
                    score_max(ahead, range(2, 3))
                if at.is_past(1) and last.exists():
                    if (r := route(at, 2)):
                        pe.wait_ge(xrT_ready, r.g + 1)
                    turn_attn(last)
                if at.exists():
                    values(at, 1)
                if ahead.exists():
                    score_max(ahead, range(3, 4))
                if at.is_past(1) and last.exists():
                    project(last)

            turn_group(NG - 1, 1, NG // 2 - 1)
            project_group(NG - 2, 0)
            pe.wait_ge(qk_copied, NG - 2)
            score_max(At(0, 0))
            turn_max(At(0, 0))
            project_group(NG - 1, 1)
            score_max(At(0, 1))
            pe.wait_ge(qk_copied, NG)
            batches(pe, step)
            return after, late

        def attend_scalar(act, bias):
            def copy_max(at):
                act.wait_ge(npart_turned, at.b + 1)
                if at.is_past(2):
                    act.wait_ge(nmax_loaded[at.c % 2], at.half * 16)
                nc.scalar.copy(npT[:, at.c % 2], ps_np[0:PARTS * H]).then_inc(npT_ready, 1)

            def exps(at, n):
                act.wait_ge(scored, at.b * NB + (n + 1) * (NB // 2))
                if at.is_past(1):
                    act.wait_ge(pv_done, at.b)
                lo, hi = n * (NB // 2), (n + 1) * (NB // 2)
                nc.scalar.activation(pT[:, lo * HB:hi * HB].rearrange("p h s -> p (h s)"),
                                     ps2[:, lo:hi].rearrange("p n s -> p (n s)"), ACT.Exp).then_inc(exp_done, 1)

            def copy_values(at):
                act.wait_ge(pv_done, at.b + 1)
                nc.scalar.copy(oT[:], psm[:]).then_inc(oT_ready, 1)

            def copy_attn(at):
                act.wait_ge(attn_turned, at.b + 1)
                nc.scalar.copy(attnT[:], ps_aT).then_inc(attnT_ready, 1)

            def norm_rows(r, half):
                act.wait_ge(r_pool, r.g * 4 + 4)
                for j in range(half * (GB // 2), (half + 1) * (GB // 2)):
                    nc.scalar.activation(xr[:, r.u, 0, j, 0:D], xs[:, r.g * GB + j], ACT.Identity,
                                         bias=shift2[:, j:j + 1], scale=rstd2[:, j:j + 1]).then_inc(xr_ready, 1)

            def copy_choice(r):
                act.wait_ge(xr_ready, (r.g + 1) * GB)
                nc.scalar.copy(xr[:, r.u, 1, :, 0:D], xr[:, r.u, 0, :, 0:D]).then_inc(xr_copied, 1)

            def copy_rows(r):
                act.wait_ge(xr_turned, r.g + 1)
                if r.is_past(1):
                    act.wait_ge(logits_done, r.g)
                nc.scalar.copy(xrT[:], psy[:]).then_inc(xrT_ready, 1)

            def odds(r):
                act.wait_ge(gap_ready, r.g + 1)
                nc.scalar.activation(ed[:], ed[:], ACT.Exp).then_inc(odds_ready, 1)

            def step(at):
                last, ahead = at.plus(-1), at.plus(AHEAD)
                if at.is_past(1) and last.exists():
                    copy_values(last)
                if (r := route(at, 2)):
                    norm_rows(r, 1)
                if at.exists():
                    exps(at, 0)
                if at.plus(1).exists():
                    copy_max(at.plus(1))
                if (r := route(at, 2)):
                    copy_rows(r)
                if (r := route(at, 4)):
                    odds(r)
                if at.exists():
                    exps(at, 1)
                if at.is_past(1) and last.exists():
                    copy_attn(last)
                if (r := route(at, 1)):
                    norm_rows(r, 0)
                if (r := route(at, 2)):
                    copy_choice(r)

            def after(part):
                if part == 0:
                    copy_values(AFTER.plus(-1))
                    odds(Group(AFTER, 2))
                else:
                    copy_attn(AFTER.plus(-1))

            def late(t):
                if t in (2, 3):
                    norm_rows(LAST, t - 2)
                elif t == 4:
                    copy_choice(LAST)
                    copy_rows(LAST)
                elif t == 8:
                    odds(LAST)

            bias(NG - 2, 0)
            copy_max(At(0, 0))
            bias(NG - 1, 1)
            batches(act, step)
            return after, late

        def attend_vector(dve, bias_v, split):
            def take_max(at, banks):
                for n in banks:
                    dve.wait_ge(max_scored, at.b * NB + (n + 1))
                    if n == 0 and at.is_past(1):
                        dve.wait_ge(npart_ready, at.b)
                    nc.vector.tensor_reduce(rmax[:, n * HB:(n + 1) * HB],
                                            ps1[:, n % 2].rearrange("p (h s) -> p h s", h=HB),
                                            AX.X, ALU.max).then_inc(max_taken, 1)

            def residual(at):
                if at.j == 0:
                    dve.wait_ge(bias_added, at.g + 1)
                dve.wait_ge(out_done, at.b + 1)
                nc.vector.scalar_tensor_tensor(out=xs[:, at.b], in0=ps_y, scalar=tg[:, 0:1], in1=xs[:, at.b],
                                               op0=ALU.mult, op1=ALU.add).then_inc(res_done, 1)

            def statistics(at):
                dve.wait_ge(res_done, at.b + 1)
                stand_alone(dve)
                nc.vector.bn_stats(st2[:, at.j], xs[:, at.b]).then_inc(r_stats, 1)

            def split_max(split, out):
                if split:
                    dve.wait_ge(max_taken, split.b * NB + NB)
                    if split.is_past(1):
                        dve.wait_ge(npart_turned, split.b)
                    nc.vector.tensor_copy(npart[:, 0], rmax[:]).then_inc(max_split, 1)
                if out:
                    residual(out)
                if split:
                    dve.wait_ge(max_split, split.b * 3 + 1)
                    nc.vector.tensor_tensor(nmax[:], rmax[:], npart[:, 0], ALU.subtract).then_inc(max_split, 1)
                    dve.wait_ge(max_split, split.b * 3 + 2)
                    nc.vector.tensor_copy(npart[:, 1], nmax[:]).then_inc(max_split, 1)
                if out:
                    statistics(out)
                if split:
                    dve.wait_ge(max_split, split.b * 3 + 3)
                    nc.vector.tensor_tensor(npart[:, 2], nmax[:], npart[:, 1], ALU.subtract).then_inc(npart_ready, 1)

            def normalise(at):
                dve.wait_ge(o_turned, at.b + 1)
                nc.vector.reciprocal(rden[:], ps_on[:, :, DK]).then_inc(rden_ready, 1)
                dve.wait_ge(rden_ready, at.b + 1)
                nc.vector.tensor_tensor(attn[:], ps_on[:, :, 0:DK], rden[:].unsqueeze(2).to_broadcast([P, H, DK]),
                                        ALU.mult).then_inc(attn_ready, 1)

            gbe = [P, GB, E]
            kgbe = [P, 2, GB, E]

            def route_mean(r):
                dve.wait_ge(r_stats, (r.g + 1) * GB)
                stand_alone(dve)
                for j in range(GB):
                    ins = nc.vector.bn_aggr(mv2[:, j], st2[:, j])
                ins.then_inc(r_mean, 1)

            def take_logits(r):
                dve.wait_ge(logits_done, r.g + 1)
                nc.vector.tensor_copy(lg[:].rearrange("p b e -> p (b e)"), ps_l).then_inc(logits_taken, 1)
                dve.wait_ge(logits_taken, r.g + 1)

            def choose(r, part):
                before = r.g * (2 * GB + 1)
                if part == 0:
                    stand_alone(dve)
                    for j in range(GB):
                        nc.vector.max(top[:, j], lg[:, j]).then_inc(choice_step, 1)
                elif part == 1:
                    dve.wait_ge(choice_step, before + GB)
                    stand_alone(dve)
                    for j in range(GB):
                        nc.vector.max_index(top_e[:, j], top[:, j], lg[:, j]).then_inc(choice_step, 1)
                    nc.vector.tensor_tensor(ed[:], top[:, :, 1], top[:, :, 0], ALU.subtract).then_inc(gap_ready, 1)
                else:
                    dve.wait_ge(choice_step, before + 2 * GB)
                    nc.vector.tensor_tensor(oh[:], iota_e[:].unsqueeze(1).unsqueeze(1).to_broadcast(kgbe),
                                            top_e[:, :, 0:2].rearrange("p b k -> p k b").unsqueeze(3).to_broadcast(kgbe),
                                            ALU.is_equal).then_inc(choice_step, 1)
                    dve.wait_ge(choice_step, before + 2 * GB + 1)
                    nc.vector.tensor_tensor(ohb[:], oh[:, 0], oh[:, 1], ALU.add).then_inc(oh_ready, 1)

            def take_ranks(r):
                dve.wait_ge(ranked, r.g + 1)
                nc.vector.tensor_tensor(rank[:], ps_l.rearrange("p (b e) -> p b e", e=E),
                                        cap_e[:].unsqueeze(1).to_broadcast(gbe), ALU.add).then_inc(rank_taken, 1)
                dve.wait_ge(rank_taken, r.g + 1)

            def places(r, part):
                if part == 0:
                    nc.vector.tensor_tensor(tmp[:], oh[:], rank[:].unsqueeze(1).to_broadcast(kgbe), ALU.mult)
                    nc.vector.tensor_reduce(new_oh[:], ohb[:].rearrange("p b e -> p e b"), AX.X, ALU.add)
                    dve.wait_ge(odds_ready, r.g + 1)
                    nc.vector.tensor_scalar(ed1[:], ed[:], 1.0, None, ALU.add).then_inc(place_step, 1)
                elif part == 1:
                    dve.wait_ge(place_step, r.g * 2 + 1)
                    nc.vector.tensor_reduce(posf[:], tmp[:], AX.X, ALU.add)
                    nc.vector.tensor_tensor(oh_sum[:], oh_sum[:], new_oh[:], ALU.add).then_inc(oh_summed, 1)
                    nc.vector.reciprocal(ed1[:], ed1[:]).then_inc(place_step, 1)
                else:
                    dve.wait_ge(place_step, r.g * 2 + 2)
                    nc.vector.tensor_copy(pos[:, r.u], posf[:]).then_inc(pos_ready, 1)
                    nc.vector.tensor_scalar(xr[:, r.u, 0, :, X_GATE], ed1[:], tg[:, 1:2], None, ALU.mult)
                    nc.vector.scalar_tensor_tensor(out=xr[:, r.u, 1, :, X_GATE], in0=ed1[:], scalar=tg[:, 1:2],
                                                   in1=ed[:], op0=ALU.mult, op1=ALU.mult).then_inc(gates_written, 1)

            def step(at):
                last, ahead = at.plus(-1), at.plus(AHEAD)
                out = last if at.is_past(1) and last.exists() else None
                chosen, placed = route(last, 2), route(at, 4)
                if out:
                    normalise(out)
                if at.known and at.b == B - 1:
                    dve.wait_ge(w_loaded, 48 * E)
                    dve.wait_ge(scored, (B - GB) * NB)
                    for t in range(2):
                        copy_weights(dve, t, t)
                if chosen:
                    take_logits(chosen)
                if placed:
                    take_ranks(placed)
                if at.known and at.b == COUNTED:
                    dve.wait_ge(counted, 1)
                    nc.vector.tensor_copy(cnt[:], ps_l[:, 0:E]).then_inc(count_taken, 1)
                for part, banks in enumerate((range(0, 2), range(2, 3), range(3, NB))):
                    if ahead.exists():
                        take_max(ahead, banks)
                    if part == 2:
                        split_max(ahead if ahead.exists() else None, out)
                    if chosen:
                        choose(chosen, part)
                    if placed:
                        places(placed, part)
                if (r := route(at, 0)):
                    route_mean(r)
                if at.known and at.b in PLANNING:
                    plan_sure(dve, PLANNING.index(at.b))

            def after(part):
                if part == 0:
                    normalise(AFTER.plus(-1))
                    take_ranks(Group(AFTER, 2))
                    for n in range(3):
                        places(Group(AFTER, 2), n)
                else:
                    residual(AFTER.plus(-1))
                    statistics(AFTER.plus(-1))
                    route_mean(LAST)

            def late(t):
                if t == 6:
                    take_logits(LAST)
                    choose(LAST, 0)
                elif t == 7:
                    choose(LAST, 1)
                    choose(LAST, 2)
                elif t == 10:
                    take_ranks(LAST)
                    for part in range(3):
                        places(LAST, part)
                elif t >= 12:
                    plan_rest(dve, t - 12)

            bias_v(NG - 2)
            take_max(At(0, 0), range(NB))
            split_max(At(0, 0), None)
            split(NG - 2, 0)
            bias_v(NG - 1)
            take_max(At(0, 1), range(NB))
            split_max(At(0, 1), None)
            nc.vector.memset(psm[:], 0.0).then_inc(zeroed, 1)
            split(NG - 1, 1)
            dve.sem_inc(oh_summed, 1)
            batches(dve, step)
            return after, late

        def attend_gpsimd(pool, last_part):
            def add_bias(g):
                rows = xs[:, bass.ds(g * GB, GB)]
                pool.tensor_tensor(rows, rows, bo_row[:].unsqueeze(1).to_broadcast([P, GB, D]), ALU.add)\
                    .then_inc(bias_added, 1)

            def copy_v(at):
                if at.is_past(2):
                    pool.wait_ge(pv_done, at.b - 1)
                stand_alone(pool)
                pool.tensor_copy(vst[:, at.c % 2], va[:, at.b]).then_inc(vst_ready, 1)

            def route_std(r):
                pool.wait_ge(r_mean, r.g + 1)
                stand_alone(pool)
                pool.tensor_scalar(rstd2[:], mv2[:, :, 1], EPS, 0.0, ALU.add, ALU.add).then_inc(r_pool, 1)
                pool.tensor_scalar(shift2[:], mv2[:, :, 0], -1.0, 0.0, ALU.mult, ALU.add).then_inc(r_pool, 1)
                pool.wait_ge(r_pool, r.g * 4 + 2)
                pool.tensor_tensor(rstd2[:], rstd2[:], minus_half[:], ALU.pow).then_inc(r_pool, 1)
                pool.wait_ge(r_pool, r.g * 4 + 3)
                pool.tensor_tensor(shift2[:], shift2[:], rstd2[:], ALU.mult).then_inc(r_pool, 1)

            def route_tokens(r):
                pool.tensor_copy(xr_u[:, r.u, :, :, X_IDX], idx_f[:]).then_inc(rows_ready, 1)
                pool.wait_ge(rows_ready, r.g * 2 + 1)
                stand_alone(pool)
                pool.tensor_scalar(idx_f[:], idx_f[:], float(GT), 0.0, ALU.add, ALU.add).then_inc(rows_ready, 1)
                pool.wait_ge(rows_ready, r.g * 2 + 2)
                stand_alone(pool)

            def scatter(r, j, choices=range(2)):
                if j == 0 and 0 in choices:
                    pool.wait_ge(pos_ready, r.g + 1)
                    pool.wait_ge(gates_written, r.g + 1)
                    pool.wait_ge(xr_copied, r.g + 1)
                    stand_alone(pool)
                for k in choices:
                    pool.indirect_dma_start(
                        out=rows_d, out_offset=bass.IndirectOffsetOnAxis(ap=pos[:, r.u, k, j:j + 1], axis=0),
                        in_=xr[:, r.u, k, j], in_offset=None).then_inc(scattered[r.u], 16)

            def step(at):
                sent = Group(at, 2)
                if (r := route(at, 1)):
                    route_std(r)
                if at.j in (1, 3) and sent.exists():
                    scatter(sent, at.j - 1)
                if at.plus(1).exists():
                    copy_v(at.plus(1))
                if at.j in (1, 3) and sent.exists():
                    scatter(sent, at.j)
                if (r := route(at, 2)):
                    route_tokens(r)
                if at.j == 3 and (not at.known or at.g + 1 < NG):
                    add_bias(at.g + 1)
                if at.j == 3 and sent.exists() and (not at.known or sent.g + 2 < NG):
                    pool.wait_ge(scattered[sent.u], sent.half * (2 * GB * 16) + 2 * GB * 16)
                    stand_alone(pool)

            copy_v(At(0, 0))
            pool.wait_ge(gates_ready, 2)
            pool.wait_ge(small_loaded, 16 * SMALL)
            pool.tensor_scalar(bo_row[:], bo_row[:], tg[:, 0:1], 0.0, ALU.mult, ALU.add).then_inc(pool_step, 1)
            pool.wait_ge(pool_step, 10)
            add_bias(0)
            for g in range(NG - 2, NG):
                last_part(g)
            def late(t):
                n = t - (LATE - 2 * GB)
                if t < GB:
                    scatter(Group(AFTER, 2), GB // 2 + t // 2, (t % 2,))
                elif n >= 0:
                    scatter(LAST, n // 2, (n % 2,))

            def after():
                for j in range(GB // 2):
                    scatter(Group(AFTER, 2), j)
                route_std(LAST)
                route_tokens(LAST)

            batches(pool, step)
            return after, late

        cnt = sb("cnt", [P, E])
        cnt_f = sb("cnt_f", [P, E])
        cnt_i = sb("cnt_i", [P, E], I32)
        nt_s = sb("nt_s", [P, E], I32)
        nt_f = sb("nt_f", [P, E])
        runs = sb("runs", [P, 2 * E])
        run_end = sb("run_end", [P, 2 * E])
        jump = sb("jump", [P, 2 * E])
        end_f = sb("end_f", [P, E])
        end_i = sb("end_i", [P, E], I32)
        past, past_by = (ks[0][:].bitcast(F32).rearrange("p h t -> p (h t)")[:, i * GT * H // 4:(i + 1) * GT * H // 4]
                         for i in range(2))
        tile_f = sb("tile_f", [P, NT])
        tile_e = sb("tile_e", [P, NT], I32)
        tile_r = sb("tile_r", [P, NT], I32)
        assert SURE < NT and (NT - SURE) * 2 * E <= GT * H // 4
        plan_step = sem("plan_step")
        counted = sem("counted")
        count_taken = sem("count_taken")
        planned = sem("planned")
        end_ready = sem("end_ready")
        tail_stored = sem("tail_stored")
        plan_steps = [0]

        def plan_then(dve, ins):
            plan_steps[0] += 1
            ins.then_inc(plan_step, 1)
            dve.wait_ge(plan_step, plan_steps[0])

        def tiles_of(dve, rounding):
            plan_then(dve, nc.vector.tensor_scalar(cnt_f[:], cnt[:], float(rounding), None, ALU.add))
            plan_then(dve, nc.vector.tensor_copy(cnt_i[:], cnt_f[:]))
            plan_then(dve, nc.vector.tensor_scalar(nt_s[:], cnt_i[:], P.bit_length() - 1, None, ALU.arith_shift_right))
            plan_then(dve, nc.vector.tensor_copy(nt_f[:], nt_s[:]))

        def run_ends(dve, n):
            plan_then(dve, nc.vector.tensor_tensor_scan(run_end[:, 0:n], ones_s[:, 0:n], runs[:, 0:n], 0.0,
                                                        ALU.mult, ALU.add))
            plan_then(dve, nc.vector.scalar_tensor_tensor(out=jump[:, 0:n], in0=runs[:, 0:n], scalar=-float(P),
                                                          in1=starts[:, 1:n + 1], op0=ALU.mult, op1=ALU.add))
            plan_then(dve, nc.vector.tensor_tensor(jump[:, 0:n], jump[:, 0:n], starts[:, 0:n], ALU.subtract))

        def place_tiles(dve, lo, hi, n, part):
            shape = [P, hi - lo, n]
            is_past, by = (t[:, 0:(hi - lo) * n].rearrange("p (t n) -> p t n", n=n) for t in (past, past_by))
            if part == 0:
                plan_then(dve, nc.vector.tensor_tensor(is_past, iota_t[:, lo:hi].unsqueeze(2).to_broadcast(shape),
                                                       run_end[:, 0:n].unsqueeze(1).to_broadcast(shape), ALU.is_ge))
                plan_then(dve, nc.vector.tensor_tensor(by, is_past, to_next[:, 0:n].unsqueeze(1).to_broadcast(shape),
                                                       ALU.mult))
            elif part == 1:
                plan_then(dve, nc.vector.tensor_reduce(tile_f[:, lo:hi], by, AX.X, ALU.add))
                plan_then(dve, nc.vector.tensor_copy(tile_e[:, lo:hi], tile_f[:, lo:hi]))
            elif part == 2:
                plan_then(dve, nc.vector.tensor_tensor(by, is_past, jump[:, 0:n].unsqueeze(1).to_broadcast(shape),
                                                       ALU.mult))
            else:
                plan_then(dve, nc.vector.tensor_reduce(tile_f[:, lo:hi], by, AX.X, ALU.add))
                plan_then(dve, nc.vector.scalar_tensor_tensor(out=tile_f[:, lo:hi], in0=iota_t[:, lo:hi],
                                                              scalar=float(P), in1=tile_f[:, lo:hi],
                                                              op0=ALU.mult, op1=ALU.add))
                nc.vector.tensor_copy(tile_r[:, lo:hi], tile_f[:, lo:hi]).then_inc(planned, 1)
                dve.wait_ge(planned, 1 if lo == 0 else 2)

        def plan_sure(dve, part):
            if part == 0:
                dve.wait_ge(count_taken, 1)
                tiles_of(dve, 0)
            elif part == 1:
                plan_then(dve, nc.vector.tensor_copy(runs[:, 0:E], nt_f[:]))
                plan_then(dve, nc.vector.tensor_copy(starts[:, 0:E], cap_e[:]))
                plan_then(dve, nc.vector.scalar_tensor_tensor(out=starts[:, E:2 * E], in0=nt_f[:], scalar=float(P),
                                                              in1=cap_e[:], op0=ALU.mult, op1=ALU.add))
                run_ends(dve, E)
            else:
                dve.wait_ge(scored, (B - GB) * NB)
                for n in range(2 * part - 4, 2 * part - 2):
                    place_tiles(dve, 0, SURE, E, n)

        def plan_rest(dve, part):
            if part == 0:
                dve.wait_ge(counted, 2)
                plan_then(dve, nc.vector.tensor_copy(cnt[:], psy[:, 0:E]))
                plan_then(dve, nc.vector.tensor_tensor(end_f[:], cnt[:], cap_e[:], ALU.add))
                nc.vector.tensor_copy(end_i[:], end_f[:]).then_inc(end_ready, 1)
            elif part == 1:
                tiles_of(dve, P - 1)
            elif part == 2:
                plan_then(dve, nc.vector.tensor_tensor(runs[:, E:2 * E], nt_f[:], runs[:, 0:E], ALU.subtract))
                run_ends(dve, 2 * E)
            elif part <= 6:
                place_tiles(dve, SURE, NT, 2 * E, part - 3)

        def plan_sync(sp):
            sp.wait_ge(end_ready, 1)
            for e in range(E):
                row = sp.value_load(end_i[0:1, e:e + 1], min_val=e * CAP, max_val=e * CAP + T)
                sp.dma_start(rows_d[bass.ds(row, P)], fill[:, e]).then_inc(tail_stored, 16)
            sp.wait_ge(planned, 2)
            sp.wait_ge(tail_stored, 16 * E)
            sp.wait_ge(fill_stored, 16 * E)
            for u in range(2):
                sp.wait_ge(scattered[u], NG // 2 * (2 * GB * 16))

        xg = sb("xg", [P, RING, XW])
        xg_u = xg[:].bitcast(U32)
        xgT = sb("xgT", [P, P])
        w13 = qs[0][:].bitcast(F32).rearrange("p h t -> p (h t)")[:, 0:2 * 2 * F]\
            .rearrange("p (u n f) -> p u n f", u=2, n=2)
        act_s, hidT = (qs[1][:].bitcast(F32).rearrange("p h t -> p (h t)")[:, i * 2 * F:(i + 1) * 2 * F]
                       .rearrange("p (u f) -> p u f", u=2) for i in range(2))
        yt = sb("yt", [P, YRING, D])
        y_sb = [ks[k][:].bitcast(F32).rearrange("p h t -> p (h t)")[:, 0:B * D].rearrange("p (b d) -> p b d", d=D)
                for k in range(2)]
        xg_loaded = [sem(f"xg_loaded{u}") for u in range(RING)]
        xg_turned = sem("xg_turned")
        xgT_ready = sem("xgT_ready")
        gate_done = sem("gate_done")
        up_done = sem("up_done")
        w13_ready = sem("w13_ready")
        silu_done = sem("silu_done")
        hid_ready = sem("hid_ready")
        down_done = sem("down_done")
        yt_ready = sem("yt_ready")
        sent = [sem(f"sent{u}") for u in range(YRING)]
        y_loaded = [sem(f"y_loaded{g}") for g in range(NG)]
        y_added = sem("y_added")
        out_ready = sem("out_ready")
        out_stored = sem("out_stored")

        ps_a, ps_b = (ps2[:, 0], ps2[:, 2]), (ps2[:, 1], ps2[:, 3])

        def ps_x(t):
            return ps1[:, 0, P:2 * P] if isinstance(t, int) and t < 2 else psm[:, 0:P]

        ps_d = ps1[:, 0, 0:D]
        assert RING % YRING == 0 and YRING % 2 == 0 and NT > 2 * RING

        def tiles(eng, step, lo, hi):
            turns = (hi - lo) // RING
            with eng.Fori(0, turns) as it:
                for c in range(lo, lo + RING):
                    step(it * RING + c, c % RING, it + c // RING)
            for t in range(lo + turns * RING, hi):
                step(t, t % RING, t // RING)

        def expert(eng, t):
            return eng.value_load(tile_e[0:1, t:t + 1] if isinstance(t, int) else tile_e[0:1, bass.ds(t, 1)],
                                  min_val=0, max_val=(E - 1) * F)

        def sent_before(u, turn):
            return turn * (RING // YRING) + u // YRING

        def copy_weights(dve, t, u):
            nc.vector.tensor_copy(
                w13[:, u % 2].rearrange("p n f -> p (n f)"),
                w13_sb[:].rearrange("p e n f -> p (e n f)")[:, bass.ds(expert(dve, t) * 2, 2 * F)])\
                .then_inc(w13_ready, 1)

        def experts_sync(sp):
            def load(t, u, turn):
                row = sp.value_load(tile_r[0:1, bass.ds(t, 1)], min_val=0, max_val=E * CAP + (E - 1) * P)
                if not (isinstance(t, int) and t < RING):
                    sp.wait_ge(sent[u % YRING], sent_before(u, turn - 1) * 16 + 16)
                sp.dma_start(xg[:, u], rows_d[bass.ds(row, P)]).then_inc(xg_loaded[u], 16)

            sp.wait_ge(planned, 1)
            for u in range(2):
                sp.wait_ge(scattered[u], len(range(u, EARLY, 2)) * (2 * GB * 16))
            for t in range(RING):
                load(t, t, 0)
            tiles(sp, load, RING, SURE)
            plan_sync(sp)
            tiles(sp, load, SURE, NT)
            wait_sent(sp)
            for g in range(NG):
                for k in range(2):
                    sp.dma_start(y_sb[k][:, g * GB:(g + 1) * GB],
                                 y_d[k * T + g * GT:k * T + (g + 1) * GT].rearrange("(b s) d -> s b d", s=S))\
                        .then_inc(y_loaded[g], 16)
            for g in range(NG):
                sp.wait_ge(out_ready, g + 1)
                sp.dma_start(out[g * GB:(g + 1) * GB].rearrange("b s d -> s b d"), xs[:, g * GB:(g + 1) * GB])\
                    .then_inc(out_stored, 16)
            sp.wait_ge(out_stored, 16 * NG)

        def wait_sent(eng):
            for u in range(YRING):
                eng.wait_ge(sent[u], 16 * len(range(u, NT, YRING)))

        def experts_tensor(pe, after, late):
            def turn_rows(t, u, turn):
                pe.wait_ge(xg_loaded[u], turn * 16 + 16)
                nc.tensor.transpose(ps_x(t), xg[:, u, 0:D], ident[:]).then_inc(xg_turned, 1)

            def up(t, u):
                pe.wait_ge(xgT_ready, t + 1)
                pe.wait_ge(w13_ready, t + 1)
                for n, (bank, done) in enumerate(((ps_a, gate_done), (ps_b, up_done))):
                    for c in range(FC):
                        ins = nc.tensor.matmul(bank[u % 2][:, c * P:(c + 1) * P], w13[:, u % 2, n, c * P:(c + 1) * P],
                                               xgT[:], start=True, stop=True)
                    ins.then_inc(done, 1)

            def down(t, u, at):
                pe.wait_ge(hid_ready, t + 1)
                pe.wait_ge(yt_ready, t + 1)
                for c in range(FC):
                    ins = nc.tensor.matmul(ps_d, hidT[:, u % 2, c * P:(c + 1) * P],
                                           w2_sb[:].rearrange("p e c d -> p (e c d)")[:, bass.ds(at + c * D, D)],
                                           start=(c == 0), stop=(c == FC - 1))
                ins.then_inc(down_done, 1)

            def step(t, u, turn):
                before = expert(pe, t - 1)
                up(t, u)
                c = u + 1
                turn_rows(t + 1, c % RING, turn + c // RING)
                down(t - 1, u - 1, before)

            pe.wait_ge(w_loaded, 48 * E)
            pe.wait_ge(planned, 1)
            pe.wait_ge(exp_done, 2 * B)
            turn_rows(0, 0, 0)
            up(0, 0)
            after(0)
            turn_rows(1, 1, 0)
            after(1)
            up(1, 1)
            after(2)
            turn_rows(2, 2, 0)
            down(0, 0, expert(pe, 0))
            after(3)
            for t in range(2, LATE):
                step(t, t % RING, t // RING)
                late(t)
            tiles(pe, step, LATE, NT - 1)
            before, own = expert(pe, NT - 2), expert(pe, NT - 1)
            up(NT - 1, (NT - 1) % RING)
            down(NT - 2, (NT - 2) % RING, before)
            down(NT - 1, (NT - 1) % RING, own)

        def experts_scalar(act, after, late):
            def copy_rows(t):
                act.wait_ge(xg_turned, t + 1)
                nc.scalar.copy(xgT[:], ps_x(t)).then_inc(xgT_ready, 1)

            def gate(t, u):
                act.wait_ge(gate_done, t + 1)
                nc.scalar.activation(act_s[:, u % 2], ps_a[u % 2], ACT.Silu).then_inc(silu_done, 1)

            def scale_out(t, u, turn):
                act.wait_ge(down_done, t + 1)
                if not (isinstance(t, int) and t < YRING):
                    act.wait_ge(sent[u % YRING], sent_before(u, turn) * 16)
                nc.scalar.activation(yt[:, u % YRING], ps_d, ACT.Copy, scale=xg[:, u, X_GATE:X_GATE + 1])\
                    .then_inc(yt_ready, 1)

            def step(t, u, turn):
                gate(t, u)
                if not (isinstance(t, int) and t == NT - 1):
                    copy_rows(t + 1)
                if not (isinstance(t, int) and t == 0):
                    scale_out(t - 1, (u - 1) % RING, turn + (u - 1) // RING)

            act.sem_inc(yt_ready, 1)
            copy_rows(0)
            after(0)
            copy_rows(1)
            gate(0, 0)
            after(1)
            late(0)
            for t in range(1, LATE):
                step(t, t % RING, t // RING)
                late(t)
            tiles(act, step, LATE, NT - 1)
            step(NT - 1, (NT - 1) % RING, (NT - 1) // RING)
            scale_out(NT - 1, (NT - 1) % RING, (NT - 1) // RING)

        def experts_vector(dve, after, late):
            def gated(t, u, turn):
                dve.wait_ge(silu_done, t + 1)
                dve.wait_ge(up_done, t + 1)
                nc.vector.tensor_tensor(hidT[:, u % 2], act_s[:, u % 2], ps_b[u % 2],
                                        ALU.mult).then_inc(hid_ready, 1)

            def step(t, u, turn):
                gated(t, u, turn)
                copy_weights(dve, t + 2, u)

            after(0)
            gated(0, 0, 0)
            copy_weights(dve, 2, 0)
            after(1)
            late(0)
            for t in range(1, LATE):
                step(t, t % RING, t // RING)
                late(t)
            tiles(dve, step, LATE, NT - 2)
            for t in range(NT - 2, NT):
                gated(t, t % RING, 0)

            for g in range(NG):
                rows = slice(g * GB, (g + 1) * GB)
                dve.wait_ge(y_loaded[g], 16 * 2)
                nc.vector.tensor_tensor(y_sb[0][:, rows], y_sb[0][:, rows], y_sb[1][:, rows], ALU.add)\
                    .then_inc(y_added, 1)
                dve.wait_ge(y_added, g + 1)
                nc.vector.tensor_tensor(xs[:, rows], xs[:, rows], y_sb[0][:, rows], ALU.add).then_inc(out_ready, 1)

        def experts_gpsimd(pool, after, late):
            def send(t, u, turn):
                pool.wait_ge(yt_ready, t + 2)
                stand_alone(pool)
                pool.indirect_dma_start(
                    out=y_d, out_offset=bass.IndirectOffsetOnAxis(ap=xg_u[:, u, X_IDX:X_IDX + 1], axis=0),
                    in_=yt[:, u % YRING], in_offset=None).then_inc(sent[u % YRING], 16)

            after()
            for t in range(LATE):
                send(t, t % RING, t // RING)
                late(t)
            tiles(pool, send, LATE, NT)
            wait_sent(pool)

        with nc.Block() as block:
            @block.sync
            def _(sp):
                last_groups = project_sync(sp)
                attend_sync(sp, last_groups)
                experts_sync(sp)

            @block.tensor
            def _(pe):
                last_groups = project_tensor(pe)
                after, late = attend_tensor(pe, *last_groups)
                experts_tensor(pe, after, late)

            @block.scalar
            def _(act):
                last_groups = project_scalar(act)
                after, late = attend_scalar(act, last_groups)
                experts_scalar(act, after, late)

            @block.vector
            def _(dve):
                last_groups = project_vector(dve)
                after, late = attend_vector(dve, *last_groups)
                experts_vector(dve, after, late)

            @block.gpsimd
            def _(pool):
                last_groups = project_gpsimd(pool)
                after, late = attend_gpsimd(pool, last_groups)
                experts_gpsimd(pool, after, late)


_INS = ["x", "ctx_1024", "mask_BxS2_ff0", "g_xattn", "g_ffn", "L0_xattn_wq", "L0_xattn_bq", "L0_xattn_wk",
        "L0_xattn_bk", "L0_xattn_wv", "L0_xattn_bv", "L0_xattn_wo", "L0_xattn_bo", "L0_ffn_gate_w",
        "L0_ffn_w1", "L0_ffn_w3", "L0_ffn_w2"]


def kernel(**inputs):
    import concourse.bacc as bacc
    from concourse.bass_utils import run_bass_kernel_spmd

    nc = bacc.Bacc("TRN2", target_bir_lowering=False, num_devices=1)
    arrays, args = {}, []
    for name in _INS:
        a = np.ascontiguousarray(inputs[name])
        arrays[f"in_{name}_dram"] = a
        args.append(nc.dram_tensor(f"in_{name}_dram", a.shape, mybir.dt.from_np(a.dtype), kind="ExternalInput").ap())
    shape = inputs["x"].shape
    args.append(nc.dram_tensor("out_0_dram", shape, F32, kind="ExternalOutput").ap())
    build(nc, *args)
    r = run_bass_kernel_spmd(nc, [arrays], core_ids=[0])
    return r.results[0]["out_0_dram"]
```
